# Optimizing a Trainium2 kernel written in Bass

```python
import numpy as np
import jax
import jax.numpy as jnp

def _softmax(x, axis=-1):
    return jax.nn.softmax(x, axis=axis)

def _gelu(x):
    return jax.nn.gelu(x, approximate=True)

def _silu(x):
    return jax.nn.silu(x)

def _sigmoid(x):
    return jax.nn.sigmoid(x)

def _layernorm(x, axis=-1, eps=1e-05):
    m = jnp.mean(x, axis=axis, keepdims=True)
    v = jnp.var(x, axis=axis, keepdims=True)
    return (x - m) / jnp.sqrt(v + eps)

def _scatter_add(tgt, idx, src, axis=0):
    return tgt.at[idx].add(src)

def _segment_sum(src, seg, n):
    return jax.ops.segment_sum(src, seg, n)
kernel_name = 'mk_gnn_ffn_d1_gnn_r8_5b1049'

def setup_inputs(seed: int=0):
    np.random.seed(seed)
    _w = jnp.asarray

    def _rec_inputs():
        import jax
        import jax.numpy as jnp
        _gk = jax.random.key(seed)
        x = -6.415e-05 + 1 * jax.random.normal(jax.random.fold_in(_gk, 1), (1250, 1024), jnp.float32)
        src = jax.random.randint(jax.random.fold_in(_gk, 2), (20000,), 0, 1250, jnp.int32)
        dst = jax.random.randint(jax.random.fold_in(_gk, 3), (20000,), 0, 1250, jnp.int32)
        _o = jnp.argsort(dst, stable=True)
        src = src[_o]
        dst = dst[_o]
        edge_type_8 = jax.random.randint(jax.random.fold_in(_gk, 12), (20000,), 0, 8, jnp.int32)
        return (x, src, dst, edge_type_8)
    x, src, dst, edge_type_8 = _rec_inputs()

    def _L0_gnn_setup():
        import jax, jax.numpy as jnp
        import numpy as np
        N, D, R, E = (1250, 1024, 8, 10000)

        def _rgcn(x, edge_index, edge_type, weight, root, bias):
            src, dst = (edge_index[0], edge_index[1])
            msgs = x[src]
            out = x @ root + bias
            n = x.shape[0]
            for r in range(weight.shape[0]):
                mask = (edge_type == r).astype(x.dtype)
                sums = jax.ops.segment_sum(msgs * mask[:, None], dst, num_segments=n)
                cnt = jax.ops.segment_sum(mask, dst, num_segments=n)
                mean = sums / jnp.maximum(cnt, 1.0)[:, None]
                out = out + mean @ weight[r]
            return out
        key = jax.random.key(seed)
        ks = jax.random.split(key, 8)
        s = 1.0 / np.sqrt(D)
        x = jax.random.normal(ks[0], (N, D), dtype=jnp.float32)
        edge_index = jax.random.randint(ks[1], (2, E), 0, N, dtype=jnp.int64)
        edge_type = jax.random.randint(ks[2], (E,), 0, R, dtype=jnp.int64)
        weight = jax.random.normal(ks[3], (R, D, D), dtype=jnp.float32) * s
        root = jax.random.normal(ks[4], (D, D), dtype=jnp.float32) * s
        bias = jnp.zeros((D,), dtype=jnp.float32)
        w_gate = jax.random.normal(ks[5], (2 * D, D), dtype=jnp.float32) * (1.0 / np.sqrt(2 * D))
        b_gate = jnp.zeros((D,), dtype=jnp.float32)
        return {'x': x, 'edge_index': edge_index, 'edge_type': edge_type, 'weight': weight, 'root': root, 'bias': bias, 'w_gate': w_gate, 'b_gate': b_gate}
    _L0_gnn_all = _L0_gnn_setup()
    _L0_gnn_in = {k: v for k, v in _L0_gnn_all.items() if k in ('weight', 'root', 'bias', 'w_gate', 'b_gate')}
    del _L0_gnn_all

    def _L0_ffn_setup():
        import jax, jax.numpy as jnp
        import numpy as np
        TOP_K = 2
        key = jax.random.key(seed)
        ks = jax.random.split(key, 5)
        B, T, D, F, E = (2, 256, 1024, 512, 8)
        x = jax.random.normal(ks[0], (B, T, D), dtype=jnp.float32)
        router_w = jax.random.normal(ks[1], (D, E + 1), dtype=jnp.float32) * 0.02
        router_b = jax.random.normal(ks[2], (E + 1,), dtype=jnp.float32) * 0.02
        w1 = jax.random.normal(ks[3], (E, D, F), dtype=jnp.float32) * 0.02
        w2 = jax.random.normal(ks[4], (E, F, D), dtype=jnp.float32) * 0.02
        return {'x': x, 'router_w': router_w, 'router_b': router_b, 'w1': w1, 'w2': w2}
    _L0_ffn_all = _L0_ffn_setup()
    _L0_ffn_in = {k: v for k, v in _L0_ffn_all.items() if k in ('router_w', 'router_b', 'w1', 'w2')}
    del _L0_ffn_all
    return {'x': x, 'src': src, 'dst': dst, 'edge_type_8': edge_type_8, 'L0_gnn_weight': _L0_gnn_in['weight'], 'L0_gnn_root': _L0_gnn_in['root'], 'L0_gnn_bias': _L0_gnn_in['bias'], 'L0_gnn_w_gate': _L0_gnn_in['w_gate'], 'L0_gnn_b_gate': _L0_gnn_in['b_gate'], 'L0_ffn_router_w': _L0_ffn_in['router_w'], 'L0_ffn_router_b': _L0_ffn_in['router_b'], 'L0_ffn_w1': _L0_ffn_in['w1'], 'L0_ffn_w2': _L0_ffn_in['w2']}

def reference(x, src, dst, edge_type_8, L0_gnn_weight, L0_gnn_root, L0_gnn_bias, L0_gnn_w_gate, L0_gnn_b_gate, L0_ffn_router_w, L0_ffn_router_b, L0_ffn_w1, L0_ffn_w2):
    import jax
    import jax.numpy as jnp

    def _L0_gnn_ref(x, edge_index, edge_type, weight, root, bias, w_gate, b_gate):
        import jax, jax.numpy as jnp
        import numpy as np
        N, D, R, E = (1250, 1024, 8, 10000)

        def _rgcn(x, edge_index, edge_type, weight, root, bias):
            src, dst = (edge_index[0], edge_index[1])
            msgs = x[src]
            out = x @ root + bias
            n = x.shape[0]
            for r in range(weight.shape[0]):
                mask = (edge_type == r).astype(x.dtype)
                sums = jax.ops.segment_sum(msgs * mask[:, None], dst, num_segments=n)
                cnt = jax.ops.segment_sum(mask, dst, num_segments=n)
                mean = sums / jnp.maximum(cnt, 1.0)[:, None]
                out = out + mean @ weight[r]
            return out
        u = _rgcn(x, edge_index, edge_type, weight, root, bias)
        z = jnp.concatenate([u, x], axis=1) @ w_gate + b_gate
        h = jnp.tanh(u) * z + x * (1.0 - z)
        return h

    def _L0_ffn_ref(x, router_w, router_b, w1, w2):
        import jax, jax.numpy as jnp
        import numpy as np
        TOP_K = 2
        E = w1.shape[0]
        logits = x @ router_w + router_b
        probs = jax.nn.softmax(logits, axis=-1)
        top_v, top_i = jax.lax.top_k(probs, TOP_K)
        gates = jnp.sum(jax.nn.one_hot(top_i, E + 1, dtype=x.dtype) * top_v[..., None], axis=-2)
        h = jax.nn.gelu(jnp.einsum('btd,edf->ebtf', x, w1), approximate=False)
        y = jnp.einsum('ebtf,efd->ebtd', h, w2)
        out = jnp.einsum('bte,ebtd->btd', gates[..., :E], y) + gates[..., E:] * x
        return out
    edge_index = jnp.stack([src, dst])
    x = x + _L0_gnn_ref(_layernorm(x, axis=-1), edge_index, edge_type_8, L0_gnn_weight, L0_gnn_root, L0_gnn_bias, L0_gnn_w_gate, L0_gnn_b_gate)
    x = x + _L0_ffn_ref(_layernorm(x, axis=-1)[None], L0_ffn_router_w, L0_ffn_router_b, L0_ffn_w1, L0_ffn_w2)[0]
    return x

_drawn_inputs = setup_inputs


def setup_inputs(seed=0):
    import zlib

    import numpy as np

    out = dict(_drawn_inputs(seed))
    spreads = {'L0_gnn_bias': (0.0, 0.1), 'L0_gnn_b_gate': (0.0, 0.1)}
    factors = {'L0_ffn_router_b': 8.0, 'L0_ffn_w1': 3.638, 'L0_ffn_w2': 3.403}
    for name, (base, spread) in spreads.items():
        noise = np.random.default_rng([zlib.crc32(name.encode()), seed]).standard_normal(out[name].shape)
        drawn = base * np.exp(spread * noise) if base else spread * noise
        out[name] = jnp.asarray(drawn.astype(out[name].dtype))
    for name, factor in factors.items():
        out[name] = (out[name] * factor).astype(out[name].dtype)
    return out
```

```python
def build_program(nc, x, src, dst, typ, w_all, bias, w_gate_u, b_gate, router_w, router_b, w1, w2, out, upto=99, dbg=None):
    from contextlib import ExitStack
    import concourse.bass as bass
    from concourse import mybir

    F32, F32R, BF16, I32 = mybir.dt.float32, mybir.dt.float32r, mybir.dt.bfloat16, mybir.dt.int32
    F8 = mybir.dt.float8e4
    ALU, ACT, AX = mybir.AluOpType, mybir.ActivationFunctionType, mybir.AxisListType
    ds = bass.ds

    P = 128
    N, D = x.shape
    T = -(-N // P)
    NP = T * P
    LAST = N - (T - 1) * P
    KT = D // P
    H = 512
    UNITS = w_all.shape[0]
    R = UNITS - 2
    ROOT, GATE_X = R, R + 1
    E = src.shape[0]
    EP = 125
    EC = E // EP
    PAIR = 2 * P
    PAIRS = (E + T * PAIR) // PAIR
    CH = 16 * -(-PAIRS // 8)
    PC = 8
    NPIECE = EC // PC
    SC = 8
    EPS = 1e-5
    TR = T * R
    NX, F = w1.shape[0], w1.shape[2]
    NX1 = NX + 1
    NCH = (2 * N + NX * P) // P

    ctx = ExitStack()

    def sem(name):
        return ctx.enter_context(nc.semaphore(name))

    def dram(name, shape, dt):
        return nc.dram_tensor(name, shape, dt, kind="Internal").ap()

    y_dram = dram("y_scratch", [UNITS * NP, D], F32)
    winv_dram = dram("winv_scratch", [TR * P, 1], F32)
    x1_dram = dram("x1_scratch", [NP, D], F32)
    xn2_dram = dram("xn2_scratch", [NP, D], F32)
    ye_dram = dram("ye_scratch", [NCH * P, D], F32)
    tok_dram = dram("tok_scratch", [(NCH + 1) * P, 1], I32)
    slot_dram = dram("slot_scratch", [CH * P, 4], I32)

    with ctx:
        def sb(stack, name, shape, dt):
            return stack.enter_context(nc.sbuf_tensor(name, shape, dt))

        def ps(stack, name, shape, dt=F32):
            return stack.enter_context(nc.psum_tensor(name, shape, dt))

        ident = sb(ctx, "ident", [P, P], F32)
        lower = sb(ctx, "lower", [P, P], F32)
        ones = sb(ctx, "ones", [P, P], F32)
        iota_row = sb(ctx, "iota_row", [P, P], F32)
        stats = sb(ctx, "stats", [P, T, 2], F32)
        starts = sb(ctx, "starts", [P, T + 2], I32)
        slots = sb(ctx, "slots", [P, CH, 4], I32)
        stats2 = sb(ctx, "stats2", [P, T, 2], F32)
        logits = sb(ctx, "logits", [P, T, NX1], F32)
        newton = sb(ctx, "newton", [P, 4], F32)
        winv = sb(ctx, "winv", [P, CH], F32)

        def inverse_root(step, out_, var, tmp):
            v, a, y = tmp[:, 0:1], tmp[:, 1:2], tmp[:, 2:3]
            step(nc.vector.tensor_scalar(v, var, EPS, None, ALU.add))
            step(nc.vector.tensor_scalar(a.bitcast(I32), v.bitcast(I32), 1, None, ALU.arith_shift_right))
            step(nc.vector.tensor_scalar(y.bitcast(I32), a.bitcast(I32), -1.0, float(0x5F3759DF), ALU.mult, ALU.add))
            for n in range(3):
                step(nc.vector.tensor_scalar(a, y, y, v, ALU.mult, ALU.mult))
                step(nc.vector.tensor_scalar(a, a, -0.5, 1.5, ALU.mult, ALU.add))
                y_new = out_ if n == 2 else y
                step(nc.vector.tensor_tensor(y_new, y, a, ALU.mult))

        with ExitStack() as ph:
            xs = sb(ph, "xs", [P, 2, D], F32)
            xn = sb(ph, "xn", [P, 2, D], F32)
            bst = sb(ph, "bst", [P, 2, 2, 6], F32)
            mv = sb(ph, "mv", [P, 2, 2], F32)
            xT_hi = sb(ph, "xT_hi", [P, KT, NP], F32R)
            xT_lo = sb(ph, "xT_lo", [P, KT, NP], F32R)
            w_stage = sb(ph, "w_stage", [P, 4, 2, H], F32)
            w_hi = [sb(ph, f"w_hi{i}", [P, KT, H], F32R) for i in range(2)]
            w_lo = [sb(ph, f"w_lo{i}", [P, KT, H], F32R) for i in range(2)]
            y_out = w_out = sb(ph, "y_out", [P, 4, H], F32)
            ps_t = ps(ph, "ps_t", [P, 2, H])
            ps_y = ps(ph, "ps_y", [P, 4, H])
            ps_cnt = ps(ph, "ps_cnt", [P, H])
            ps_pre = ps(ph, "ps_pre", [P, 2, H // 2])

            edge_i = sb(ph, "edge_i", [EP, 3, EC], I32)
            tile_i = sb(ph, "tile_i", [EP, EC], I32)
            loc_i = edge_i[:, 1, :]
            edge_f = sb(ph, "edge_f", [EP, 5, EC], F32)
            ohT = sb(ph, "ohT", [EP, T, EC], BF16)
            cum = [v[0:EP, :, :].rearrange("p a b -> p (a b)")[:, 0:T * EC].rearrange("p (k c) -> p k c", k=T) for v in (xs, xn)]
            slot_f = edge_i[:, 0, :].bitcast(F32)
            slot_i = sb(ph, "slot_i", [EP, EC], I32)
            rec = sb(ph, "rec", [EP, EC, 4], I32)
            oh_key = sb(ph, "oh_key", [EP, 2, PC, TR], F8)
            oh_loc = sb(ph, "oh_loc", [EP, 2, PC, P], F8)
            pre = sb(ph, "pre", [P, 6, 16], F32)
            pre_i = sb(ph, "pre_i", [P, 16], I32)
            cnt = sb(ph, "cnt", [TR, 2, P], F32)
            fill = slots
            rec_buf = sb(ph, "rec_buf", [EP, 2, SC, 4], I32)
            idx_buf = sb(ph, "idx_buf", [P, 2, SC], I32)
            win_buf = sb(ph, "win_buf", [P, 2, SC], F32)

            s_x = [sem(f"x_loaded{i}") for i in range(2)]
            s_xpad = sem("x_padded")
            s_const = sem("constants_made")
            s_stat = sem("stats_chain")
            s_pass, q_pass, q_pass2, z_pass = (sem(f"wait_passed{i}") for i in range(4))
            s_xn = sem("x_normed")
            s_xT = sem("x_transposed")
            s_xhi = sem("xT_hi_made")
            s_xlo = sem("xT_lo_made")
            s_w = [sem(f"w_loaded{i}") for i in range(4)]
            s_whi = sem("w_hi_made")
            s_wlo = sem("w_lo_made")
            s_half = sem("half_multiplied")
            s_y = sem("y_multiplied")
            s_ysb = sem("y_copied")
            s_yst = [sem(f"y_stored{i}") for i in range(4)]
            s_edge = sem("edges_loaded")
            s_fill = sem("filler_made")
            s_fst = sem("filler_stored")
            s_dve = sem("sort_chain")
            s_oh = sem("onehots_made")
            s_ohu = sem("onehots_used")
            s_row = sem("row_totals_made")
            s_pre = sem("prefixes_multiplied")
            s_cinv = sem("winv_made")
            s_cst = sem("winv_stored")
            s_rec = sem("records_made")
            s_cp = sem("scatter_copied")
            s_sc = [sem(f"scattered{i}") for i in range(2)]
            s_sl = sem("slots_loaded")
            s_ga = [sem(f"winv_gathered{i}") for i in range(2)]

            y_view = y_dram.rearrange("(u t p) (h n) -> u t p h n", t=T, p=P, h=2)
            w_view = w_all.rearrange("u (k p) (h n) -> u p k h n", p=P, h=2)

            with nc.Block() as block:
                @block.sync
                def _(sp):
                    for i in range(2):
                        sp.dma_start(xs[:, i, :], x[i * P:(i + 1) * P, :]).then_inc(s_x[i], 16)
                    for i, a in enumerate((src, dst, typ)):
                        sp.dma_start(edge_i[:, i, :], a.rearrange("(p c) -> p c", c=EC)).then_inc(s_edge, 16)

                    def load_w(u, half):
                        for q in range(4):
                            n = u * 2 + half
                            if not (isinstance(n, int) and n == 0):
                                sp.wait_ge(s_wlo, n * 4 - 3 + q)
                            sp.dma_start(w_stage[:, q, :, :], w_view[ds(u, 1), :, 2 * q:2 * q + 2, half, :]
                                         .rearrange("u p k n -> (u p) k n")).then_inc(s_w[q], 16)

                    load_w(0, 0)
                    for t in range(2, T):
                        sp.wait_ge(s_xn, t - 1)
                        if t < T - 1:
                            sp.dma_start(xs[:, t % 2, :], x[t * P:(t + 1) * P, :]).then_inc(s_x[t % 2], 16)
                        else:
                            sp.wait_ge(s_xpad, 1)
                            sp.dma_start(xs[0:LAST, t % 2, :], x[t * P:N, :]).then_inc(s_x[t % 2], 16)
                    load_w(0, 1)

                    def store_y(u, half):
                        for t in range(T):
                            sp.wait_ge(s_ysb, (u * 2 + half) * T + t + 1)
                            sp.dma_start(y_view[ds(u, 1), t, :, half, :].rearrange("u p n -> (u p) n"),
                                         y_out[:, (half * T + t) % 4, :]).then_inc(s_yst[(half * T + t) % 4], 16)

                    with sp.Fori(0, UNITS - 1) as u:
                        for half in range(2):
                            load_w(u + 1, half)
                            store_y(u, half)
                    for half in range(2):
                        store_y(UNITS - 1, half)
                    for i in range(4):
                        sp.wait_ge(s_yst[i], 16 * UNITS * 2 * T // 4)

                @block.gpsimd
                def _(pool):
                    nc.gpsimd.memset(ident[:, :], 0.0).then_inc(s_const, 1)
                    nc.gpsimd.memset(lower[:, :], 1.0).then_inc(s_const, 1)
                    nc.gpsimd.memset(ones[:, :], 1.0).then_inc(s_const, 1)
                    nc.gpsimd.iota(iota_row[:, :], [[1, P]], base=0, channel_multiplier=0,
                                   allow_small_or_imprecise_dtypes=True).then_inc(s_const, 1)
                    pool.wait_ge(s_const, 4)
                    nc.gpsimd.affine_select(out=ident[:, :], in_=ident[:, :], compare_op=ALU.not_equal, fill=1.0,
                                            base=0, pattern=[[-1, P]], channel_multiplier=1).then_inc(s_const, 1)
                    nc.gpsimd.affine_select(out=lower[:, :], in_=lower[:, :], compare_op=ALU.is_gt, fill=0.0,
                                            base=0, pattern=[[1, P]], channel_multiplier=-1).then_inc(s_const, 1)
                    nc.gpsimd.memset(fill[:, :, :], 0).then_inc(s_fill, 1)
                    pool.wait_ge(s_fill, 1)
                    nc.gpsimd.memset(fill[:, :, 2:3], 2 * P - 1).then_inc(s_fill, 1)
                    pool.wait_ge(s_fill, 2)
                    pool.dma_start(slot_dram.rearrange("(p g) w -> p (g w)", p=P),
                                   fill[:, :, :].rearrange("p g w -> p (g w)")).then_inc(s_fst, 16)
                    pool.wait_ge(s_fst, 16)
                    pool.wait_ge(s_cinv, 1)
                    pool.dma_start(winv_dram.rearrange("(k c) o -> k (c o)", c=P), cnt[:, 1, :]).then_inc(s_cst, 16)
                    pool.wait_ge(s_rec, 1)

                    def scatter(i, first=False):
                        for b in range(2):
                            n = i * 2 + b
                            if not first:
                                pool.wait_ge(s_sc[b], i * (16 * SC))
                            nc.gpsimd.tensor_copy(rec_buf[:, b, :, :], rec[:, ds(n * SC, SC), :]).then_inc(s_cp, 1)
                            nc.gpsimd.tensor_copy(idx_buf[0:EP, b, :], slot_i[:, ds(n * SC, SC)]).then_inc(s_cp, 1)
                            pool.wait_ge(s_cp, n * 2 + 2)
                            pool.sem_inc(s_pass, 1)
                            for c in range(SC):
                                pool.indirect_dma_start(
                                    slot_dram, bass.IndirectOffsetOnAxis(idx_buf[0:EP, b, c:c + 1], 0),
                                    rec_buf[:, b, c, :], None, bounds_check=CH * P - 1).then_inc(s_sc[b], 16)

                    scatter(0, True)
                    with pool.Fori(1, EC // (2 * SC)) as i:
                        scatter(i)
                    for b in range(2):
                        pool.wait_ge(s_sc[b], 16 * EC // 2)
                    for i in range(2):
                        g = slice(i * CH // 2, (i + 1) * CH // 2)
                        pool.dma_start(slots[:, g, :], slot_dram.rearrange("(g p) w -> p g w", p=P)[:, g, :]).then_inc(s_sl, 16)
                        pool.wait_ge(s_sl, 16 * (i + 1))
                    pool.wait_ge(s_cst, 16)

                    COPIED = 2 * (EC // SC)

                    def gather(i, first=False):
                        for b in range(2):
                            n = i * 2 + b
                            nc.gpsimd.tensor_copy(idx_buf[:, b, :], slots[:, ds(n * SC, SC), 1]).then_inc(s_cp, 1)
                            pool.wait_ge(s_cp, n + (COPIED + 1))
                            pool.sem_inc(s_pass, 1)
                            for c in range(SC):
                                pool.indirect_dma_start(
                                    win_buf[:, b, c:c + 1], None, winv_dram,
                                    bass.IndirectOffsetOnAxis(idx_buf[:, b, c:c + 1], 0),
                                    bounds_check=TR * P - 1).then_inc(s_ga[b], 16)
                            if not (first and b == 0):
                                take(n - 1, 1 - b, i - 1 + b)

                    def take(n, b, i):
                        pool.wait_ge(s_ga[b], i * (16 * SC) + 16 * SC)
                        nc.gpsimd.tensor_copy(winv[:, ds(n * SC, SC)], win_buf[:, b, :])

                    gather(0, True)
                    with pool.Fori(1, CH // (2 * SC)) as i:
                        gather(i)
                    take(CH // SC - 1, 1, CH // (2 * SC) - 1)

                @block.scalar
                def _(act):
                    for t in range(T):
                        act.wait_ge(s_xT, t + 1)
                        nc.scalar.activation(xT_hi[:, :, t * P:(t + 1) * P],
                                             ps_t[:, :, :].rearrange("p b (k c) -> p (b k) c", c=P), ACT.Copy).then_inc(s_xhi, 1)

                    def split_hi(n, half, first=False):
                        if not first:
                            act.wait_ge(s_half, n - 1)
                        for q in range(4):
                            act.wait_ge(s_w[q], n * 16 + 16)
                            nc.scalar.activation(w_hi[half][:, 2 * q:2 * q + 2, :], w_stage[:, q, :, :], ACT.Copy).then_inc(s_whi, 1)

                    def copy_y(u, half, first=False):
                        for t in range(T):
                            m = half * T + t
                            act.wait_ge(s_y, u * (2 * T) + m + 1)
                            i = m % 4
                            if not (first and t < 4):
                                act.wait_ge(s_yst[i], u * (16 * 2 * T // 4) + 16 * (m // 4))
                            nc.scalar.activation(y_out[:, i, :], ps_y[:, i, :], ACT.Copy).then_inc(s_ysb, 1)

                    for half in range(2):
                        split_hi(half, half, True)
                    for half in range(2):
                        copy_y(0, half, half == 0)
                        split_hi(half + 2, half)
                    with act.Fori(1, UNITS - 1) as u:
                        for half in range(2):
                            copy_y(u, half)
                            split_hi(u * 2 + half + 2, half)
                    for half in range(2):
                        copy_y(UNITS - 1, half)

                @block.vector
                def _(dve):
                    st = [0]

                    def stat(ins):
                        st[0] += 1
                        ins.then_inc(s_stat, 1)
                        dve.wait_ge(s_stat, st[0])

                    def xT_low(t):
                        dve.wait_ge(s_xhi, t + 1)
                        nc.vector.tensor_tensor(xT_lo[:, :, t * P:(t + 1) * P],
                                                ps_t[:, :, :].rearrange("p b (k c) -> p (b k) c", c=P),
                                                xT_hi[:, :, t * P:(t + 1) * P].bitcast(F32), ALU.subtract).then_inc(s_xlo, 1)

                    for t in range(T):
                        b = t % 2
                        dve.wait_ge(s_x[b], 16 * (t // 2 + 1))
                        for h in range(2):
                            i = nc.vector.bn_stats(bst[:, b, h, :], xs[:, b, h * H:(h + 1) * H])
                        stat(i)
                        stat(nc.vector.bn_aggr(mv[:, b, :], bst[:, b, :, :].rearrange("p h s -> p (h s)")))
                        nc.vector.tensor_copy(stats[:, t, 0:1], mv[:, b, 0:1])
                        inverse_root(stat, stats[:, t, 1:2], mv[:, b, 1:2], newton)
                        if t >= 2:
                            dve.wait_ge(s_xT, t - 1)
                        nc.vector.tensor_scalar(xn[:, b, :], xs[:, b, :], stats[:, t, 0:1], stats[:, t, 1:2],
                                                ALU.subtract, ALU.mult).then_inc(s_xn, 1)
                        if t == T - 3:
                            dve.wait_ge(s_xn, t + 1)
                            nc.vector.memset(xs[:, (T - 1) % 2, :], 0.0).then_inc(s_xpad, 1)
                        if t >= 1:
                            xT_low(t - 1)
                    xT_low(T - 1)

                    def split_lo(n, half, first=False):
                        for q in range(4):
                            dve.wait_ge(s_whi, n * 4 + q + 1)
                            nc.vector.tensor_tensor(w_lo[half][:, 2 * q:2 * q + 2, :], w_stage[:, q, :, :],
                                                    w_hi[half][:, 2 * q:2 * q + 2, :].bitcast(F32), ALU.subtract).then_inc(s_wlo, 1)

                    ch = [0]

                    def step(ins):
                        ch[0] += 1
                        ins.then_inc(s_dve, 1)
                        dve.wait_ge(s_dve, ch[0])

                    split_lo(0, 0)
                    split_lo(1, 1)
                    dve.wait_ge(s_edge, 48)
                    dve.wait_ge(s_const, 6)
                    nc.vector.tensor_scalar(tile_i[:, :], edge_i[:, 1, :], 7, None, ALU.arith_shift_right)
                    nc.vector.tensor_scalar(loc_i, edge_i[:, 1, :], P - 1, None, ALU.bitwise_and)
                    nc.vector.tensor_copy(edge_f[:, 0, :], edge_i[:, 0, :])
                    step(nc.vector.tensor_copy(edge_f[:, 2, :], edge_i[:, 2, :]))
                    nc.vector.tensor_copy(edge_f[:, 1, :], loc_i)
                    step(nc.vector.tensor_copy(edge_f[:, 3, :], tile_i[:, :]))
                    step(nc.vector.scalar_tensor_tensor(edge_f[:, 4, :], edge_f[:, 2, :], float(T), edge_f[:, 3, :], ALU.mult, ALU.add))

                    def onehots(j):
                        c, b = slice(j * PC, (j + 1) * PC), j % 2
                        if j >= 2:
                            dve.wait_ge(s_ohu, j - 1)
                        nc.vector.tensor_tensor(oh_key[:, b, :, :], edge_f[:, 4, c].unsqueeze(2).broadcast_to([EP, PC, TR]),
                                                iota_row[0:EP, 0:TR].unsqueeze(1).broadcast_to([EP, PC, TR]), ALU.is_equal, saturate=False).then_inc(s_oh, 1)
                        nc.vector.tensor_tensor(oh_loc[:, b, :, :], edge_f[:, 1, c].unsqueeze(2).broadcast_to([EP, PC, P]),
                                                iota_row[0:EP, :].unsqueeze(1).broadcast_to([EP, PC, P]), ALU.is_equal, saturate=False).then_inc(s_oh, 1)

                    onehots(0)
                    onehots(1)
                    dve.wait_ge(s_xT, T)
                    step(nc.vector.tensor_tensor(ohT[:, :, :], edge_f[:, 3, :].unsqueeze(1).broadcast_to([EP, T, EC]),
                                                 iota_row[0:EP, 0:T].unsqueeze(2).broadcast_to([EP, T, EC]), ALU.is_equal))
                    a, b, d = ohT, cum[0], 1
                    while d < EC:
                        nc.vector.tensor_copy(b[:, :, 0:d], a[:, :, 0:d])
                        step(nc.vector.tensor_tensor(b[:, :, d:EC], a[:, :, d:EC], a[:, :, 0:EC - d], ALU.add))
                        a, b, d = b, (cum[1] if b is cum[0] else cum[0]), 2 * d
                    run, tmp = a, b
                    nc.vector.tensor_copy(pre[0:EP, 0, 0:T], run[:, :, EC - 1]).then_inc(s_row, 1)
                    split_lo(2, 0)
                    for j in range(2, NPIECE):
                        onehots(j)
                    dve.wait_ge(s_pre, 1)
                    step(nc.vector.tensor_scalar(pre_i[:, 0:T], ps_pre[:, 1, 0:T], float(PAIR - 1), None, ALU.add))
                    step(nc.vector.tensor_scalar(pre_i[:, 0:T], pre_i[:, 0:T], PAIR.bit_length() - 1, None, ALU.arith_shift_right))
                    nc.vector.memset(pre[:, 2, 0:1], 0.0)
                    step(nc.vector.tensor_scalar(pre[:, 1, 0:T], pre_i[:, 0:T], 1.0, None, ALU.max))
                    for k in range(T):
                        step(nc.vector.tensor_tensor(pre[:, 2, k + 1:k + 2], pre[:, 2, k:k + 1], pre[:, 1, k:k + 1], ALU.add))
                    nc.vector.tensor_copy(starts[:, 0:T + 1], pre[:, 2, 0:T + 1])
                    step(nc.vector.tensor_scalar(pre_i[:, 0:1], pre[:, 2, T:T + 1], 3.0, None, ALU.add))
                    nc.vector.tensor_scalar(starts[:, T + 1:T + 2], pre_i[:, 0:1], 2, None, ALU.arith_shift_right)
                    step(nc.vector.scalar_tensor_tensor(pre[0:EP, 3, 0:T], pre[0:EP, 2, 0:T], float(PAIR), ps_pre[0:EP, 0, 0:T], ALU.mult, ALU.add))
                    step(nc.vector.tensor_scalar(pre[0:EP, 3, 0:T], pre[0:EP, 3, 0:T], -1.0, None, ALU.add))
                    step(nc.vector.tensor_tensor(tmp[:, :, :], run[:, :, :], pre[0:EP, 3, 0:T].unsqueeze(2).broadcast_to([EP, T, EC]), ALU.add))
                    step(nc.vector.tensor_tensor(tmp[:, :, :], tmp[:, :, :], ohT[:, :, :], ALU.mult))
                    step(nc.vector.tensor_reduce(slot_f, tmp[:, :, :].rearrange("p k c -> p c k"), AX.X, ALU.add))
                    nc.vector.tensor_copy(slot_i[:, :], slot_f)
                    nc.vector.memset(rec[:, :, 3], 0)
                    nc.vector.scalar_tensor_tensor(rec[:, :, 0], edge_f[:, 2, :], float(NP), edge_f[:, 0, :], ALU.mult, ALU.add)
                    nc.vector.scalar_tensor_tensor(rec[:, :, 1], edge_f[:, 4, :], float(P), edge_f[:, 1, :], ALU.mult, ALU.add)
                    step(nc.vector.tensor_copy(rec[:, :, 2], edge_f[:, 1, :]))
                    dve.wait_ge(s_ohu, NPIECE)
                    step(nc.vector.tensor_scalar(cnt[:, 0, :], ps_cnt[0:TR, 0:P], 1.0, None, ALU.max))
                    nc.vector.reciprocal(cnt[:, 1, :], cnt[:, 0, :]).then_inc(s_cinv, 1)
                    dve.wait_ge(s_cinv, 1)
                    nc.vector.memset(cnt[:, 0, 0:1], 0.0).then_inc(s_rec, 1)
                    split_lo(3, 1)
                    with dve.Fori(2, UNITS) as u:
                        for half in range(2):
                            split_lo(u * 2 + half, half)

                @block.tensor
                def _(pe):
                    pe.wait_ge(s_const, 6)
                    for t in range(T):
                        pe.wait_ge(s_xn, t + 1)
                        if t >= 1:
                            pe.wait_ge(s_xlo, t)
                        for k in range(KT):
                            i = nc.tensor.transpose(ps_t[:, k // 4, (k % 4) * P:(k % 4 + 1) * P],
                                                    xn[:, t % 2, k * P:(k + 1) * P], ident[:, :])
                        i.then_inc(s_xT, 1)

                    def multiply(n, half, first=False):
                        pe.wait_ge(s_wlo, n * 4 + 4)
                        if first:
                            pe.wait_ge(s_xlo, T)
                        for t in range(T):
                            if not (first and t < 4):
                                pe.wait_ge(s_ysb, n * T + t - 3)
                            for k in range(KT):
                                hi, lo = xT_hi[:, k, t * P:(t + 1) * P], xT_lo[:, k, t * P:(t + 1) * P]
                                nc.tensor.matmul(ps_y[:, (half * T + t) % 4, :], lo, w_hi[half][:, k, :], start=(k == 0), stop=False)
                                nc.tensor.matmul(ps_y[:, (half * T + t) % 4, :], hi, w_lo[half][:, k, :], start=False, stop=False)
                                i = nc.tensor.matmul(ps_y[:, (half * T + t) % 4, :], hi, w_hi[half][:, k, :], start=False, stop=(k == KT - 1))
                            i.then_inc(s_y, 1)
                        pe.wait_ge(s_y, n * T + T)
                        pe.sem_inc(s_half, 1)

                    def count(j):
                        pe.wait_ge(s_oh, 2 * j + 2)
                        for c in range(PC):
                            i = nc.tensor.matmul(ps_cnt[0:TR, 0:P], oh_key[:, j % 2, c, :], oh_loc[:, j % 2, c, :],
                                                 start=(j == 0 and c == 0), stop=(j == NPIECE - 1 and c == PC - 1))
                        i.then_inc(s_ohu, 1)

                    multiply(0, 0, True)
                    count(0)
                    count(1)
                    pe.wait_ge(s_row, 1)
                    nc.tensor.matmul(ps_pre[0:EP, 0, 0:T], lower[0:EP, 0:EP], pre[0:EP, 0, 0:T], start=True, stop=True)
                    nc.tensor.matmul(ps_pre[:, 1, 0:T], ones[0:EP, :], pre[0:EP, 0, 0:T], start=True, stop=True).then_inc(s_pre, 1)
                    multiply(1, 1)
                    for j in range(2, NPIECE):
                        count(j)
                    with pe.Fori(1, UNITS) as u:
                        for half in range(2):
                            multiply(u * 2 + half, half)

        with ExitStack() as ph:
            G8 = 8
            LAG = 3
            msg = sb(ph, "msg", [P, G8, D], F32)
            sel = [sb(ph, f"sel{i}", [P, P], F32) for i in range(2)]
            row_idx = sb(ph, "row_idx", [P, 2, 4], I32)
            slot_loc = sb(ph, "slot_loc", [P, CH], F32)
            y_root = sb(ph, "y_root", [P, D], F32)
            y_gate = sb(ph, "y_gate", [P, 2, D], F32)
            xr = sb(ph, "xr", [P, 2, D], F32)
            xnr = sb(ph, "xnr", [P, 2, D], F32)
            u_sb = sb(ph, "u_sb", [P, 2, D], F32)
            uT_hi = sb(ph, "uT_hi", [P, KT, P], F32R)
            uT_lo = sb(ph, "uT_lo", [P, KT, P], F32R)
            x1 = sb(ph, "x1", [P, 2, D], F32)
            xn2 = sb(ph, "xn2", [P, 2, D], F32)
            xn2T = sb(ph, "xn2T", [P, KT, P], F32)
            wg_hi = sb(ph, "wg_hi", [P, KT, D], F32R)
            wg_lo = sb(ph, "wg_lo", [P, KT, D], F32R)
            wg_stage = sb(ph, "wg_stage", [P, 4, D], F32)
            rw = sb(ph, "rw", [P, KT, NX1], F32)
            rows = sb(ph, "rows", [3, D], F32)
            pick = sb(ph, "pick", [3, 3, P], F32)
            zero_row = sb(ph, "zero_row", [1, H], BF16)
            affine = sb(ph, "affine", [P, 2, T], F32)
            bst2 = sb(ph, "bst2", [P, 2, 6], F32)
            mv2 = sb(ph, "mv2", [P, 2], F32)
            ps_u = ps(ph, "ps_u", [P, 2, H])
            ps_z = ps(ph, "ps_z", [P, 2, H])
            ps_tr = ps(ph, "ps_tr", [P, 2, H])
            ps_log = ps(ph, "ps_log", [P, 4, P])

            q_par = [sem(f"params_loaded{i}") for i in range(2)]
            q_wg = [sem(f"wg_loaded{i}") for i in range(4)]
            q_wghi, q_wglo = sem("wg_hi_made"), sem("wg_lo_made")
            q_cst = sem("phase2_constants")
            q_yr, q_yg, q_xr = sem("y_root_loaded"), [sem(f"y_gate_loaded{i}") for i in range(2)], [sem(f"x_again_loaded{i}") for i in range(2)]
            q_idx = sem("row_idx_copied")
            q_ga = [sem(f"message_gathered{i}") for i in range(G8)]
            q_land = sem("messages_there")
            q_sel = sem("selection_made")
            q_agg = sem("message_summed")
            q_psu, q_u, q_ut = sem("u_summed"), sem("u_made"), sem("u_transposed")
            q_uhi, q_ulo = sem("uT_hi_made"), sem("uT_lo_made")
            q_z, q_act = sem("z_multiplied"), sem("gate_terms_made")
            q_xn = sem("x_norm_again")
            q_dve = sem("gate_chain")
            q_st = sem("stat2_chain")
            q_x1, q_xn2 = sem("x1_made"), sem("xn2_made")
            q_x1s, q_xn2s = [sem(f"x1_stored{i}") for i in range(2)], [sem(f"xn2_stored{i}") for i in range(2)]
            q_n2t, q_n2c, q_log, q_logc = sem("xn2_transposed"), sem("xn2T_copied"), sem("logits_made"), sem("logits_copied")

            with nc.Block() as block:
                def bounds(eng, t):
                    a = eng.value_load(starts[0:1, ds(t, 1)], min_val=0, max_val=PAIRS - 1)
                    b = eng.value_load(starts[0:1, ds(t + 1, 1)], min_val=0, max_val=PAIRS)
                    return a, b

                def stages(eng, stage):
                    stage(0, 0)
                    stage(0, 1)
                    with eng.Fori(1, T // 2) as j:
                        for b in range(2):
                            stage(j, b)

                @block.sync
                def _(sp):
                    sp.wait_ge(q_cst, 4)
                    sp.dma_start(rows[0:1, :], bias).then_inc(q_par[0], 16)
                    sp.dma_start(rows[1:2, :], b_gate).then_inc(q_par[0], 16)
                    sp.dma_start(rows[2:3, 0:NX1], router_b).then_inc(q_par[0], 16)
                    sp.dma_start(rw[:, :, :], router_w.rearrange("(k p) e -> p k e", p=P)).then_inc(q_par[1], 16)
                    yr = y_dram[ROOT * NP:(ROOT + 1) * NP, :].rearrange("(t p) n -> t p n", p=P)
                    yg = y_dram[GATE_X * NP:(GATE_X + 1) * NP, :].rearrange("(t p) n -> t p n", p=P)
                    x_t = x[0:(T - 1) * P, :].rearrange("(t p) n -> t p n", p=P)
                    x1_t = x1_dram.rearrange("(t p) n -> t p n", p=P)
                    xn2_t = xn2_dram.rearrange("(t p) n -> t p n", p=P)
                    wg_t = w_gate_u.rearrange("(k p) n -> p k n", p=P)

                    def load(j, b):
                        t = j * 2 + b
                        if not (isinstance(t, int) and t == 0):
                            sp.wait_ge(q_u, t)
                        sp.dma_start(y_root[:, :], yr[ds(t, 1), :, :].rearrange("t p n -> (t p) n")).then_inc(q_yr, 16)
                        if not (isinstance(t, int) and t < 2):
                            sp.wait_ge(q_x1, t - 1)
                        sp.dma_start(y_gate[:, b, :], yg[ds(t, 1), :, :].rearrange("t p n -> (t p) n")).then_inc(q_yg[b], 16)
                        if isinstance(t, int) and t == T - 1:
                            sp.dma_start(xr[0:LAST, b, :], x[t * P:N, :]).then_inc(q_xr[b], 16)
                        else:
                            sp.dma_start(xr[:, b, :], x_t[ds(t, 1), :, :].rearrange("t p n -> (t p) n")).then_inc(q_xr[b], 16)

                    def store(t, b):
                        sp.wait_ge(q_x1, t + 1)
                        sp.dma_start(x1_t[ds(t, 1), :, :].rearrange("t p n -> (t p) n"), x1[:, b, :]).then_inc(q_x1s[b], 16)
                        sp.wait_ge(q_xn2, t + 1)
                        sp.dma_start(xn2_t[ds(t, 1), :, :].rearrange("t p n -> (t p) n"), xn2[:, b, :]).then_inc(q_xn2s[b], 16)

                    for k in range(KT):
                        if k >= 4:
                            sp.wait_ge(q_wglo, k - 3)
                        sp.dma_start(wg_stage[:, k % 4, :], wg_t[:, k, :]).then_inc(q_wg[k % 4], 16)
                    load(0, 0)
                    load(0, 1)
                    with sp.Fori(1, T // 2 - 1) as j:
                        for b in range(2):
                            load(j, b)
                            store(j * 2 + b - 2, b)
                    for b in range(2):
                        load(T // 2 - 1, b)
                        store(T + b - 4, b)
                    for b in range(2):
                        store(T + b - 2, b)
                    for b in range(2):
                        sp.wait_ge(q_x1s[b], 16 * (T // 2))
                        sp.wait_ge(q_xn2s[b], 16 * (T // 2))

                @block.gpsimd
                def _(pool):
                    eights = pool.value_load(starts[0:1, T + 1:T + 2], min_val=2, max_val=-(-CH // G8))

                    def eight(q, first=False):
                        for j in range(G8):
                            h = j // 4
                            if j % 4 == 0:
                                nc.gpsimd.tensor_copy(row_idx[:, h, :], slots[:, ds(q * G8 + j, 4), 0]).then_inc(q_idx, 1)
                                pool.wait_ge(q_idx, q * 2 + h + 1)
                            pool.wait_ge(q_agg, q * G8 + j + 1)
                            pool.sem_inc(q_pass, 1)
                            pool.indirect_dma_start(msg[:, j, :], None, y_dram,
                                                    bass.IndirectOffsetOnAxis(row_idx[:, h, j % 4:j % 4 + 1], 0),
                                                    bounds_check=UNITS * NP - 1).then_inc(q_ga[j], 16)
                            if not (first and j < LAG):
                                pool.wait_ge(q_ga[(j - LAG) % G8], q * 16 + (16 if j >= LAG else 0))
                                pool.sem_inc(q_land, 1)

                    eight(0, True)
                    with pool.Fori(1, eights) as q:
                        eight(q)
                    for j in range(G8 - LAG, G8):
                        pool.wait_ge(q_ga[j], eights * 16)
                        pool.sem_inc(q_land, 1)

                @block.scalar
                def _(act):
                    for k in range(KT):
                        act.wait_ge(q_wg[k % 4], 16 * (k // 4 + 1))
                        nc.scalar.activation(wg_hi[:, k, :], wg_stage[:, k % 4, :], ACT.Copy).then_inc(q_wghi, 1)

                    def gate(j, b):
                        t = j * 2 + b
                        act.wait_ge(q_ut, t + 1)
                        nc.scalar.activation(uT_hi[:, :, :].rearrange("p k c -> p (k c)"), ps_tr[:, :, :].rearrange("p a n -> p (a n)"), ACT.Copy).then_inc(q_uhi, 1)
                        nc.scalar.activation(u_sb[:, b, :], u_sb[:, b, :], ACT.Tanh).then_inc(q_act, 1)
                        act.wait_ge(q_xr[b], j * 16 + 16)
                        nc.scalar.activation(xnr[:, b, :], xr[:, b, :], ACT.Identity, scale=stats[:, ds(t, 1), 1], bias=affine[:, 1, ds(t, 1)]).then_inc(q_xn, 1)
                        act.wait_ge(q_xn, t + 1)
                        nc.scalar.activation(xr[:, b, :], xr[:, b, :], ACT.Identity, scale=affine[:, 0, ds(t, 1)], bias=affine[:, 1, ds(t, 1)]).then_inc(q_act, 1)

                    def logit_copy(t):
                        act.wait_ge(q_n2t, t + 1)
                        nc.scalar.activation(xn2T[:, :, :].rearrange("p k c -> p (k c)"), ps_tr[:, :, :].rearrange("p a n -> p (a n)"), ACT.Copy).then_inc(q_n2c, 1)

                    def stage(j, b):
                        if not (isinstance(j, int) and j == 0):
                            logit_copy(j * 2 + b - 2)
                        gate(j, b)

                    act.wait_ge(q_cst, 5)
                    stages(act, stage)
                    logit_copy(T - 2)
                    logit_copy(T - 1)

                @block.vector
                def _(dve):
                    nc.vector.memset(zero_row[:, :], 0.0)
                    nc.vector.memset(rows[:, :], 0.0).then_inc(q_cst, 1)
                    nc.vector.tensor_copy(slot_loc[:, :], slots[:, :, 2]).then_inc(q_cst, 1)
                    nc.vector.tensor_scalar(affine[:, 0, :], stats[:, :, 1], 1.0, None, ALU.add).then_inc(q_cst, 1)
                    nc.vector.scalar_tensor_tensor(affine[:, 1, :], stats[:, :, 0], -1.0, stats[:, :, 1], ALU.mult, ALU.mult).then_inc(q_cst, 1)
                    nc.vector.tensor_copy(pick[:, :, :], ident[0:3, 0:3].unsqueeze(2).broadcast_to([3, 3, P])).then_inc(q_cst, 1)
                    for k in range(KT):
                        dve.wait_ge(q_wghi, k + 1)
                        nc.vector.tensor_tensor(wg_lo[:, k, :], wg_stage[:, k % 4, :], wg_hi[:, k, :].bitcast(F32), ALU.subtract).then_inc(q_wglo, 1)

                    def messages(t, b):
                        first, last = bounds(dve, t)
                        with dve.Fori(first, last) as i:
                            for j in range(2):
                                g = i * 2 + j
                                dve.wait_ge(q_agg, g + G8 - 1)
                                nc.vector.tensor_scalar(sel[j][:, :], iota_row[:, :], slot_loc[:, ds(g, 1)], winv[:, ds(g, 1)],
                                                        ALU.is_equal, ALU.mult).then_inc(q_sel, 1)

                    def take_u(t, b):
                        dve.wait_ge(q_psu, t + 1)
                        dve.wait_ge(q_yr, t * 16 + 16)
                        nc.vector.tensor_tensor(u_sb[:, b, :], ps_u[:, :, :].rearrange("p a n -> p (a n)"), y_root[:, :], ALU.add).then_inc(q_u, 1)

                    def low_u(t, b):
                        dve.wait_ge(q_uhi, t + 1)
                        nc.vector.tensor_tensor(uT_lo[:, :, :].rearrange("p k c -> p (k c)"), ps_tr[:, :, :].rearrange("p a n -> p (a n)"),
                                                uT_hi[:, :, :].rearrange("p k c -> p (k c)").bitcast(F32), ALU.subtract).then_inc(q_ulo, 1)

                    NS = 12
                    def update(j, b):
                        t = j * 2 + b
                        early = isinstance(j, int) and j == 0
                        n3, n12 = t * 3, t * (NS + 2)
                        dve.wait_ge(q_z, t + 1)
                        dve.wait_ge(q_yg[b], j * 16 + 16)
                        dve.wait_ge(q_act, t * 2 + 2)
                        nc.vector.tensor_tensor(y_gate[:, b, :], ps_z[:, :, :].rearrange("p a n -> p (a n)"), y_gate[:, b, :], ALU.add).then_inc(q_dve, 1)
                        nc.vector.tensor_tensor(xnr[:, b, :], u_sb[:, b, :], xnr[:, b, :], ALU.subtract).then_inc(q_dve, 1)
                        dve.wait_ge(q_dve, n3 + 2)
                        nc.vector.tensor_tensor(y_gate[:, b, :], y_gate[:, b, :], xnr[:, b, :], ALU.mult).then_inc(q_dve, 1)
                        dve.wait_ge(q_dve, n3 + 3)
                        if not early:
                            dve.wait_ge(q_x1s[b], j * 16)
                        nc.vector.tensor_tensor(x1[:, b, :], y_gate[:, b, :], xr[:, b, :], ALU.add).then_inc(q_x1, 1)
                        dve.wait_ge(q_x1, t + 1)
                        for h in range(2):
                            i = nc.vector.bn_stats(bst2[:, h, :], x1[:, b, h * H:(h + 1) * H])
                        k = [0]

                        def step(ins):
                            k[0] += 1
                            ins.then_inc(q_st, 1)
                            dve.wait_ge(q_st, n12 + k[0])

                        step(i)
                        dve.sem_inc(q_pass2, 1)
                        step(nc.vector.bn_aggr(mv2[:, :], bst2[:, :, :].rearrange("p h s -> p (h s)")))
                        nc.vector.tensor_copy(stats2[:, ds(t, 1), 0], mv2[:, 0:1])
                        inverse_root(step, stats2[:, ds(t, 1), 1], mv2[:, 1:2], newton)
                        assert k[0] == NS + 2
                        if not early:
                            dve.wait_ge(q_xn2s[b], j * 16)
                            dve.wait_ge(q_n2t, t - 1)
                        nc.vector.tensor_scalar(xn2[:, b, :], x1[:, b, :], mv2[:, 0:1], stats2[:, ds(t, 1), 1], ALU.subtract, ALU.mult).then_inc(q_xn2, 1)

                    def stage(j, b):
                        t = j * 2 + b
                        messages(t, b)
                        take_u(t, b)
                        low_u(t, b)
                        if not (isinstance(t, int) and t == 0):
                            update(j if b else j - 1, 1 - b)

                    stages(dve, stage)
                    update(T // 2 - 1, 1)
                    dve.wait_ge(q_log, T)
                    nc.vector.tensor_copy(logits[:, :, :], ps_log[:, 0, 0:T * NX1].rearrange("p (t e) -> p t e", e=NX1)).then_inc(q_logc, 1)

                @block.tensor
                def _(pe):
                    pe.sem_inc(q_agg, G8)
                    pe.wait_ge(q_par[0], 48)
                    pe.wait_ge(q_par[1], 16)
                    pe.wait_ge(q_cst, 5)

                    def messages(t, b, opener=False):
                        if not (isinstance(t, int) and t == 0):
                            pe.wait_ge(q_u, t)
                        for h in range(2):
                            nc.tensor.matmul(ps_u[:, h, :], pick[:, 0, :], rows[:, h * H:(h + 1) * H], start=True, stop=False)
                        first, last = bounds(pe, t)
                        with pe.Fori(first, last) as i:
                            for j in range(2):
                                g = i * 2 + j
                                pe.wait_ge(q_sel, g + 1)
                                pe.wait_ge(q_land, g + 1)
                                for h in range(2):
                                    m = nc.tensor.matmul(ps_u[:, h, :], sel[j][:, :],
                                                         msg[:, ds((i % 4) * 2 + j, 1), h * H:(h + 1) * H].rearrange("p a n -> p (a n)"),
                                                         start=False, stop=False)
                                m.then_inc(q_agg, 1)
                        for h in range(2):
                            m = nc.tensor.matmul(ps_u[:, h, :], zero_row[0:1, 0:P], zero_row[0:1, :], start=False, stop=True)
                        m.then_inc(q_psu, 1)

                    def turn_u(t, b):
                        pe.wait_ge(q_u, t + 1)
                        if isinstance(t, int) and t == 1:
                            pe.wait_ge(q_ulo, 1)
                        elif not isinstance(t, int):
                            pe.wait_ge(q_n2c, t - 1)
                        for k in range(KT):
                            m = nc.tensor.transpose(ps_tr[:, k // 4, (k % 4) * P:(k % 4 + 1) * P], u_sb[:, b, k * P:(k + 1) * P], ident[:, :])
                        m.then_inc(q_ut, 1)

                    def gate(t, b):
                        pe.wait_ge(q_ulo, t + 1)
                        if not (isinstance(t, int) and t == 0):
                            pe.wait_ge(q_dve, t * 3 - 2)
                        else:
                            pe.wait_ge(q_wglo, KT)
                        for h in range(2):
                            w = slice(h * H, (h + 1) * H)
                            nc.tensor.matmul(ps_z[:, h, :], pick[:, 1, :], rows[:, w], start=True, stop=False)
                            for k in range(KT):
                                nc.tensor.matmul(ps_z[:, h, :], uT_lo[:, k, :], wg_hi[:, k, w], start=False, stop=False)
                                nc.tensor.matmul(ps_z[:, h, :], uT_hi[:, k, :], wg_lo[:, k, w], start=False, stop=False)
                                m = nc.tensor.matmul(ps_z[:, h, :], uT_hi[:, k, :], wg_hi[:, k, w], start=False, stop=(k == KT - 1))
                        m.then_inc(q_z, 1)

                    def router(t, b):
                        pe.wait_ge(q_xn2, t + 1)
                        pe.wait_ge(q_ulo, min(t + 2, T) if isinstance(t, int) else t + 2)
                        for k in range(KT):
                            m = nc.tensor.transpose(ps_tr[:, k // 4, (k % 4) * P:(k % 4 + 1) * P], xn2[:, b, k * P:(k + 1) * P], ident[:, :])
                        m.then_inc(q_n2t, 1)
                        pe.wait_ge(q_n2c, t + 1)
                        o = ps_log[:, 0, ds(t * NX1, NX1)]
                        nc.tensor.matmul(o, pick[:, 2, :], rows[:, 0:NX1], start=True, stop=False)
                        for k in range(KT):
                            m = nc.tensor.matmul(o, xn2T[:, k, :], rw[:, k, :], start=False, stop=(k == KT - 1))
                        m.then_inc(q_log, 1)

                    def stage(j, b):
                        t = j * 2 + b
                        messages(t, b)
                        if not (isinstance(j, int) and j == 0):
                            router(t - 2, b)
                        turn_u(t, b)
                        gate(t, b)

                    stages(pe, stage)
                    router(T - 2, 0)
                    router(T - 1, 1)

        with ExitStack() as ph:
            FK = F // P
            tok_id = sb(ph, "tok_id", [P, T], I32)
            real = sb(ph, "real", [P, T], F32)
            tri = sb(ph, "tri", [P, NX1, NX1], F32)
            prob = sb(ph, "prob", [P, T, NX1], F32)
            cmp_ = sb(ph, "cmp", [P, 2, T * NX1 * NX1], F32)
            rank = sb(ph, "rank", [P, T, NX1], F32)
            pickAB = sb(ph, "pick_ab", [P, 2, T, NX1], F32)
            tmp9 = sb(ph, "tmp9", [P, T, NX1], F32)
            red = sb(ph, "red", [P, 12, T], F32)
            cume = [sb(ph, f"cume{i}", [P, NX, T], F32) for i in range(2)]
            pre3 = sb(ph, "pre3", [P, 4, 16], F32)
            pre3_i = sb(ph, "pre3_i", [P, 16], I32)
            chunk0 = sb(ph, "chunk0", [P, NX + 1], I32)
            idx_sc = sb(ph, "idx_sc", [P, 2, T], I32)
            idx_ga = sb(ph, "idx_ga", [P, 2, T], I32)
            gates = sb(ph, "gates", [P, 3, T], F32)
            mix = sb(ph, "mix", [P, 2, T], F32)
            tok = sb(ph, "tok", [P, NCH + 1], I32)
            tok_col = sb(ph, "tok_col", [P, 2], I32)
            e_stage = sb(ph, "e_stage", [P, 4, D], F32)
            w1_hi = [sb(ph, f"w1_hi{i}", [P, KT, F], F32R) for i in range(2)]
            w1_lo = [sb(ph, f"w1_lo{i}", [P, KT, F], F32R) for i in range(2)]
            w2_hi = [sb(ph, f"w2_hi{i}", [P, FK, D], F32R) for i in range(2)]
            w2_lo = [sb(ph, f"w2_lo{i}", [P, FK, D], F32R) for i in range(2)]
            xg = sb(ph, "xg", [P, D], F32)
            xgT_hi = sb(ph, "xgT_hi", [P, D], F32R)
            xgT_lo = sb(ph, "xgT_lo", [P, D], F32R)
            h_sb = sb(ph, "h_sb", [P, F], F32)
            hT_hi = sb(ph, "hT_hi", [P, F], F32R)
            hT_lo = sb(ph, "hT_lo", [P, F], F32R)
            y_sb = sb(ph, "y_sb", [P, D], F32)
            ps_x = ps(ph, "ps_x", [P, D])
            ps_h = ps(ph, "ps_h", [P, F])
            ps_hT = ps(ph, "ps_hT", [P, F])
            ps_y2 = ps(ph, "ps_y2", [P, D])
            ps_rt = ps(ph, "ps_rt", [P, 2, H // 2])

            z_cst, z_tab = sem("phase3_constants"), sem("token_table_cleared")
            z_dve, z_exp = sem("routing_chain"), sem("exp_made")
            z_row, z_pre, z_idx = sem("expert_row_totals"), sem("expert_prefixes"), sem("slots_of_choices")
            z_sc, z_tok, z_col = sem("tokens_scattered"), sem("tokens_loaded"), sem("token_column_copied")
            z_w = [sem(f"expert_stage{i}") for i in range(4)]
            z_whi, z_wlo = sem("expert_hi_made"), sem("expert_lo_made")
            z_pe = sem("pe_wait_passed")
            z_xg, z_xt, z_xhi, z_xlo = sem("tokens_gathered"), sem("tokens_turned"), sem("tokens_hi_made"), sem("tokens_lo_made")
            z_h, z_gelu, z_ht = sem("hidden_multiplied"), sem("gelu_made"), sem("hidden_turned")
            z_hhi, z_hlo = sem("hidden_hi_made"), sem("hidden_lo_made")
            z_y, z_yc, z_ys = sem("expert_out_multiplied"), sem("expert_out_copied"), sem("expert_out_stored")

            with nc.Block() as block:
                def all_experts(eng, others):
                    others(0, 0)
                    with eng.Fori(0, NX // 2 - 1) as j:
                        for b in range(2):
                            others(j * 2 + b + 1, 1 - b, lead=True)

                def bounds(eng, e):
                    first = 0 if isinstance(e, int) and e == 0 else eng.value_load(chunk0[0:1, ds(e, 1)], min_val=1, max_val=NCH - 1)
                    last = eng.value_load(chunk0[0:1, ds(e + 1, 1)], min_val=1, max_val=NCH)
                    return first, last

                @block.gpsimd
                def _(pool):
                    nc.gpsimd.iota(tok_id[:, :], [[P, T]], base=0, channel_multiplier=1).then_inc(z_cst, 1)
                    nc.gpsimd.memset(real[:, :], 1.0).then_inc(z_cst, 1)
                    nc.gpsimd.memset(tri[:, :, :], 1.0).then_inc(z_cst, 1)
                    nc.gpsimd.memset(tok[:, :], 0).then_inc(z_cst, 1)
                    pool.wait_ge(z_cst, 4)
                    pool.dma_start(tok_dram.rearrange("(p g) o -> p (g o)", p=P), tok[:, :]).then_inc(z_tab, 16)
                    nc.gpsimd.affine_select(out=real[:, :], in_=real[:, :], compare_op=ALU.is_ge, fill=0.0, base=N - 1,
                                            pattern=[[-P, T]], channel_multiplier=-1).then_inc(z_cst, 1)
                    nc.gpsimd.affine_select(out=tri[:, :, :], in_=tri[:, :, :], compare_op=ALU.is_gt, fill=0.0, base=0,
                                            pattern=[[1, NX1], [-1, NX1]], channel_multiplier=0).then_inc(z_cst, 1)
                    pool.wait_ge(z_tab, 16)
                    pool.wait_ge(z_idx, 1)
                    for c in range(2):
                        for t in range(T):
                            pool.indirect_dma_start(tok_dram, bass.IndirectOffsetOnAxis(idx_sc[:, c, t:t + 1], 0),
                                                    tok_id[:, t:t + 1], None, bounds_check=NCH * P - 1,
                                                    oob_is_err=False).then_inc(z_sc, 16)
                    pool.wait_ge(z_sc, 16 * 2 * T)
                    pool.dma_start(tok[:, :], tok_dram.rearrange("(g p) o -> p (g o)", p=P), allow_slow_non_contiguous=True).then_inc(z_tok, 16)
                    pool.wait_ge(z_tok, 16)
                    total = pool.value_load(chunk0[0:1, NX:NX + 1], min_val=NX, max_val=NCH)

                    def gather(g):
                        nc.gpsimd.tensor_copy(tok_col[:, 0:1], tok[:, ds(g, 1)]).then_inc(z_col, 1)
                        pool.wait_ge(z_col, g + 1)
                        pool.sem_inc(z_pass, 1)
                        pool.indirect_dma_start(xg[:, :], None, xn2_dram, bass.IndirectOffsetOnAxis(tok_col[:, 0:1], 0),
                                                bounds_check=NP - 1).then_inc(z_xg, 16)

                    gather(0)
                    with pool.Fori(1, total + 1) as g:
                        pool.wait_ge(z_xg, g * 16)
                        pool.wait_ge(z_xt, g)
                        gather(g)
                    pool.wait_ge(z_xg, total * 16 + 16)

                @block.sync
                def _(sp):
                    w1_t = w1.rearrange("e (q k p) f -> e q p k f", p=P, k=2)
                    w2_t = w2.rearrange("e (k p) n -> e k p n", p=P)

                    def weights(e, first=False):
                        for q in range(8):
                            if not (first and q < 4):
                                sp.wait_ge(z_wlo, e * 8 + (q - 3))
                            part = w1_t[ds(e, 1), q, :, :, :].rearrange("e p k f -> (e p) k f") if q < 4 else \
                                w2_t[ds(e, 1), q - 4, :, :].rearrange("e p n -> (e p) n")
                            to = e_stage[:, q % 4, :].rearrange("p (k f) -> p k f", k=2) if q < 4 else e_stage[:, q % 4, :]
                            sp.dma_start(to, part).then_inc(z_w[q % 4], 16)

                    weights(0, True)
                    with sp.Fori(1, NX) as e:
                        weights(e)

                @block.scalar
                def _(act):
                    act.sem_inc(z_ys, 16)
                    act.sem_inc(z_yc, 2)
                    act.wait_ge(z_dve, 1)
                    nc.scalar.activation(prob[:, :, :], prob[:, :, :], ACT.Exp).then_inc(z_exp, 1)

                    def split_hi(e, b, q):
                        act.wait_ge(z_w[q % 4], e * 32 + (q // 4) * 16 + 16)
                        to = w1_hi[b][:, 2 * q:2 * q + 2, :].rearrange("p k f -> p (k f)") if q < 4 else w2_hi[b][:, q - 4, :]
                        nc.scalar.activation(to, e_stage[:, q % 4, :], ACT.Copy).then_inc(z_whi, 1)

                    def turn_hi(n):
                        act.wait_ge(z_xt, n)
                        nc.scalar.activation(xgT_hi[:, :], ps_x[:, :], ACT.Copy).then_inc(z_xhi, 1)

                    def hidden_hi(g):
                        act.wait_ge(z_ht, g + 1)
                        nc.scalar.activation(hT_hi[:, :], ps_hT[:, :], ACT.Copy).then_inc(z_hhi, 1)

                    def gelu(g):
                        act.wait_ge(z_h, g + 1)
                        nc.scalar.activation(h_sb[:, :], ps_h[:, :], ACT.Gelu).then_inc(z_gelu, 1)

                    def take_y(g):
                        act.wait_ge(z_y, g + 1)
                        act.wait_ge(z_ys, g * 16 + 16)
                        nc.scalar.activation(y_sb[:, 0:H], ps_y2[:, 0:H], ACT.Copy).then_inc(z_yc, 1)
                        act.wait_ge(z_yc, g * 2 + 4)
                        act.dma_start(ye_dram.rearrange("(g p) n -> g p n", p=P)[ds(g, 1), :, :].rearrange("g p n -> (g p) n"),
                                      y_sb[:, :]).then_inc(z_ys, 16)

                    def step(g, parts=()):
                        hidden_hi(g - 1)
                        for p in parts[:2]:
                            split_hi(*p)
                        gelu(g)
                        turn_hi(g + 2)
                        for p in parts[2:]:
                            split_hi(*p)
                        take_y(g - 1)

                    def expert(e, b, lead=False, more=True):
                        first, last = bounds(act, e)
                        parts = [[(e + 1, 1 - b, 4 * i + q) for q in range(4)] if more else [] for i in range(2)]
                        if lead:
                            step(first, parts[0])
                        else:
                            for p in parts[0]:
                                split_hi(*p)
                        if more:
                            with act.If(last - first < 2):
                                for p in parts[1]:
                                    split_hi(*p)
                        with act.If(first + 1 < last):
                            step(first + 1, parts[1])
                            with act.If(first + 2 < last):
                                with act.Fori(first + 2, last) as g:
                                    step(g)

                    for q in range(4):
                        split_hi(0, 0, q)
                    turn_hi(1)
                    for q in range(4, 8):
                        split_hi(0, 0, q)
                    gelu(0)
                    turn_hi(2)
                    all_experts(act, expert)
                    expert(NX - 1, 1, True, False)
                    total = act.value_load(chunk0[0:1, NX:NX + 1], min_val=NX, max_val=NCH)
                    hidden_hi(total - 1)
                    take_y(total - 1)
                    with act.If(total < NCH):
                        with act.Fori(total, NCH) as g:
                            act.dma_start(ye_dram.rearrange("(g p) n -> g p n", p=P)[ds(g, 1), :, :].rearrange("g p n -> (g p) n"),
                                          y_sb[:, :]).then_inc(z_ys, 16)
                    act.wait_ge(z_ys, NCH * 16 + 16)

                @block.vector
                def _(dve):
                    n = [0]

                    def step(ins):
                        n[0] += 1
                        ins.then_inc(z_dve, 1)
                        dve.wait_ge(z_dve, n[0])

                    flat = "p t e -> p (t e)"
                    nc.vector.tensor_reduce(red[:, 0, :], logits[:, :, :], AX.X, ALU.max).then_inc(z_row, 1)
                    dve.wait_ge(z_row, 1)
                    step(nc.vector.tensor_tensor(prob[:, :, :], logits[:, :, :], red[:, 0, :].unsqueeze(2).broadcast_to([P, T, NX1]), ALU.subtract))
                    dve.wait_ge(z_exp, 1)
                    step(nc.vector.tensor_reduce(red[:, 1, :], prob[:, :, :], AX.X, ALU.add))
                    step(nc.vector.reciprocal(red[:, 2, :], red[:, 1, :]))
                    step(nc.vector.tensor_tensor(prob[:, :, :], prob[:, :, :], red[:, 2, :].unsqueeze(2).broadcast_to([P, T, NX1]), ALU.mult))
                    gt = cmp_[:, 0, :].rearrange("p (t j i) -> p t j i", j=NX1, i=NX1)
                    eq = cmp_[:, 1, :].rearrange("p (t j i) -> p t j i", j=NX1, i=NX1)
                    p_i = prob[:, :, :].unsqueeze(2).broadcast_to([P, T, NX1, NX1])
                    p_j = prob[:, :, :].unsqueeze(3).broadcast_to([P, T, NX1, NX1])
                    dve.wait_ge(z_cst, 6)
                    nc.vector.tensor_tensor(gt, p_i, p_j, ALU.is_gt)
                    step(nc.vector.tensor_tensor(eq, p_i, p_j, ALU.is_equal))
                    step(nc.vector.tensor_tensor(eq, eq, tri[:, :, :].unsqueeze(1).broadcast_to([P, T, NX1, NX1]), ALU.mult))
                    step(nc.vector.tensor_tensor(cmp_[:, 0, :], cmp_[:, 0, :], cmp_[:, 1, :], ALU.add))
                    step(nc.vector.tensor_reduce(rank[:, :, :], gt, AX.X, ALU.add))
                    for c in range(2):
                        step(nc.vector.tensor_scalar(pickAB[:, c, :, :], rank[:, :, :], float(c), None, ALU.is_equal))
                    for c in range(2):
                        step(nc.vector.tensor_tensor(pickAB[:, c, :, :], pickAB[:, c, :, :], real[:, :].unsqueeze(2).broadcast_to([P, T, NX1]), ALU.mult))
                    step(nc.vector.tensor_tensor(cume[0][:, :, :], pickAB[:, 0, :, 0:NX].rearrange("p t e -> p e t"),
                                                 pickAB[:, 1, :, 0:NX].rearrange("p t e -> p e t"), ALU.add))
                    a, b, d = cume[0], cume[1], 1
                    while d < T:
                        nc.vector.tensor_copy(b[:, :, 0:d], a[:, :, 0:d])
                        step(nc.vector.tensor_tensor(b[:, :, d:T], a[:, :, d:T], a[:, :, 0:T - d], ALU.add))
                        a, b, d = b, a, 2 * d
                    nc.vector.tensor_copy(pre3[:, 0, 0:NX], a[:, :, T - 1]).then_inc(z_row, 1)
                    for c in range(2):
                        step(nc.vector.tensor_tensor(tmp9[:, :, :], prob[:, :, :], pickAB[:, c, :, :], ALU.mult))
                        step(nc.vector.tensor_reduce(gates[:, c, :], tmp9[:, :, 0:NX], AX.X, ALU.add))
                        step(nc.vector.tensor_copy(red[:, 3 + c, :], tmp9[:, :, NX]))
                    step(nc.vector.tensor_tensor(gates[:, 2, :], red[:, 3, :], red[:, 4, :], ALU.add))
                    step(nc.vector.tensor_tensor(red[:, 5, :], gates[:, 2, :], stats2[:, :, 1], ALU.mult))
                    nc.vector.tensor_scalar(mix[:, 0, :], red[:, 5, :], 1.0, None, ALU.add)
                    step(nc.vector.scalar_tensor_tensor(mix[:, 1, :], red[:, 5, :], -1.0, stats2[:, :, 0], ALU.mult, ALU.mult))
                    dve.wait_ge(z_pre, 1)
                    step(nc.vector.tensor_scalar(pre3_i[:, 0:NX], ps_rt[:, 1, 0:NX], float(P - 1), None, ALU.add))
                    step(nc.vector.tensor_scalar(pre3_i[:, 0:NX], pre3_i[:, 0:NX], P.bit_length() - 1, None, ALU.arith_shift_right))
                    nc.vector.memset(pre3[:, 2, 0:1], 0.0)
                    step(nc.vector.tensor_scalar(pre3[:, 1, 0:NX], pre3_i[:, 0:NX], 1.0, None, ALU.max))
                    for k in range(NX):
                        step(nc.vector.tensor_tensor(pre3[:, 2, k + 1:k + 2], pre3[:, 2, k:k + 1], pre3[:, 1, k:k + 1], ALU.add))
                    nc.vector.tensor_copy(chunk0[:, :], pre3[:, 2, 0:NX + 1])
                    step(nc.vector.scalar_tensor_tensor(pre3[:, 3, 0:NX], pre3[:, 2, 0:NX], float(P), ps_rt[:, 0, 0:NX], ALU.mult, ALU.add))
                    step(nc.vector.tensor_scalar(pre3[:, 3, 0:NX], pre3[:, 3, 0:NX], -1.0, None, ALU.add))
                    step(nc.vector.tensor_tensor(b[:, :, :], a[:, :, :], pre3[:, 3, 0:NX].unsqueeze(2).broadcast_to([P, NX, T]), ALU.add))
                    for c in range(2):
                        chosen = pickAB[:, c, :, 0:NX]
                        step(nc.vector.tensor_tensor(tmp9[:, :, 0:NX], chosen, b[:, :, :].rearrange("p e t -> p t e"), ALU.mult))
                        step(nc.vector.tensor_reduce(red[:, 6, :], tmp9[:, :, 0:NX], AX.X, ALU.add))
                        step(nc.vector.tensor_copy(idx_ga[:, c, :], red[:, 6, :]))
                        step(nc.vector.tensor_reduce(red[:, 7, :], chosen, AX.X, ALU.add))
                        step(nc.vector.tensor_scalar(red[:, 7, :], red[:, 7, :], -float(2 * NCH * P), float(2 * NCH * P), ALU.mult, ALU.add))
                        step(nc.vector.tensor_tensor(idx_sc[:, c, :], red[:, 6, :], red[:, 7, :], ALU.add))
                    dve.sem_inc(z_idx, 1)

                    def split_lo(e, b, q):
                        dve.wait_ge(z_whi, e * 8 + q + 1)
                        hi = w1_hi[b][:, 2 * q:2 * q + 2, :].rearrange("p k f -> p (k f)") if q < 4 else w2_hi[b][:, q - 4, :]
                        lo = w1_lo[b][:, 2 * q:2 * q + 2, :].rearrange("p k f -> p (k f)") if q < 4 else w2_lo[b][:, q - 4, :]
                        nc.vector.tensor_tensor(lo, e_stage[:, q % 4, :], hi.bitcast(F32), ALU.subtract).then_inc(z_wlo, 1)

                    def turn_lo(n):
                        dve.wait_ge(z_xhi, n)
                        nc.vector.tensor_tensor(xgT_lo[:, :], ps_x[:, :], xgT_hi[:, :].bitcast(F32), ALU.subtract).then_inc(z_xlo, 1)

                    def hidden_lo(g):
                        dve.wait_ge(z_hhi, g + 1)
                        nc.vector.tensor_tensor(hT_lo[:, :], ps_hT[:, :], hT_hi[:, :].bitcast(F32), ALU.subtract).then_inc(z_hlo, 1)

                    def take_y(g):
                        dve.wait_ge(z_y, g + 1)
                        dve.wait_ge(z_ys, g * 16 + 16)
                        nc.vector.tensor_copy(y_sb[:, H:D], ps_y2[:, H:D]).then_inc(z_yc, 1)

                    def low_step(g, parts=()):
                        hidden_lo(g - 1)
                        for p in parts[:2]:
                            split_lo(*p)
                        turn_lo(g + 2)
                        for p in parts[2:]:
                            split_lo(*p)
                        take_y(g - 1)

                    def expert(e, b, lead=False, more=True):
                        first, last = bounds(dve, e)
                        parts = [[(e + 1, 1 - b, 4 * i + q) for q in range(4)] if more else [] for i in range(2)]
                        if lead:
                            low_step(first, parts[0])
                        else:
                            for p in parts[0]:
                                split_lo(*p)
                        if more:
                            with dve.If(last - first < 2):
                                for p in parts[1]:
                                    split_lo(*p)
                        with dve.If(first + 1 < last):
                            low_step(first + 1, parts[1])
                            with dve.If(first + 2 < last):
                                with dve.Fori(first + 2, last) as g:
                                    low_step(g)

                    for q in range(4):
                        split_lo(0, 0, q)
                    turn_lo(1)
                    for q in range(4, 8):
                        split_lo(0, 0, q)
                    turn_lo(2)
                    all_experts(dve, expert)
                    expert(NX - 1, 1, True, False)
                    total = dve.value_load(chunk0[0:1, NX:NX + 1], min_val=NX, max_val=NCH)
                    hidden_lo(total - 1)
                    take_y(total - 1)

                @block.tensor
                def _(pe):
                    pe.wait_ge(z_row, 2)
                    nc.tensor.matmul(ps_rt[:, 0, 0:NX], lower[:, :], pre3[:, 0, 0:NX], start=True, stop=True)
                    nc.tensor.matmul(ps_rt[:, 1, 0:NX], ones[:, :], pre3[:, 0, 0:NX], start=True, stop=True).then_inc(z_pre, 1)
                    pe.wait_ge(z_idx, 1)

                    def turn(n):
                        pe.wait_ge(z_xg, n * 16)
                        for k in range(KT):
                            m = nc.tensor.transpose(ps_x[:, k * P:(k + 1) * P], xg[:, k * P:(k + 1) * P], ident[:, :])
                        m.then_inc(z_xt, 1)

                    def first_product(g, b):
                        pe.wait_ge(z_xlo, g + 1)
                        for k in range(KT):
                            w = slice(k * P, (k + 1) * P)
                            nc.tensor.matmul(ps_h[:, :], xgT_lo[:, w], w1_hi[b][:, k, :], start=(k == 0), stop=False)
                            nc.tensor.matmul(ps_h[:, :], xgT_hi[:, w], w1_lo[b][:, k, :], start=False, stop=False)
                            m = nc.tensor.matmul(ps_h[:, :], xgT_hi[:, w], w1_hi[b][:, k, :], start=False, stop=(k == KT - 1))
                        m.then_inc(z_h, 1)

                    def turn_hidden(g):
                        pe.wait_ge(z_gelu, g + 1)
                        for k in range(FK):
                            m = nc.tensor.transpose(ps_hT[:, k * P:(k + 1) * P], h_sb[:, k * P:(k + 1) * P], ident[:, :])
                        m.then_inc(z_ht, 1)

                    def second_product(g, b):
                        pe.wait_ge(z_hlo, g + 1)
                        pe.wait_ge(z_yc, g * 2 + 2)
                        for h in range(2):
                            o = slice(h * H, (h + 1) * H)
                            for k in range(FK):
                                w = slice(k * P, (k + 1) * P)
                                nc.tensor.matmul(ps_y2[:, o], hT_lo[:, w], w2_hi[b][:, k, o], start=(k == 0), stop=False)
                                nc.tensor.matmul(ps_y2[:, o], hT_hi[:, w], w2_lo[b][:, k, o], start=False, stop=False)
                                m = nc.tensor.matmul(ps_y2[:, o], hT_hi[:, w], w2_hi[b][:, k, o], start=False, stop=(k == FK - 1))
                        m.then_inc(z_y, 1)

                    def step(g, b, b_before):
                        turn_hidden(g - 1)
                        first_product(g, b)
                        turn(g + 2)
                        second_product(g - 1, b_before)

                    def expert(e, b, lead=False):
                        first, last = bounds(pe, e)
                        if lead:
                            pe.wait_ge(z_wlo, e * 8 + 4)
                            pe.sem_inc(z_pe, 1)
                            step(first, b, 1 - b)
                        with pe.If(first + 1 < last):
                            pe.wait_ge(z_wlo, e * 8 + 8)
                            pe.sem_inc(z_pe, 1)
                            with pe.Fori(first + 1, last) as g:
                                step(g, b, b)

                    turn(1)
                    pe.wait_ge(z_wlo, 4)
                    first_product(0, 0)
                    turn(2)
                    all_experts(pe, expert)
                    expert(NX - 1, 1, True)
                    total = pe.value_load(chunk0[0:1, NX:NX + 1], min_val=NX, max_val=NCH)
                    turn_hidden(total - 1)
                    pe.wait_ge(z_wlo, NX * 8)
                    second_product(total - 1, 1)

            ya = [e_stage[:, i, :] for i in range(2)]
            yb = [e_stage[:, 2 + i, :] for i in range(2)]
            xo = [xg[:, :], y_sb[:, :]]
            f_x, f_ga, f_mix, f_sum = [sem(f"x1_loaded{i}") for i in range(2)], [sem(f"out_gathered{i}") for i in range(2)], sem("x1_mixed"), sem("out_summed")
            f_out = [sem(f"out_stored{i}") for i in range(2)]
            with nc.Block() as block:
                @block.gpsimd
                def _(pool):
                    for t in range(T):
                        b = t % 2
                        if t >= 2:
                            pool.wait_ge(f_sum, 2 * (t - 2) + 2)
                        for c, to in enumerate((ya[b], yb[b])):
                            pool.indirect_dma_start(to, None, ye_dram, bass.IndirectOffsetOnAxis(idx_ga[:, c, t:t + 1], 0),
                                                    bounds_check=NCH * P - 1).then_inc(f_ga[b], 16)

                @block.sync
                def _(sp):
                    for t in range(T):
                        b = t % 2
                        if t >= 2:
                            sp.wait_ge(f_sum, 2 * (t - 2) + 2)
                            sp.dma_start(out[(t - 2) * P:(t - 1) * P, :], xo[b]).then_inc(f_out[b], 16)
                            sp.wait_ge(f_out[b], 16 * (t // 2))
                        sp.dma_start(xo[b], x1_dram[t * P:(t + 1) * P, :]).then_inc(f_x[b], 16)
                    for t in (T - 2, T - 1):
                        n = LAST if t == T - 1 else P
                        sp.wait_ge(f_sum, 2 * t + 2)
                        sp.dma_start(out[t * P:t * P + n, :], xo[t % 2][0:n, :]).then_inc(f_out[t % 2], 16)
                    for b in range(2):
                        sp.wait_ge(f_out[b], 16 * (T // 2))

                @block.scalar
                def _(act):
                    for t in range(T):
                        b = t % 2
                        act.wait_ge(f_x[b], 16 * (t // 2 + 1))
                        nc.scalar.activation(xo[b], xo[b], ACT.Identity, scale=mix[:, 0, t:t + 1], bias=mix[:, 1, t:t + 1]).then_inc(f_mix, 1)

                @block.vector
                def _(dve):
                    for t in range(T):
                        b = t % 2
                        dve.wait_ge(f_mix, t + 1)
                        dve.wait_ge(f_ga[b], 32 * (t // 2 + 1))
                        nc.vector.scalar_tensor_tensor(xo[b], ya[b], gates[:, 0, t:t + 1], xo[b], ALU.mult, ALU.add).then_inc(f_sum, 1)
                        dve.wait_ge(f_sum, 2 * t + 1)
                        nc.vector.scalar_tensor_tensor(xo[b], yb[b], gates[:, 1, t:t + 1], xo[b], ALU.mult, ALU.add).then_inc(f_sum, 1)


def kernel(**inputs):
    import numpy as np
    import concourse.bacc as bacc
    from concourse import mybir
    from concourse.bass_utils import run_bass_kernel_spmd

    a = lay_out(inputs)
    nc = bacc.Bacc("TRN2", target_bir_lowering=False, num_devices=1)
    args = {k: nc.dram_tensor(k, v.shape, mybir.dt.from_np(v.dtype), kind="ExternalInput").ap() for k, v in a.items()}
    out = nc.dram_tensor("out", inputs["x"].shape, mybir.dt.float32, kind="ExternalOutput").ap()
    build_program(nc, out=out, **args)
    r = run_bass_kernel_spmd(nc, [a], core_ids=[0])
    return r.results[0]["out"]


def lay_out(inputs):
    import numpy as np
    g = {k: np.ascontiguousarray(v) for k, v in inputs.items()}
    d = g["x"].shape[1]
    return dict(x=g["x"], src=g["src"], dst=g["dst"], typ=g["edge_type_8"],
                w_all=np.concatenate([g["L0_gnn_weight"], g["L0_gnn_root"][None], g["L0_gnn_w_gate"][None, d:]]),
                bias=g["L0_gnn_bias"][None], w_gate_u=g["L0_gnn_w_gate"][:d], b_gate=g["L0_gnn_b_gate"][None],
                router_w=g["L0_ffn_router_w"], router_b=g["L0_ffn_router_b"][None], w1=g["L0_ffn_w1"], w2=g["L0_ffn_w2"])
```

```python
def build_program(nc, x, src, dst, typ, w_all, bias, w_gate_u, b_gate, router_w, router_b, w1, w2, out, upto=99, dbg=None):
    from contextlib import ExitStack
    import concourse.bass as bass
    from concourse import mybir

    F32, F32R, BF16, I32 = mybir.dt.float32, mybir.dt.float32r, mybir.dt.bfloat16, mybir.dt.int32
    F8 = mybir.dt.float8e4
    ALU, ACT, AX = mybir.AluOpType, mybir.ActivationFunctionType, mybir.AxisListType
    ds = bass.ds

    P = 128
    N, D = x.shape
    T = -(-N // P)
    NP = T * P
    LAST = N - (T - 1) * P
    KT = D // P
    H = 512
    UNITS = w_all.shape[0]
    R = UNITS - 2
    ROOT, GATE_X = R, R + 1
    E = src.shape[0]
    EP = 125
    EC = E // EP
    PAIR = 2 * P
    PAIRS = (E + T * PAIR) // PAIR
    CH = 16 * -(-PAIRS // 8)
    PC = 8
    NPIECE = EC // PC
    SC = 8
    EPS = 1e-5
    TR = T * R
    NX, F = w1.shape[0], w1.shape[2]
    NX1 = NX + 1
    NCH = (2 * N + NX * P) // P

    ctx = ExitStack()

    def sem(name):
        return ctx.enter_context(nc.semaphore(name))

    def dram(name, shape, dt):
        return nc.dram_tensor(name, shape, dt, kind="Internal").ap()

    y_dram = dram("y_scratch", [UNITS * NP, D], F32)
    winv_dram = dram("winv_scratch", [TR * P, 1], F32)
    x1_dram = dram("x1_scratch", [NP, D], F32)
    xn2_dram = dram("xn2_scratch", [NP, D], F32)
    ye_dram = dram("ye_scratch", [NCH * P, D], F32)
    tok_dram = dram("tok_scratch", [(NCH + 1) * P, 1], I32)
    slot_dram = dram("slot_scratch", [CH * P, 4], I32)

    with ctx:
        def sb(stack, name, shape, dt):
            return stack.enter_context(nc.sbuf_tensor(name, shape, dt))

        def ps(stack, name, shape, dt=F32):
            return stack.enter_context(nc.psum_tensor(name, shape, dt))

        ident = sb(ctx, "ident", [P, P], F32)
        lower = sb(ctx, "lower", [P, P], F32)
        ones = sb(ctx, "ones", [P, P], F32)
        iota_row = sb(ctx, "iota_row", [P, P], F32)
        stats = sb(ctx, "stats", [P, T, 2], F32)
        starts = sb(ctx, "starts", [P, T + 2], I32)
        slots = sb(ctx, "slots", [P, CH, 4], I32)
        stats2 = sb(ctx, "stats2", [P, T, 2], F32)
        logits = sb(ctx, "logits", [P, T, NX1], F32)
        newton = sb(ctx, "newton", [P, 4], F32)
        winv = sb(ctx, "winv", [P, CH], F32)

        def inverse_root(step, out_, var, tmp):
            v, a, y = tmp[:, 0:1], tmp[:, 1:2], tmp[:, 2:3]
            step(nc.vector.tensor_scalar(v, var, EPS, None, ALU.add))
            step(nc.vector.tensor_scalar(a.bitcast(I32), v.bitcast(I32), 1, None, ALU.arith_shift_right))
            step(nc.vector.tensor_scalar(y.bitcast(I32), a.bitcast(I32), -1.0, float(0x5F3759DF), ALU.mult, ALU.add))
            for n in range(3):
                step(nc.vector.tensor_scalar(a, y, y, v, ALU.mult, ALU.mult))
                step(nc.vector.tensor_scalar(a, a, -0.5, 1.5, ALU.mult, ALU.add))
                y_new = out_ if n == 2 else y
                step(nc.vector.tensor_tensor(y_new, y, a, ALU.mult))

        with ExitStack() as ph:
            xs = sb(ph, "xs", [P, 2, D], F32)
            xn = sb(ph, "xn", [P, 2, D], F32)
            bst = sb(ph, "bst", [P, 2, 2, 6], F32)
            mv = sb(ph, "mv", [P, 2, 2], F32)
            xT_hi = sb(ph, "xT_hi", [P, KT, NP], F32R)
            xT_lo = sb(ph, "xT_lo", [P, KT, NP], F32R)
            w_stage = sb(ph, "w_stage", [P, 4, 2, H], F32)
            w_hi = [sb(ph, f"w_hi{i}", [P, KT, H], F32R) for i in range(2)]
            w_lo = [sb(ph, f"w_lo{i}", [P, KT, H], F32R) for i in range(2)]
            y_out = w_out = sb(ph, "y_out", [P, 4, H], F32)
            ps_t = ps(ph, "ps_t", [P, 2, H])
            ps_y = ps(ph, "ps_y", [P, 4, H])
            ps_cnt = ps(ph, "ps_cnt", [P, H])
            ps_pre = ps(ph, "ps_pre", [P, 2, H // 2])

            edge_i = sb(ph, "edge_i", [EP, 3, EC], I32)
            tile_i = sb(ph, "tile_i", [EP, EC], I32)
            loc_i = edge_i[:, 1, :]
            edge_f = sb(ph, "edge_f", [EP, 5, EC], F32)
            ohT = sb(ph, "ohT", [EP, T, EC], BF16)
            cum = [v[0:EP, :, :].rearrange("p a b -> p (a b)")[:, 0:T * EC].rearrange("p (k c) -> p k c", k=T) for v in (xs, xn)]
            slot_f = edge_i[:, 0, :].bitcast(F32)
            slot_i = sb(ph, "slot_i", [EP, EC], I32)
            rec = sb(ph, "rec", [EP, EC, 4], I32)
            oh_key = sb(ph, "oh_key", [EP, 2, PC, TR], F8)
            oh_loc = sb(ph, "oh_loc", [EP, 2, PC, P], F8)
            pre = sb(ph, "pre", [P, 6, 16], F32)
            pre_i = sb(ph, "pre_i", [P, 16], I32)
            cnt = sb(ph, "cnt", [TR, 2, P], F32)
            fill = slots
            rec_buf = sb(ph, "rec_buf", [EP, 2, SC, 4], I32)
            idx_buf = sb(ph, "idx_buf", [P, 2, SC], I32)
            win_buf = sb(ph, "win_buf", [P, 2, SC], F32)

            s_x = [sem(f"x_loaded{i}") for i in range(2)]
            s_xpad = sem("x_padded")
            s_const = sem("constants_made")
            s_stat = sem("stats_chain")
            s_pass, q_pass, q_pass2, z_pass = (sem(f"wait_passed{i}") for i in range(4))
            s_xn = sem("x_normed")
            s_xT = sem("x_transposed")
            s_xhi = sem("xT_hi_made")
            s_xlo = sem("xT_lo_made")
            s_w = [sem(f"w_loaded{i}") for i in range(4)]
            s_whi = sem("w_hi_made")
            s_wlo = sem("w_lo_made")
            s_half = sem("half_multiplied")
            s_y = sem("y_multiplied")
            s_ysb = sem("y_copied")
            s_yst = [sem(f"y_stored{i}") for i in range(4)]
            s_edge = sem("edges_loaded")
            s_fill = sem("filler_made")
            s_fst = sem("filler_stored")
            s_dve = sem("sort_chain")
            s_oh = sem("onehots_made")
            s_ohu = sem("onehots_used")
            s_row = sem("row_totals_made")
            s_pre = sem("prefixes_multiplied")
            s_cinv = sem("winv_made")
            s_cst = sem("winv_stored")
            s_rec = sem("records_made")
            s_cp = sem("scatter_copied")
            s_sc = [sem(f"scattered{i}") for i in range(2)]
            s_sl = sem("slots_loaded")
            s_ga = [sem(f"winv_gathered{i}") for i in range(2)]

            assert T - 1 + 4 <= NPIECE <= 2 * T + 3
            y_view = y_dram.rearrange("(u t p) (h n) -> u t p h n", t=T, p=P, h=2)
            w_view = w_all.rearrange("u (k p) (h n) -> u p k h n", p=P, h=2)

            with nc.Block() as block:
                @block.sync
                def _(sp):
                    for i in range(2):
                        sp.dma_start(xs[:, i, :], x[i * P:(i + 1) * P, :]).then_inc(s_x[i], 16)
                    for i, a in enumerate((src, dst, typ)):
                        sp.dma_start(edge_i[:, i, :], a.rearrange("(p c) -> p c", c=EC)).then_inc(s_edge, 16)

                    def load_w(u, half):
                        for q in range(4):
                            n = u * 2 + half
                            if not (isinstance(n, int) and n == 0):
                                sp.wait_ge(s_wlo, n * 4 - 3 + q)
                            sp.dma_start(w_stage[:, q, :, :], w_view[ds(u, 1), :, 2 * q:2 * q + 2, half, :]
                                         .rearrange("u p k n -> (u p) k n")).then_inc(s_w[q], 16)

                    load_w(0, 0)
                    for t in range(2, T):
                        sp.wait_ge(s_xn, t - 1)
                        if t < T - 1:
                            sp.dma_start(xs[:, t % 2, :], x[t * P:(t + 1) * P, :]).then_inc(s_x[t % 2], 16)
                        else:
                            sp.wait_ge(s_xpad, 1)
                            sp.dma_start(xs[0:LAST, t % 2, :], x[t * P:N, :]).then_inc(s_x[t % 2], 16)
                        if t == T // 2:
                            load_w(0, 1)

                    def store_y(u, half):
                        for t in range(T):
                            sp.wait_ge(s_ysb, (u * 2 + half) * T + t + 1)
                            sp.dma_start(y_view[ds(u, 1), t, :, half, :].rearrange("u p n -> (u p) n"),
                                         y_out[:, (half * T + t) % 4, :]).then_inc(s_yst[(half * T + t) % 4], 16)

                    load_w(1, 0)
                    load_w(1, 1)
                    store_y(0, 1)
                    with sp.Fori(1, UNITS - 1) as u:
                        for half in range(2):
                            load_w(u + 1, half)
                            store_y(u, half)
                    for half in range(2):
                        store_y(UNITS - 1, half)
                    for i in range(4):
                        sp.wait_ge(s_yst[i], 16 * UNITS * 2 * T // 4)

                @block.gpsimd
                def _(pool):
                    nc.gpsimd.memset(ident[:, :], 0.0).then_inc(s_const, 1)
                    nc.gpsimd.memset(lower[:, :], 1.0).then_inc(s_const, 1)
                    nc.gpsimd.memset(ones[:, :], 1.0).then_inc(s_const, 1)
                    nc.gpsimd.iota(iota_row[:, :], [[1, P]], base=0, channel_multiplier=0,
                                   allow_small_or_imprecise_dtypes=True).then_inc(s_const, 1)
                    pool.wait_ge(s_const, 4)
                    nc.gpsimd.affine_select(out=ident[:, :], in_=ident[:, :], compare_op=ALU.not_equal, fill=1.0,
                                            base=0, pattern=[[-1, P]], channel_multiplier=1).then_inc(s_const, 1)
                    nc.gpsimd.affine_select(out=lower[:, :], in_=lower[:, :], compare_op=ALU.is_gt, fill=0.0,
                                            base=0, pattern=[[1, P]], channel_multiplier=-1).then_inc(s_const, 1)
                    nc.gpsimd.memset(fill[:, :, :], 0).then_inc(s_fill, 1)
                    pool.wait_ge(s_fill, 1)
                    nc.gpsimd.memset(fill[:, :, 2:3], 2 * P - 1).then_inc(s_fill, 1)
                    pool.wait_ge(s_fill, 2)
                    pool.dma_start(slot_dram.rearrange("(p g) w -> p (g w)", p=P),
                                   fill[:, :, :].rearrange("p g w -> p (g w)")).then_inc(s_fst, 16)
                    pool.wait_ge(s_fst, 16)
                    pool.wait_ge(s_cinv, 1)
                    pool.dma_start(winv_dram.rearrange("(k c) o -> k (c o)", c=P), cnt[:, 1, :]).then_inc(s_cst, 16)
                    pool.wait_ge(s_rec, 1)

                    def scatter(i, first=False):
                        for b in range(2):
                            n = i * 2 + b
                            if not first:
                                pool.wait_ge(s_sc[b], i * (16 * SC))
                            nc.gpsimd.tensor_copy(rec_buf[:, b, :, :], rec[:, ds(n * SC, SC), :]).then_inc(s_cp, 1)
                            nc.gpsimd.tensor_copy(idx_buf[0:EP, b, :], slot_i[:, ds(n * SC, SC)]).then_inc(s_cp, 1)
                            pool.wait_ge(s_cp, n * 2 + 2)
                            pool.sem_inc(s_pass, 1)
                            for c in range(SC):
                                pool.indirect_dma_start(
                                    slot_dram, bass.IndirectOffsetOnAxis(idx_buf[0:EP, b, c:c + 1], 0),
                                    rec_buf[:, b, c, :], None, bounds_check=CH * P - 1).then_inc(s_sc[b], 16)

                    scatter(0, True)
                    with pool.Fori(1, EC // (2 * SC)) as i:
                        scatter(i)
                    for b in range(2):
                        pool.wait_ge(s_sc[b], 16 * EC // 2)
                    for i in range(2):
                        g = slice(i * CH // 2, (i + 1) * CH // 2)
                        pool.dma_start(slots[:, g, :], slot_dram.rearrange("(g p) w -> p g w", p=P)[:, g, :]).then_inc(s_sl, 16)
                        pool.wait_ge(s_sl, 16 * (i + 1))
                    pool.wait_ge(s_cst, 16)

                    COPIED = 2 * (EC // SC)

                    def gather(i, first=False):
                        for b in range(2):
                            n = i * 2 + b
                            nc.gpsimd.tensor_copy(idx_buf[:, b, :], slots[:, ds(n * SC, SC), 1]).then_inc(s_cp, 1)
                            pool.wait_ge(s_cp, n + (COPIED + 1))
                            pool.sem_inc(s_pass, 1)
                            for c in range(SC):
                                pool.indirect_dma_start(
                                    win_buf[:, b, c:c + 1], None, winv_dram,
                                    bass.IndirectOffsetOnAxis(idx_buf[:, b, c:c + 1], 0),
                                    bounds_check=TR * P - 1).then_inc(s_ga[b], 16)
                            if not (first and b == 0):
                                take(n - 1, 1 - b, i - 1 + b)

                    def take(n, b, i):
                        pool.wait_ge(s_ga[b], i * (16 * SC) + 16 * SC)
                        nc.gpsimd.tensor_copy(winv[:, ds(n * SC, SC)], win_buf[:, b, :])

                    gather(0, True)
                    with pool.Fori(1, CH // (2 * SC)) as i:
                        gather(i)
                    take(CH // SC - 1, 1, CH // (2 * SC) - 1)

                @block.scalar
                def _(act):
                    def xT_high(t):
                        act.wait_ge(s_xT, t + 1)
                        nc.scalar.activation(xT_hi[:, :, t * P:(t + 1) * P],
                                             ps_t[:, :, :].rearrange("p b (k c) -> p (b k) c", c=P), ACT.Copy).then_inc(s_xhi, 1)

                    def split_hi(n, half, first=False, parts=range(4)):
                        if not first:
                            act.wait_ge(s_half, n - 1)
                        for q in parts:
                            act.wait_ge(s_w[q], n * 16 + 16)
                            nc.scalar.activation(w_hi[half][:, 2 * q:2 * q + 2, :], w_stage[:, q, :, :], ACT.Copy).then_inc(s_whi, 1)

                    def copy_tile(u, half, t, first=False):
                        m = half * T + t
                        act.wait_ge(s_y, u * (2 * T) + m + 1)
                        i = m % 4
                        if not (first and t < 4):
                            act.wait_ge(s_yst[i], u * (16 * 2 * T // 4) + 16 * (m // 4))
                        nc.scalar.activation(y_out[:, i, :], ps_y[:, i, :], ACT.Copy).then_inc(s_ysb, 1)

                    def copy_y(u, half):
                        for t in range(T):
                            copy_tile(u, half, t)

                    def first_y(t):
                        copy_tile(0, 0, t, True)
                        act.wait_ge(s_ysb, t + 1)
                        act.dma_start(y_view[0, t, :, 0, :], y_out[:, t % 4, :]).then_inc(s_yst[t % 4], 16)

                    for t in range(T):
                        xT_high(t)
                        if t == 0:
                            split_hi(0, 0, True)
                        if t >= T - 4:
                            split_hi(1, 1, True, (t - T + 4,))
                        if t >= 1:
                            first_y(t - 1)
                    first_y(T - 1)
                    split_hi(2, 0)
                    copy_y(0, 1)
                    split_hi(3, 1)
                    with act.Fori(1, UNITS - 1) as u:
                        for half in range(2):
                            copy_y(u, half)
                            split_hi(u * 2 + half + 2, half)
                    for half in range(2):
                        copy_y(UNITS - 1, half)

                @block.vector
                def _(dve):
                    st = [0]

                    def stat(ins):
                        st[0] += 1
                        ins.then_inc(s_stat, 1)
                        dve.wait_ge(s_stat, st[0])

                    def split_lo(n, half, parts=range(4)):
                        for q in parts:
                            dve.wait_ge(s_whi, n * 4 + q + 1)
                            nc.vector.tensor_tensor(w_lo[half][:, 2 * q:2 * q + 2, :], w_stage[:, q, :, :],
                                                    w_hi[half][:, 2 * q:2 * q + 2, :].bitcast(F32), ALU.subtract).then_inc(s_wlo, 1)

                    def xT_low(t):
                        dve.wait_ge(s_xhi, t + 1)
                        nc.vector.tensor_tensor(xT_lo[:, :, t * P:(t + 1) * P],
                                                ps_t[:, :, :].rearrange("p b (k c) -> p (b k) c", c=P),
                                                xT_hi[:, :, t * P:(t + 1) * P].bitcast(F32), ALU.subtract).then_inc(s_xlo, 1)

                    for t in range(T):
                        b = t % 2
                        dve.wait_ge(s_x[b], 16 * (t // 2 + 1))
                        for h in range(2):
                            i = nc.vector.bn_stats(bst[:, b, h, :], xs[:, b, h * H:(h + 1) * H])
                        stat(i)
                        stat(nc.vector.bn_aggr(mv[:, b, :], bst[:, b, :, :].rearrange("p h s -> p (h s)")))
                        nc.vector.tensor_copy(stats[:, t, 0:1], mv[:, b, 0:1])
                        inverse_root(stat, stats[:, t, 1:2], mv[:, b, 1:2], newton)
                        if t >= 2:
                            dve.wait_ge(s_xT, t - 1)
                        nc.vector.tensor_scalar(xn[:, b, :], xs[:, b, :], stats[:, t, 0:1], stats[:, t, 1:2],
                                                ALU.subtract, ALU.mult).then_inc(s_xn, 1)
                        if t == T - 3:
                            dve.wait_ge(s_xn, t + 1)
                            nc.vector.memset(xs[:, (T - 1) % 2, :], 0.0).then_inc(s_xpad, 1)
                        if t >= 1:
                            xT_low(t - 1)
                        if t == 1:
                            split_lo(0, 0)
                        if t >= T - 3:
                            split_lo(1, 1, (t - T + 3,))
                    split_lo(1, 1, (3,))
                    xT_low(T - 1)

                    ch = [0]

                    def step(ins):
                        ch[0] += 1
                        ins.then_inc(s_dve, 1)
                        dve.wait_ge(s_dve, ch[0])

                    dve.wait_ge(s_edge, 48)
                    dve.wait_ge(s_const, 6)
                    nc.vector.tensor_scalar(tile_i[:, :], edge_i[:, 1, :], 7, None, ALU.arith_shift_right)
                    nc.vector.tensor_scalar(loc_i, edge_i[:, 1, :], P - 1, None, ALU.bitwise_and)
                    nc.vector.tensor_copy(edge_f[:, 0, :], edge_i[:, 0, :])
                    step(nc.vector.tensor_copy(edge_f[:, 2, :], edge_i[:, 2, :]))
                    nc.vector.tensor_copy(edge_f[:, 1, :], loc_i)
                    step(nc.vector.tensor_copy(edge_f[:, 3, :], tile_i[:, :]))
                    step(nc.vector.scalar_tensor_tensor(edge_f[:, 4, :], edge_f[:, 2, :], float(T), edge_f[:, 3, :], ALU.mult, ALU.add))

                    def onehots(j):
                        c, b = slice(j * PC, (j + 1) * PC), j % 2
                        if j >= 2:
                            dve.wait_ge(s_ohu, j - 1)
                        nc.vector.tensor_tensor(oh_key[:, b, :, :], edge_f[:, 4, c].unsqueeze(2).broadcast_to([EP, PC, TR]),
                                                iota_row[0:EP, 0:TR].unsqueeze(1).broadcast_to([EP, PC, TR]), ALU.is_equal, saturate=False).then_inc(s_oh, 1)
                        nc.vector.tensor_tensor(oh_loc[:, b, :, :], edge_f[:, 1, c].unsqueeze(2).broadcast_to([EP, PC, P]),
                                                iota_row[0:EP, :].unsqueeze(1).broadcast_to([EP, PC, P]), ALU.is_equal, saturate=False).then_inc(s_oh, 1)

                    onehots(0)
                    onehots(1)
                    dve.wait_ge(s_xT, T)
                    step(nc.vector.tensor_tensor(ohT[:, :, :], edge_f[:, 3, :].unsqueeze(1).broadcast_to([EP, T, EC]),
                                                 iota_row[0:EP, 0:T].unsqueeze(2).broadcast_to([EP, T, EC]), ALU.is_equal))
                    a, b, d = ohT, cum[0], 1
                    while d < EC:
                        nc.vector.tensor_copy(b[:, :, 0:d], a[:, :, 0:d])
                        step(nc.vector.tensor_tensor(b[:, :, d:EC], a[:, :, d:EC], a[:, :, 0:EC - d], ALU.add))
                        a, b, d = b, (cum[1] if b is cum[0] else cum[0]), 2 * d
                    run, tmp = a, b
                    nc.vector.tensor_copy(pre[0:EP, 0, 0:T], run[:, :, EC - 1]).then_inc(s_row, 1)
                    split_lo(2, 0)
                    for j in range(2, 6):
                        onehots(j)
                    dve.wait_ge(s_pre, 1)
                    step(nc.vector.tensor_scalar(pre_i[:, 0:T], ps_pre[:, 1, 0:T], float(PAIR - 1), None, ALU.add))
                    step(nc.vector.tensor_scalar(pre_i[:, 0:T], pre_i[:, 0:T], PAIR.bit_length() - 1, None, ALU.arith_shift_right))
                    nc.vector.memset(pre[:, 2, 0:1], 0.0)
                    step(nc.vector.tensor_scalar(pre[:, 1, 0:T], pre_i[:, 0:T], 1.0, None, ALU.max))
                    for k in range(T):
                        step(nc.vector.tensor_tensor(pre[:, 2, k + 1:k + 2], pre[:, 2, k:k + 1], pre[:, 1, k:k + 1], ALU.add))
                    nc.vector.tensor_copy(starts[:, 0:T + 1], pre[:, 2, 0:T + 1])
                    step(nc.vector.tensor_scalar(pre_i[:, 0:1], pre[:, 2, T:T + 1], 3.0, None, ALU.add))
                    nc.vector.tensor_scalar(starts[:, T + 1:T + 2], pre_i[:, 0:1], 2, None, ALU.arith_shift_right)
                    step(nc.vector.scalar_tensor_tensor(pre[0:EP, 3, 0:T], pre[0:EP, 2, 0:T], float(PAIR), ps_pre[0:EP, 0, 0:T], ALU.mult, ALU.add))
                    step(nc.vector.tensor_scalar(pre[0:EP, 3, 0:T], pre[0:EP, 3, 0:T], -1.0, None, ALU.add))
                    step(nc.vector.tensor_tensor(tmp[:, :, :], run[:, :, :], pre[0:EP, 3, 0:T].unsqueeze(2).broadcast_to([EP, T, EC]), ALU.add))
                    step(nc.vector.tensor_tensor(tmp[:, :, :], tmp[:, :, :], ohT[:, :, :], ALU.mult))
                    step(nc.vector.tensor_reduce(slot_f, tmp[:, :, :].rearrange("p k c -> p c k"), AX.X, ALU.add))
                    nc.vector.tensor_copy(slot_i[:, :], slot_f)
                    nc.vector.memset(rec[:, :, 3], 0)
                    nc.vector.scalar_tensor_tensor(rec[:, :, 0], edge_f[:, 2, :], float(NP), edge_f[:, 0, :], ALU.mult, ALU.add)
                    nc.vector.scalar_tensor_tensor(rec[:, :, 1], edge_f[:, 4, :], float(P), edge_f[:, 1, :], ALU.mult, ALU.add)
                    step(nc.vector.tensor_copy(rec[:, :, 2], edge_f[:, 1, :]))
                    for j in range(6, NPIECE):
                        onehots(j)
                        if j == NPIECE // 2:
                            split_lo(3, 1)
                        if j == NPIECE - 3:
                            split_lo(4, 0)
                    dve.wait_ge(s_ohu, NPIECE)
                    step(nc.vector.tensor_scalar(cnt[:, 0, :], ps_cnt[0:TR, 0:P], 1.0, None, ALU.max))
                    nc.vector.reciprocal(cnt[:, 1, :], cnt[:, 0, :]).then_inc(s_cinv, 1)
                    dve.wait_ge(s_cinv, 1)
                    nc.vector.memset(cnt[:, 0, 0:1], 0.0).then_inc(s_rec, 1)
                    split_lo(5, 1)
                    with dve.Fori(3, UNITS) as u:
                        for half in range(2):
                            split_lo(u * 2 + half, half)

                @block.tensor
                def _(pe):
                    pe.wait_ge(s_const, 6)

                    def turn_x(t):
                        pe.wait_ge(s_xn, t + 1)
                        if t >= 1:
                            pe.wait_ge(s_xlo, t)
                        for k in range(KT):
                            i = nc.tensor.transpose(ps_t[:, k // 4, (k % 4) * P:(k % 4 + 1) * P],
                                                    xn[:, t % 2, k * P:(k + 1) * P], ident[:, :])
                        i.then_inc(s_xT, 1)

                    def product(n, half, t, first=False):
                        if not (first and t < 4):
                            pe.wait_ge(s_ysb, n * T + t - 3)
                        for k in range(KT):
                            hi, lo = xT_hi[:, k, t * P:(t + 1) * P], xT_lo[:, k, t * P:(t + 1) * P]
                            nc.tensor.matmul(ps_y[:, (half * T + t) % 4, :], lo, w_hi[half][:, k, :], start=(k == 0), stop=False)
                            nc.tensor.matmul(ps_y[:, (half * T + t) % 4, :], hi, w_lo[half][:, k, :], start=False, stop=False)
                            i = nc.tensor.matmul(ps_y[:, (half * T + t) % 4, :], hi, w_hi[half][:, k, :], start=False, stop=(k == KT - 1))
                        i.then_inc(s_y, 1)

                    def multiply(n, half, between=None):
                        pe.wait_ge(s_wlo, n * 4 + 4)
                        for t in range(T):
                            product(n, half, t)
                            if between:
                                between(t)
                        pe.wait_ge(s_y, n * T + T)
                        pe.sem_inc(s_half, 1)

                    def count(j):
                        pe.wait_ge(s_oh, 2 * j + 2)
                        for c in range(PC):
                            i = nc.tensor.matmul(ps_cnt[0:TR, 0:P], oh_key[:, j % 2, c, :], oh_loc[:, j % 2, c, :],
                                                 start=(j == 0 and c == 0), stop=(j == NPIECE - 1 and c == PC - 1))
                        i.then_inc(s_ohu, 1)

                    def prefixes():
                        pe.wait_ge(s_row, 1)
                        nc.tensor.matmul(ps_pre[0:EP, 0, 0:T], lower[0:EP, 0:EP], pre[0:EP, 0, 0:T], start=True, stop=True)
                        nc.tensor.matmul(ps_pre[:, 1, 0:T], ones[0:EP, :], pre[0:EP, 0, 0:T], start=True, stop=True).then_inc(s_pre, 1)

                    turn_x(0)
                    for t in range(1, T):
                        turn_x(t)
                        if t == 1:
                            pe.wait_ge(s_wlo, 4)
                        product(0, 0, t - 1, True)
                    pe.wait_ge(s_xlo, T)
                    product(0, 0, T - 1, True)
                    pe.wait_ge(s_y, T)
                    pe.sem_inc(s_half, 1)
                    def first_counts(t):
                        if t in (2, 3):
                            count(t - 2)
                        if t == T - 3:
                            prefixes()
                        if t >= T - 2:
                            count(t - T + 4)

                    multiply(1, 1, first_counts)
                    multiply(2, 0, lambda t: count(t + 3) if t >= 1 else None)
                    multiply(3, 1, lambda t: count(T + 3 + t) if T + 3 + t < NPIECE else None)
                    with pe.Fori(2, UNITS) as u:
                        for half in range(2):
                            multiply(u * 2 + half, half)

        with ExitStack() as ph:
            G8 = 8
            LAG = 3
            msg = sb(ph, "msg", [P, G8, D], F32)
            S = 512
            part_hi = sb(ph, "part_hi", [P, 4, S], F32R)
            part_lo = sb(ph, "part_lo", [P, 4, S], F32R)
            sel = [sb(ph, f"sel{i}", [P, P], F32R) for i in range(2)]
            row_idx = sb(ph, "row_idx", [P, 2, 4], I32)
            slot_loc = sb(ph, "slot_loc", [P, CH], F32)
            y_root = sb(ph, "y_root", [P, D], F32)
            y_gate = sb(ph, "y_gate", [P, D], F32)
            xr = sb(ph, "xr", [P, 2, D], F32)
            xnr = sb(ph, "xnr", [P, D], F32)
            u_sb = sb(ph, "u_sb", [P, 2, D], F32)
            tanh_u = sb(ph, "tanh_u", [P, D], F32)
            z_sb = sb(ph, "z_sb", [P, D], F32)
            uT_hi = sb(ph, "uT_hi", [P, KT, P], F32R)
            uT_lo = sb(ph, "uT_lo", [P, KT, P], F32R)
            x1 = sb(ph, "x1", [P, D], F32)
            xn2 = sb(ph, "xn2", [P, D], F32)
            xn2T = sb(ph, "xn2T", [P, KT, P], F32)
            wg_hi = sb(ph, "wg_hi", [P, KT, D], F32R)
            wg_lo = sb(ph, "wg_lo", [P, KT, D], F32R)
            wg_stage = sb(ph, "wg_stage", [P, 2, D], F32)
            rw = sb(ph, "rw", [P, KT, NX1], F32)
            rows = sb(ph, "rows", [3, D], F32)
            pick = sb(ph, "pick", [3, 3, P], F32)
            zero_row = sb(ph, "zero_row", [1, H], BF16)
            affine = sb(ph, "affine", [P, 2, T], F32)
            bst2 = sb(ph, "bst2", [P, 2, 6], F32)
            mv2 = sb(ph, "mv2", [P, 2], F32)
            ps_u = ps(ph, "ps_u", [P, 2, H])
            ps_z = ps(ph, "ps_z", [P, 2, H])
            ps_tr = ps(ph, "ps_tr", [P, 2, H])
            ps_log = ps(ph, "ps_log", [P, 4, P])

            q_par = [sem(f"params_loaded{i}") for i in range(2)]
            q_wg = [sem(f"wg_loaded{i}") for i in range(2)]
            q_wghi, q_wglo = sem("wg_hi_made"), sem("wg_lo_made")
            q_cst = sem("phase2_constants")
            q_yr, q_yg, q_xr = sem("y_root_loaded"), sem("y_gate_loaded"), [sem(f"x_again_loaded{i}") for i in range(2)]
            q_idx = sem("row_idx_copied")
            q_ga = [sem(f"message_gathered{i}") for i in range(G8)]
            q_land = sem("messages_there")
            q_mhi, q_msc = sem("message_hi_made"), sem("message_scaled")
            q_sel = sem("message_lo_and_selection_made")
            q_agg = sem("message_summed")
            q_psu, q_u, q_ut = sem("u_summed"), sem("u_made"), sem("u_transposed")
            q_uhi, q_ulo = sem("uT_hi_made"), sem("uT_lo_made")
            q_z, q_zc, q_act = sem("z_multiplied"), sem("z_copied"), sem("gate_terms_made")
            q_xn = sem("x_norm_again")
            q_dve = sem("gate_chain")
            q_st = sem("stat2_chain")
            q_x1, q_xn2 = sem("x1_made"), sem("xn2_made")
            q_x1s, q_xn2s = sem("x1_stored"), sem("xn2_stored")
            q_n2t, q_n2c, q_log, q_logc = sem("xn2_transposed"), sem("xn2T_copied"), sem("logits_made"), sem("logits_copied")

            with nc.Block() as block:
                def bounds(eng, t):
                    a = eng.value_load(starts[0:1, ds(t, 1)], min_val=0, max_val=PAIRS - 1)
                    b = eng.value_load(starts[0:1, ds(t + 1, 1)], min_val=0, max_val=PAIRS)
                    return a, b

                def since(t, k):
                    return not isinstance(t, int) or t >= k

                def stages(eng, stage, begun=0, peel_last=False):
                    for t in range(begun, 4):
                        stage(t // 2, t % 2)
                    with eng.Fori(2, T // 2 - (1 if peel_last else 0)) as j:
                        for b in range(2):
                            stage(j, b)
                    if peel_last:
                        for b in range(2):
                            stage(T // 2 - 1, b)

                @block.sync
                def _(sp):
                    sp.wait_ge(q_cst, 4)
                    sp.dma_start(rows[0:1, :], bias).then_inc(q_par[0], 16)
                    sp.dma_start(rows[1:2, :], b_gate).then_inc(q_par[0], 16)
                    sp.dma_start(rows[2:3, 0:NX1], router_b).then_inc(q_par[0], 16)
                    sp.dma_start(rw[:, :, :], router_w.rearrange("(k p) e -> p k e", p=P)).then_inc(q_par[1], 16)
                    yr = y_dram[ROOT * NP:(ROOT + 1) * NP, :].rearrange("(t p) n -> t p n", p=P)
                    yg = y_dram[GATE_X * NP:(GATE_X + 1) * NP, :].rearrange("(t p) n -> t p n", p=P)
                    x_t = x[0:(T - 1) * P, :].rearrange("(t p) n -> t p n", p=P)
                    x1_t = x1_dram.rearrange("(t p) n -> t p n", p=P)
                    xn2_t = xn2_dram.rearrange("(t p) n -> t p n", p=P)
                    wg_t = w_gate_u.rearrange("(k p) n -> p k n", p=P)

                    def load_gate(t):
                        sp.dma_start(y_gate[:, :], yg[ds(t, 1), :, :].rearrange("t p n -> (t p) n")).then_inc(q_yg, 16)

                    def store(t):
                        sp.dma_start(x1_t[ds(t, 1), :, :].rearrange("t p n -> (t p) n"), x1[:, :]).then_inc(q_x1s, 16)
                        sp.wait_ge(q_xn2, t + 1)
                        sp.dma_start(xn2_t[ds(t, 1), :, :].rearrange("t p n -> (t p) n"), xn2[:, :]).then_inc(q_xn2s, 16)

                    def stage(j, b):
                        t = j * 2 + b
                        if since(t, 1):
                            sp.wait_ge(q_u, t)
                        sp.dma_start(y_root[:, :], yr[ds(t, 1), :, :].rearrange("t p n -> (t p) n")).then_inc(q_yr, 16)
                        if since(t, 2):
                            sp.wait_ge(q_x1, t - 1)
                        if since(t, 1):
                            load_gate(t - 1)
                        if isinstance(t, int) and t == T - 1:
                            sp.dma_start(xr[0:LAST, b, :], x[t * P:N, :]).then_inc(q_xr[b], 16)
                        else:
                            sp.dma_start(xr[:, b, :], x_t[ds(t, 1), :, :].rearrange("t p n -> (t p) n")).then_inc(q_xr[b], 16)
                        if since(t, 2):
                            store(t - 2)

                    for k in range(KT):
                        if k >= 2:
                            sp.wait_ge(q_wglo, k - 1)
                        sp.dma_start(wg_stage[:, k % 2, :], wg_t[:, k, :]).then_inc(q_wg[k % 2], 16)
                        if k == 1:
                            stage(0, 0)
                    stages(sp, stage, begun=1, peel_last=True)
                    for t in (T - 2, T - 1):
                        sp.wait_ge(q_x1, t + 1)
                        if t == T - 2:
                            load_gate(T - 1)
                        store(t)
                    sp.wait_ge(q_x1s, 16 * T)
                    sp.wait_ge(q_xn2s, 16 * T)

                @block.gpsimd
                def _(pool):
                    eights = pool.value_load(starts[0:1, T + 1:T + 2], min_val=2, max_val=-(-CH // G8))

                    def eight(q, first=False):
                        for j in range(G8):
                            h = j // 4
                            if j % 4 == 0:
                                nc.gpsimd.tensor_copy(row_idx[:, h, :], slots[:, ds(q * G8 + j, 4), 0]).then_inc(q_idx, 1)
                                pool.wait_ge(q_idx, q * 2 + h + 1)
                            pool.wait_ge(q_agg, q * G8 + j + 1)
                            pool.sem_inc(q_pass, 1)
                            pool.indirect_dma_start(msg[:, j, :], None, y_dram,
                                                    bass.IndirectOffsetOnAxis(row_idx[:, h, j % 4:j % 4 + 1], 0),
                                                    bounds_check=UNITS * NP - 1).then_inc(q_ga[j], 16)
                            if not (first and j < LAG):
                                pool.wait_ge(q_ga[(j - LAG) % G8], q * 16 + (16 if j >= LAG else 0))
                                pool.sem_inc(q_land, 1)

                    eight(0, True)
                    with pool.Fori(1, eights) as q:
                        eight(q)
                    for j in range(G8 - LAG, G8):
                        pool.wait_ge(q_ga[j], eights * 16)
                        pool.sem_inc(q_land, 1)

                @block.scalar
                def _(act):
                    def scale(i):
                        for j in range(2):
                            g = i * 2 + j
                            m, c = msg[:, ds((i % 4) * 2 + j, 1), :].rearrange("p a n -> p (a n)"), winv[:, ds(g, 1)]
                            act.wait_ge(q_land, g + 1)
                            act.wait_ge(q_agg, g + G8 - 3)
                            nc.scalar.activation(part_hi[:, ds((i % 2) * 2 + j, 1), :].rearrange("p a n -> p (a n)"), m[:, 0:S],
                                                 ACT.Copy, scale=c).then_inc(q_mhi, 1)
                            nc.scalar.activation(m[:, S:D], m[:, S:D], ACT.Copy, scale=c).then_inc(q_msc, 1)

                    def terms(j, b):
                        t = j * 2 + b
                        if since(t, 1):
                            act.wait_ge(q_dve, t * 3)
                        nc.scalar.activation(tanh_u[:, :], u_sb[:, b, :], ACT.Tanh).then_inc(q_act, 1)
                        act.wait_ge(q_xr[b], j * 16 + 16)
                        nc.scalar.activation(xnr[:, :], xr[:, b, :], ACT.Identity, scale=stats[:, ds(t, 1), 1], bias=affine[:, 1, ds(t, 1)]).then_inc(q_xn, 1)
                        act.wait_ge(q_xn, t + 1)
                        nc.scalar.activation(xr[:, b, :], xr[:, b, :], ACT.Identity, scale=affine[:, 0, ds(t, 1)], bias=affine[:, 1, ds(t, 1)]).then_inc(q_act, 1)

                    def copy_n2(t):
                        act.wait_ge(q_n2t, t + 1)
                        nc.scalar.activation(xn2T[:, :, :].rearrange("p k c -> p (k c)"), ps_tr[:, :, :].rearrange("p a n -> p (a n)"), ACT.Copy).then_inc(q_n2c, 1)

                    def copy_z(t):
                        act.wait_ge(q_z, t + 1)
                        nc.scalar.activation(z_sb[:, :], ps_z[:, :, :].rearrange("p a n -> p (a n)"), ACT.Copy).then_inc(q_zc, 1)

                    def high_u(t):
                        act.wait_ge(q_ut, t + 1)
                        nc.scalar.activation(uT_hi[:, :, :].rearrange("p k c -> p (k c)"), ps_tr[:, :, :].rearrange("p a n -> p (a n)"), ACT.Copy).then_inc(q_uhi, 1)

                    def wg_high(k):
                        act.wait_ge(q_wg[k % 2], 16 * (k // 2 + 1))
                        if k >= 2:
                            act.wait_ge(q_wglo, k - 1)
                        nc.scalar.activation(wg_hi[:, k, :], wg_stage[:, k % 2, :], ACT.Copy).then_inc(q_wghi, 1)

                    def stage(j, b):
                        t = j * 2 + b
                        first, last = bounds(act, t)
                        if not since(t, 2):
                            wg_high(4 * t)
                            wg_high(4 * t + 1)
                        with act.If(first + 1 < last):
                            with act.Fori(first + 1, last) as i:
                                scale(i)
                        if not since(t, 2):
                            wg_high(4 * t + 2)
                            wg_high(4 * t + 3)
                        if since(t, 3):
                            copy_n2(t - 3)
                        if since(t, 1):
                            terms(j if b else j - 1, 1 - b)
                        if not (isinstance(t, int) and t == T - 1):
                            scale(bounds(act, t + 1)[0])
                        if since(t, 1):
                            copy_z(t - 1)
                        high_u(t)

                    act.wait_ge(q_cst, 5)
                    scale(bounds(act, 0)[0])
                    stages(act, stage, peel_last=True)
                    terms(T // 2 - 1, 1)
                    copy_n2(T - 3)
                    copy_z(T - 1)
                    copy_n2(T - 2)
                    copy_n2(T - 1)

                @block.vector
                def _(dve):
                    nc.vector.memset(zero_row[:, :], 0.0)
                    nc.vector.memset(rows[:, :], 0.0).then_inc(q_cst, 1)
                    nc.vector.tensor_copy(slot_loc[:, :], slots[:, :, 2]).then_inc(q_cst, 1)
                    nc.vector.tensor_scalar(affine[:, 0, :], stats[:, :, 1], 1.0, None, ALU.add).then_inc(q_cst, 1)
                    nc.vector.scalar_tensor_tensor(affine[:, 1, :], stats[:, :, 0], -1.0, stats[:, :, 1], ALU.mult, ALU.mult).then_inc(q_cst, 1)
                    nc.vector.tensor_copy(pick[:, :, :], ident[0:3, 0:3].unsqueeze(2).broadcast_to([3, 3, P])).then_inc(q_cst, 1)
                    def wg_low(k):
                        dve.wait_ge(q_wghi, k + 1)
                        nc.vector.tensor_tensor(wg_lo[:, k, :], wg_stage[:, k % 2, :], wg_hi[:, k, :].bitcast(F32), ALU.subtract).then_inc(q_wglo, 1)

                    def select(i):
                        for j in range(2):
                            g = i * 2 + j
                            place = ds((i % 2) * 2 + j, 1)
                            dve.wait_ge(q_mhi, g + 1)
                            nc.vector.scalar_tensor_tensor(part_lo[:, place, :].rearrange("p a n -> p (a n)"),
                                                           msg[:, ds((i % 4) * 2 + j, 1), 0:S].rearrange("p a n -> p (a n)"), winv[:, ds(g, 1)],
                                                           part_hi[:, place, :].rearrange("p a n -> p (a n)").bitcast(F32), ALU.mult, ALU.subtract)
                            dve.wait_ge(q_agg, g + G8 - 1)
                            nc.vector.tensor_scalar(sel[j][:, :], iota_row[:, :], slot_loc[:, ds(g, 1)], None,
                                                    ALU.is_equal).then_inc(q_sel, 1)

                    def messages(t, between):
                        first, last = bounds(dve, t)
                        select(first)
                        between()
                        with dve.If(first + 1 < last):
                            with dve.Fori(first + 1, last) as i:
                                select(i)

                    def take_u(t, b):
                        dve.wait_ge(q_psu, t + 1)
                        dve.wait_ge(q_yr, t * 16 + 16)
                        nc.vector.tensor_tensor(u_sb[:, b, :], ps_u[:, :, :].rearrange("p a n -> p (a n)"), y_root[:, :], ALU.add).then_inc(q_u, 1)

                    def low_u(t):
                        dve.wait_ge(q_uhi, t + 1)
                        nc.vector.tensor_tensor(uT_lo[:, :, :].rearrange("p k c -> p (k c)"), ps_tr[:, :, :].rearrange("p a n -> p (a n)"),
                                                uT_hi[:, :, :].rearrange("p k c -> p (k c)").bitcast(F32), ALU.subtract).then_inc(q_ulo, 1)

                    NS = 12
                    def update(j, b):
                        t = j * 2 + b
                        n3, n12 = t * 3, t * (NS + 2)
                        dve.wait_ge(q_zc, t + 1)
                        dve.wait_ge(q_yg, t * 16 + 16)
                        dve.wait_ge(q_act, t * 2 + 2)
                        nc.vector.tensor_tensor(y_gate[:, :], z_sb[:, :], y_gate[:, :], ALU.add).then_inc(q_dve, 1)
                        nc.vector.tensor_tensor(xnr[:, :], tanh_u[:, :], xnr[:, :], ALU.subtract).then_inc(q_dve, 1)
                        dve.wait_ge(q_dve, n3 + 2)
                        nc.vector.tensor_tensor(y_gate[:, :], y_gate[:, :], xnr[:, :], ALU.mult).then_inc(q_dve, 1)
                        dve.wait_ge(q_dve, n3 + 3)
                        if since(t, 1):
                            dve.wait_ge(q_x1s, t * 16)
                        nc.vector.tensor_tensor(x1[:, :], y_gate[:, :], xr[:, b, :], ALU.add).then_inc(q_x1, 1)
                        dve.wait_ge(q_x1, t + 1)
                        for h in range(2):
                            i = nc.vector.bn_stats(bst2[:, h, :], x1[:, h * H:(h + 1) * H])
                        k = [0]

                        def step(ins):
                            k[0] += 1
                            ins.then_inc(q_st, 1)
                            dve.wait_ge(q_st, n12 + k[0])

                        step(i)
                        dve.sem_inc(q_pass2, 1)
                        step(nc.vector.bn_aggr(mv2[:, :], bst2[:, :, :].rearrange("p h s -> p (h s)")))
                        nc.vector.tensor_copy(stats2[:, ds(t, 1), 0], mv2[:, 0:1])
                        inverse_root(step, stats2[:, ds(t, 1), 1], mv2[:, 1:2], newton)
                        assert k[0] == NS + 2
                        if since(t, 1):
                            dve.wait_ge(q_xn2s, t * 16)
                            dve.wait_ge(q_n2t, t)
                        nc.vector.tensor_scalar(xn2[:, :], x1[:, :], mv2[:, 0:1], stats2[:, ds(t, 1), 1], ALU.subtract, ALU.mult).then_inc(q_xn2, 1)

                    def stage(j, b):
                        t = j * 2 + b

                        def between():
                            if since(t, 1):
                                low_u(t - 1)
                            if not since(t, 2):
                                wg_low(4 * t)
                                wg_low(4 * t + 1)

                        messages(t, between)
                        take_u(t, b)
                        if not since(t, 2):
                            wg_low(4 * t + 2)
                            wg_low(4 * t + 3)
                        if since(t, 2):
                            update(j - 1, b)

                    stages(dve, stage)
                    low_u(T - 1)
                    for b in range(2):
                        update(T // 2 - 1, b)
                    dve.wait_ge(q_log, T)
                    nc.vector.tensor_copy(logits[:, :, :], ps_log[:, 0, 0:T * NX1].rearrange("p (t e) -> p t e", e=NX1)).then_inc(q_logc, 1)

                @block.tensor
                def _(pe):
                    pe.sem_inc(q_agg, G8)
                    pe.wait_ge(q_par[0], 48)
                    pe.wait_ge(q_par[1], 16)
                    pe.wait_ge(q_cst, 5)

                    def messages(t, b, opener=False):
                        if not (isinstance(t, int) and t == 0):
                            pe.wait_ge(q_u, t)
                        for h in range(2):
                            nc.tensor.matmul(ps_u[:, h, :], pick[:, 0, :], rows[:, h * H:(h + 1) * H], start=True, stop=False)
                        first, last = bounds(pe, t)
                        with pe.Fori(first, last) as i:
                            for j in range(2):
                                g = i * 2 + j
                                pe.wait_ge(q_sel, g + 1)
                                for part in (part_hi, part_lo):
                                    for h in range(-(-S // H)):
                                        c = slice(h * H, min(S, h * H + H))
                                        nc.tensor.matmul(ps_u[:, h, 0:c.stop - c.start], sel[j][:, :],
                                                         part[:, ds((i % 2) * 2 + j, 1), c].rearrange("p a n -> p (a n)"),
                                                         start=False, stop=False)
                                pe.wait_ge(q_msc, g + 1)
                                nc.tensor.matmul(ps_u[:, 1, S - H:H], sel[j][:, :].bitcast(F32),
                                                 msg[:, ds((i % 4) * 2 + j, 1), S:D].rearrange("p a n -> p (a n)"),
                                                 start=False, stop=False).then_inc(q_agg, 1)
                        for h in range(2):
                            m = nc.tensor.matmul(ps_u[:, h, :], zero_row[0:1, 0:P], zero_row[0:1, :], start=False, stop=True)
                        m.then_inc(q_psu, 1)

                    def turn_u(t, b):
                        pe.wait_ge(q_u, t + 1)
                        if since(t, 1):
                            pe.wait_ge(q_ulo, t)
                        for k in range(KT):
                            m = nc.tensor.transpose(ps_tr[:, k // 4, (k % 4) * P:(k % 4 + 1) * P], u_sb[:, b, k * P:(k + 1) * P], ident[:, :])
                        m.then_inc(q_ut, 1)

                    def gate(t):
                        pe.wait_ge(q_ulo, t + 1)
                        if since(t, 1):
                            pe.wait_ge(q_zc, t)
                        else:
                            pe.wait_ge(q_wglo, KT)
                        for h in range(2):
                            w = slice(h * H, (h + 1) * H)
                            nc.tensor.matmul(ps_z[:, h, :], pick[:, 1, :], rows[:, w], start=True, stop=False)
                            for k in range(KT):
                                nc.tensor.matmul(ps_z[:, h, :], uT_lo[:, k, :], wg_hi[:, k, w], start=False, stop=False)
                                nc.tensor.matmul(ps_z[:, h, :], uT_hi[:, k, :], wg_lo[:, k, w], start=False, stop=False)
                                m = nc.tensor.matmul(ps_z[:, h, :], uT_hi[:, k, :], wg_hi[:, k, w], start=False, stop=(k == KT - 1))
                        m.then_inc(q_z, 1)

                    def turn_n2(t):
                        pe.wait_ge(q_xn2, t + 1)
                        pe.wait_ge(q_ulo, min(t + 3, T) if isinstance(t, int) else t + 3)
                        for k in range(KT):
                            m = nc.tensor.transpose(ps_tr[:, k // 4, (k % 4) * P:(k % 4 + 1) * P], xn2[:, k * P:(k + 1) * P], ident[:, :])
                        m.then_inc(q_n2t, 1)

                    def router(t):
                        pe.wait_ge(q_n2c, t + 1)
                        o = ps_log[:, 0, ds(t * NX1, NX1)]
                        nc.tensor.matmul(o, pick[:, 2, :], rows[:, 0:NX1], start=True, stop=False)
                        for k in range(KT):
                            m = nc.tensor.matmul(o, xn2T[:, k, :], rw[:, k, :], start=False, stop=(k == KT - 1))
                        m.then_inc(q_log, 1)

                    def stage(j, b):
                        t = j * 2 + b
                        messages(t, b)
                        if since(t, 3):
                            turn_n2(t - 3)
                        if since(t, 1):
                            gate(t - 1)
                        if since(t, 3):
                            router(t - 3)
                        turn_u(t, b)

                    stages(pe, stage)
                    turn_n2(T - 3)
                    gate(T - 1)
                    router(T - 3)
                    turn_n2(T - 2)
                    router(T - 2)
                    turn_n2(T - 1)
                    router(T - 1)

        with ExitStack() as ph:
            FK = F // P
            tok_id = sb(ph, "tok_id", [P, T], I32)
            real = sb(ph, "real", [P, T], F32)
            tri = sb(ph, "tri", [P, NX1, NX1], F32)
            prob = sb(ph, "prob", [P, T, NX1], F32)
            cmp_ = sb(ph, "cmp", [P, 2, T * NX1 * NX1], F32)
            rank = sb(ph, "rank", [P, T, NX1], F32)
            pickAB = sb(ph, "pick_ab", [P, 2, T, NX1], F32)
            tmp9 = sb(ph, "tmp9", [P, T, NX1], F32)
            red = sb(ph, "red", [P, 12, T], F32)
            cume = [sb(ph, f"cume{i}", [P, NX, T], F32) for i in range(2)]
            pre3 = sb(ph, "pre3", [P, 4, 16], F32)
            pre3_i = sb(ph, "pre3_i", [P, 16], I32)
            chunk0 = sb(ph, "chunk0", [P, NX + 1], I32)
            idx_sc = sb(ph, "idx_sc", [P, 2, T], I32)
            idx_ga = sb(ph, "idx_ga", [P, 2, T], I32)
            gates = sb(ph, "gates", [P, 3, T], F32)
            mix = sb(ph, "mix", [P, 2, T], F32)
            tok = sb(ph, "tok", [P, NCH + 1], I32)
            tok_col = sb(ph, "tok_col", [P, 2], I32)
            e_stage = sb(ph, "e_stage", [P, 4, D], F32)
            w1_hi = [sb(ph, f"w1_hi{i}", [P, KT, F], F32R) for i in range(2)]
            w1_lo = [sb(ph, f"w1_lo{i}", [P, KT, F], F32R) for i in range(2)]
            w2_hi = [sb(ph, f"w2_hi{i}", [P, FK, D], F32R) for i in range(2)]
            w2_lo = [sb(ph, f"w2_lo{i}", [P, FK, D], F32R) for i in range(2)]
            xg = sb(ph, "xg", [P, D], F32)
            xgT_hi = sb(ph, "xgT_hi", [P, D], F32R)
            xgT_lo = sb(ph, "xgT_lo", [P, D], F32R)
            h_sb = sb(ph, "h_sb", [P, F], F32)
            hT_hi = sb(ph, "hT_hi", [P, F], F32R)
            hT_lo = sb(ph, "hT_lo", [P, F], F32R)
            y_sb = sb(ph, "y_sb", [P, D], F32)
            ps_x = ps(ph, "ps_x", [P, D])
            ps_h = ps(ph, "ps_h", [P, F])
            ps_hT = ps(ph, "ps_hT", [P, F])
            ps_y2 = ps(ph, "ps_y2", [P, D])
            ps_rt = ps(ph, "ps_rt", [P, 2, H // 2])

            z_cst, z_tab = sem("phase3_constants"), sem("token_table_cleared")
            z_dve, z_exp = sem("routing_chain"), sem("exp_made")
            z_row, z_pre, z_idx = sem("expert_row_totals"), sem("expert_prefixes"), sem("slots_of_choices")
            z_sc, z_tok, z_col = sem("tokens_scattered"), sem("tokens_loaded"), sem("token_column_copied")
            z_w = [sem(f"expert_stage{i}") for i in range(4)]
            z_whi, z_wlo = sem("expert_hi_made"), sem("expert_lo_made")
            z_pe = sem("pe_wait_passed")
            z_xg, z_xt, z_xhi, z_xlo = sem("tokens_gathered"), sem("tokens_turned"), sem("tokens_hi_made"), sem("tokens_lo_made")
            z_h, z_gelu, z_ht = sem("hidden_multiplied"), sem("gelu_made"), sem("hidden_turned")
            z_hhi, z_hlo = sem("hidden_hi_made"), sem("hidden_lo_made")
            z_y, z_yc, z_ys = sem("expert_out_multiplied"), sem("expert_out_copied"), sem("expert_out_stored")

            with nc.Block() as block:
                def all_experts(eng, others):
                    others(0, 0)
                    with eng.Fori(0, NX // 2 - 1) as j:
                        for b in range(2):
                            others(j * 2 + b + 1, 1 - b, lead=True)

                def bounds(eng, e):
                    first = 0 if isinstance(e, int) and e == 0 else eng.value_load(chunk0[0:1, ds(e, 1)], min_val=1, max_val=NCH - 1)
                    last = eng.value_load(chunk0[0:1, ds(e + 1, 1)], min_val=1, max_val=NCH)
                    return first, last

                @block.gpsimd
                def _(pool):
                    nc.gpsimd.iota(tok_id[:, :], [[P, T]], base=0, channel_multiplier=1).then_inc(z_cst, 1)
                    nc.gpsimd.memset(real[:, :], 1.0).then_inc(z_cst, 1)
                    nc.gpsimd.memset(tri[:, :, :], 1.0).then_inc(z_cst, 1)
                    nc.gpsimd.memset(tok[:, :], 0).then_inc(z_cst, 1)
                    pool.wait_ge(z_cst, 4)
                    pool.dma_start(tok_dram.rearrange("(p g) o -> p (g o)", p=P), tok[:, :]).then_inc(z_tab, 16)
                    nc.gpsimd.affine_select(out=real[:, :], in_=real[:, :], compare_op=ALU.is_ge, fill=0.0, base=N - 1,
                                            pattern=[[-P, T]], channel_multiplier=-1).then_inc(z_cst, 1)
                    nc.gpsimd.affine_select(out=tri[:, :, :], in_=tri[:, :, :], compare_op=ALU.is_gt, fill=0.0, base=0,
                                            pattern=[[1, NX1], [-1, NX1]], channel_multiplier=0).then_inc(z_cst, 1)
                    pool.wait_ge(z_tab, 16)
                    pool.wait_ge(z_idx, 1)
                    for c in range(2):
                        for t in range(T):
                            pool.indirect_dma_start(tok_dram, bass.IndirectOffsetOnAxis(idx_sc[:, c, t:t + 1], 0),
                                                    tok_id[:, t:t + 1], None, bounds_check=NCH * P - 1,
                                                    oob_is_err=False).then_inc(z_sc, 16)
                    pool.wait_ge(z_sc, 16 * 2 * T)
                    pool.dma_start(tok[:, :], tok_dram.rearrange("(g p) o -> p (g o)", p=P), allow_slow_non_contiguous=True).then_inc(z_tok, 16)
                    pool.wait_ge(z_tok, 16)
                    total = pool.value_load(chunk0[0:1, NX:NX + 1], min_val=NX, max_val=NCH)

                    def gather(g):
                        nc.gpsimd.tensor_copy(tok_col[:, 0:1], tok[:, ds(g, 1)]).then_inc(z_col, 1)
                        pool.wait_ge(z_col, g + 1)
                        pool.sem_inc(z_pass, 1)
                        pool.indirect_dma_start(xg[:, :], None, xn2_dram, bass.IndirectOffsetOnAxis(tok_col[:, 0:1], 0),
                                                bounds_check=NP - 1).then_inc(z_xg, 16)

                    gather(0)
                    with pool.Fori(1, total + 1) as g:
                        pool.wait_ge(z_xg, g * 16)
                        pool.wait_ge(z_xt, g)
                        gather(g)
                    pool.wait_ge(z_xg, total * 16 + 16)

                @block.sync
                def _(sp):
                    w1_t = w1.rearrange("e (q k p) f -> e q p k f", p=P, k=2)
                    w2_t = w2.rearrange("e (k p) n -> e k p n", p=P)

                    def weights(e, first=False):
                        for q in range(8):
                            if not (first and q < 4):
                                sp.wait_ge(z_wlo, e * 8 + (q - 3))
                            part = w1_t[ds(e, 1), q, :, :, :].rearrange("e p k f -> (e p) k f") if q < 4 else \
                                w2_t[ds(e, 1), q - 4, :, :].rearrange("e p n -> (e p) n")
                            to = e_stage[:, q % 4, :].rearrange("p (k f) -> p k f", k=2) if q < 4 else e_stage[:, q % 4, :]
                            sp.dma_start(to, part).then_inc(z_w[q % 4], 16)

                    weights(0, True)
                    with sp.Fori(1, NX) as e:
                        weights(e)

                @block.scalar
                def _(act):
                    act.sem_inc(z_ys, 16)
                    act.sem_inc(z_yc, 2)
                    act.wait_ge(z_dve, 1)
                    nc.scalar.activation(prob[:, :, :], prob[:, :, :], ACT.Exp).then_inc(z_exp, 1)

                    def split_hi(e, b, q):
                        act.wait_ge(z_w[q % 4], e * 32 + (q // 4) * 16 + 16)
                        to = w1_hi[b][:, 2 * q:2 * q + 2, :].rearrange("p k f -> p (k f)") if q < 4 else w2_hi[b][:, q - 4, :]
                        nc.scalar.activation(to, e_stage[:, q % 4, :], ACT.Copy).then_inc(z_whi, 1)

                    def turn_hi(n):
                        act.wait_ge(z_xt, n)
                        nc.scalar.activation(xgT_hi[:, :], ps_x[:, :], ACT.Copy).then_inc(z_xhi, 1)

                    def hidden_hi(g):
                        act.wait_ge(z_ht, g + 1)
                        nc.scalar.activation(hT_hi[:, :], ps_hT[:, :], ACT.Copy).then_inc(z_hhi, 1)

                    def gelu(g):
                        act.wait_ge(z_h, g + 1)
                        nc.scalar.activation(h_sb[:, :], ps_h[:, :], ACT.Gelu).then_inc(z_gelu, 1)

                    def take_y(g):
                        act.wait_ge(z_y, g + 1)
                        act.wait_ge(z_ys, g * 16 + 16)
                        nc.scalar.activation(y_sb[:, 0:H], ps_y2[:, 0:H], ACT.Copy).then_inc(z_yc, 1)
                        act.wait_ge(z_yc, g * 2 + 4)
                        act.dma_start(ye_dram.rearrange("(g p) n -> g p n", p=P)[ds(g, 1), :, :].rearrange("g p n -> (g p) n"),
                                      y_sb[:, :]).then_inc(z_ys, 16)

                    def step(g, parts=()):
                        hidden_hi(g - 1)
                        for p in parts[:2]:
                            split_hi(*p)
                        gelu(g)
                        turn_hi(g + 2)
                        for p in parts[2:]:
                            split_hi(*p)
                        take_y(g - 1)

                    def expert(e, b, lead=False, more=True):
                        first, last = bounds(act, e)
                        parts = [[(e + 1, 1 - b, 4 * i + q) for q in range(4)] if more else [] for i in range(2)]
                        if lead:
                            step(first, parts[0])
                        else:
                            for p in parts[0]:
                                split_hi(*p)
                        if more:
                            with act.If(last - first < 2):
                                for p in parts[1]:
                                    split_hi(*p)
                        with act.If(first + 1 < last):
                            step(first + 1, parts[1])
                            with act.If(first + 2 < last):
                                with act.Fori(first + 2, last) as g:
                                    step(g)

                    for q in range(4):
                        split_hi(0, 0, q)
                    turn_hi(1)
                    for q in range(4, 8):
                        split_hi(0, 0, q)
                    gelu(0)
                    turn_hi(2)
                    all_experts(act, expert)
                    expert(NX - 1, 1, True, False)
                    total = act.value_load(chunk0[0:1, NX:NX + 1], min_val=NX, max_val=NCH)
                    hidden_hi(total - 1)
                    take_y(total - 1)
                    with act.If(total < NCH):
                        with act.Fori(total, NCH) as g:
                            act.dma_start(ye_dram.rearrange("(g p) n -> g p n", p=P)[ds(g, 1), :, :].rearrange("g p n -> (g p) n"),
                                          y_sb[:, :]).then_inc(z_ys, 16)
                    act.wait_ge(z_ys, NCH * 16 + 16)

                @block.vector
                def _(dve):
                    n = [0]

                    def step(ins):
                        n[0] += 1
                        ins.then_inc(z_dve, 1)
                        dve.wait_ge(z_dve, n[0])

                    flat = "p t e -> p (t e)"
                    nc.vector.tensor_reduce(red[:, 0, :], logits[:, :, :], AX.X, ALU.max).then_inc(z_row, 1)
                    dve.wait_ge(z_row, 1)
                    step(nc.vector.tensor_tensor(prob[:, :, :], logits[:, :, :], red[:, 0, :].unsqueeze(2).broadcast_to([P, T, NX1]), ALU.subtract))
                    dve.wait_ge(z_exp, 1)
                    step(nc.vector.tensor_reduce(red[:, 1, :], prob[:, :, :], AX.X, ALU.add))
                    step(nc.vector.reciprocal(red[:, 2, :], red[:, 1, :]))
                    step(nc.vector.tensor_tensor(prob[:, :, :], prob[:, :, :], red[:, 2, :].unsqueeze(2).broadcast_to([P, T, NX1]), ALU.mult))
                    gt = cmp_[:, 0, :].rearrange("p (t j i) -> p t j i", j=NX1, i=NX1)
                    eq = cmp_[:, 1, :].rearrange("p (t j i) -> p t j i", j=NX1, i=NX1)
                    p_i = prob[:, :, :].unsqueeze(2).broadcast_to([P, T, NX1, NX1])
                    p_j = prob[:, :, :].unsqueeze(3).broadcast_to([P, T, NX1, NX1])
                    dve.wait_ge(z_cst, 6)
                    nc.vector.tensor_tensor(gt, p_i, p_j, ALU.is_gt)
                    step(nc.vector.tensor_tensor(eq, p_i, p_j, ALU.is_equal))
                    step(nc.vector.tensor_tensor(eq, eq, tri[:, :, :].unsqueeze(1).broadcast_to([P, T, NX1, NX1]), ALU.mult))
                    step(nc.vector.tensor_tensor(cmp_[:, 0, :], cmp_[:, 0, :], cmp_[:, 1, :], ALU.add))
                    step(nc.vector.tensor_reduce(rank[:, :, :], gt, AX.X, ALU.add))
                    for c in range(2):
                        step(nc.vector.tensor_scalar(pickAB[:, c, :, :], rank[:, :, :], float(c), None, ALU.is_equal))
                    for c in range(2):
                        step(nc.vector.tensor_tensor(pickAB[:, c, :, :], pickAB[:, c, :, :], real[:, :].unsqueeze(2).broadcast_to([P, T, NX1]), ALU.mult))
                    step(nc.vector.tensor_tensor(cume[0][:, :, :], pickAB[:, 0, :, 0:NX].rearrange("p t e -> p e t"),
                                                 pickAB[:, 1, :, 0:NX].rearrange("p t e -> p e t"), ALU.add))
                    a, b, d = cume[0], cume[1], 1
                    while d < T:
                        nc.vector.tensor_copy(b[:, :, 0:d], a[:, :, 0:d])
                        step(nc.vector.tensor_tensor(b[:, :, d:T], a[:, :, d:T], a[:, :, 0:T - d], ALU.add))
                        a, b, d = b, a, 2 * d
                    nc.vector.tensor_copy(pre3[:, 0, 0:NX], a[:, :, T - 1]).then_inc(z_row, 1)
                    for c in range(2):
                        step(nc.vector.tensor_tensor(tmp9[:, :, :], prob[:, :, :], pickAB[:, c, :, :], ALU.mult))
                        step(nc.vector.tensor_reduce(gates[:, c, :], tmp9[:, :, 0:NX], AX.X, ALU.add))
                        step(nc.vector.tensor_copy(red[:, 3 + c, :], tmp9[:, :, NX]))
                    step(nc.vector.tensor_tensor(gates[:, 2, :], red[:, 3, :], red[:, 4, :], ALU.add))
                    step(nc.vector.tensor_tensor(red[:, 5, :], gates[:, 2, :], stats2[:, :, 1], ALU.mult))
                    nc.vector.tensor_scalar(mix[:, 0, :], red[:, 5, :], 1.0, None, ALU.add)
                    step(nc.vector.scalar_tensor_tensor(mix[:, 1, :], red[:, 5, :], -1.0, stats2[:, :, 0], ALU.mult, ALU.mult))
                    dve.wait_ge(z_pre, 1)
                    step(nc.vector.tensor_scalar(pre3_i[:, 0:NX], ps_rt[:, 1, 0:NX], float(P - 1), None, ALU.add))
                    step(nc.vector.tensor_scalar(pre3_i[:, 0:NX], pre3_i[:, 0:NX], P.bit_length() - 1, None, ALU.arith_shift_right))
                    nc.vector.memset(pre3[:, 2, 0:1], 0.0)
                    step(nc.vector.tensor_scalar(pre3[:, 1, 0:NX], pre3_i[:, 0:NX], 1.0, None, ALU.max))
                    for k in range(NX):
                        step(nc.vector.tensor_tensor(pre3[:, 2, k + 1:k + 2], pre3[:, 2, k:k + 1], pre3[:, 1, k:k + 1], ALU.add))
                    nc.vector.tensor_copy(chunk0[:, :], pre3[:, 2, 0:NX + 1])
                    step(nc.vector.scalar_tensor_tensor(pre3[:, 3, 0:NX], pre3[:, 2, 0:NX], float(P), ps_rt[:, 0, 0:NX], ALU.mult, ALU.add))
                    step(nc.vector.tensor_scalar(pre3[:, 3, 0:NX], pre3[:, 3, 0:NX], -1.0, None, ALU.add))
                    step(nc.vector.tensor_tensor(b[:, :, :], a[:, :, :], pre3[:, 3, 0:NX].unsqueeze(2).broadcast_to([P, NX, T]), ALU.add))
                    for c in range(2):
                        chosen = pickAB[:, c, :, 0:NX]
                        step(nc.vector.tensor_tensor(tmp9[:, :, 0:NX], chosen, b[:, :, :].rearrange("p e t -> p t e"), ALU.mult))
                        step(nc.vector.tensor_reduce(red[:, 6, :], tmp9[:, :, 0:NX], AX.X, ALU.add))
                        step(nc.vector.tensor_copy(idx_ga[:, c, :], red[:, 6, :]))
                        step(nc.vector.tensor_reduce(red[:, 7, :], chosen, AX.X, ALU.add))
                        step(nc.vector.tensor_scalar(red[:, 7, :], red[:, 7, :], -float(2 * NCH * P), float(2 * NCH * P), ALU.mult, ALU.add))
                        step(nc.vector.tensor_tensor(idx_sc[:, c, :], red[:, 6, :], red[:, 7, :], ALU.add))
                    dve.sem_inc(z_idx, 1)

                    def split_lo(e, b, q):
                        dve.wait_ge(z_whi, e * 8 + q + 1)
                        hi = w1_hi[b][:, 2 * q:2 * q + 2, :].rearrange("p k f -> p (k f)") if q < 4 else w2_hi[b][:, q - 4, :]
                        lo = w1_lo[b][:, 2 * q:2 * q + 2, :].rearrange("p k f -> p (k f)") if q < 4 else w2_lo[b][:, q - 4, :]
                        nc.vector.tensor_tensor(lo, e_stage[:, q % 4, :], hi.bitcast(F32), ALU.subtract).then_inc(z_wlo, 1)

                    def turn_lo(n):
                        dve.wait_ge(z_xhi, n)
                        nc.vector.tensor_tensor(xgT_lo[:, :], ps_x[:, :], xgT_hi[:, :].bitcast(F32), ALU.subtract).then_inc(z_xlo, 1)

                    def hidden_lo(g):
                        dve.wait_ge(z_hhi, g + 1)
                        nc.vector.tensor_tensor(hT_lo[:, :], ps_hT[:, :], hT_hi[:, :].bitcast(F32), ALU.subtract).then_inc(z_hlo, 1)

                    def take_y(g):
                        dve.wait_ge(z_y, g + 1)
                        dve.wait_ge(z_ys, g * 16 + 16)
                        nc.vector.tensor_copy(y_sb[:, H:D], ps_y2[:, H:D]).then_inc(z_yc, 1)

                    def low_step(g, parts=()):
                        hidden_lo(g - 1)
                        for p in parts[:2]:
                            split_lo(*p)
                        turn_lo(g + 2)
                        for p in parts[2:]:
                            split_lo(*p)
                        take_y(g - 1)

                    def expert(e, b, lead=False, more=True):
                        first, last = bounds(dve, e)
                        parts = [[(e + 1, 1 - b, 4 * i + q) for q in range(4)] if more else [] for i in range(2)]
                        if lead:
                            low_step(first, parts[0])
                        else:
                            for p in parts[0]:
                                split_lo(*p)
                        if more:
                            with dve.If(last - first < 2):
                                for p in parts[1]:
                                    split_lo(*p)
                        with dve.If(first + 1 < last):
                            low_step(first + 1, parts[1])
                            with dve.If(first + 2 < last):
                                with dve.Fori(first + 2, last) as g:
                                    low_step(g)

                    for q in range(4):
                        split_lo(0, 0, q)
                    turn_lo(1)
                    for q in range(4, 8):
                        split_lo(0, 0, q)
                    turn_lo(2)
                    all_experts(dve, expert)
                    expert(NX - 1, 1, True, False)
                    total = dve.value_load(chunk0[0:1, NX:NX + 1], min_val=NX, max_val=NCH)
                    hidden_lo(total - 1)
                    take_y(total - 1)

                @block.tensor
                def _(pe):
                    pe.wait_ge(z_row, 2)
                    nc.tensor.matmul(ps_rt[:, 0, 0:NX], lower[:, :], pre3[:, 0, 0:NX], start=True, stop=True)
                    nc.tensor.matmul(ps_rt[:, 1, 0:NX], ones[:, :], pre3[:, 0, 0:NX], start=True, stop=True).then_inc(z_pre, 1)
                    pe.wait_ge(z_idx, 1)

                    def turn(n):
                        pe.wait_ge(z_xg, n * 16)
                        for k in range(KT):
                            m = nc.tensor.transpose(ps_x[:, k * P:(k + 1) * P], xg[:, k * P:(k + 1) * P], ident[:, :])
                        m.then_inc(z_xt, 1)

                    def first_product(g, b):
                        pe.wait_ge(z_xlo, g + 1)
                        for k in range(KT):
                            w = slice(k * P, (k + 1) * P)
                            nc.tensor.matmul(ps_h[:, :], xgT_lo[:, w], w1_hi[b][:, k, :], start=(k == 0), stop=False)
                            nc.tensor.matmul(ps_h[:, :], xgT_hi[:, w], w1_lo[b][:, k, :], start=False, stop=False)
                            m = nc.tensor.matmul(ps_h[:, :], xgT_hi[:, w], w1_hi[b][:, k, :], start=False, stop=(k == KT - 1))
                        m.then_inc(z_h, 1)

                    def turn_hidden(g):
                        pe.wait_ge(z_gelu, g + 1)
                        for k in range(FK):
                            m = nc.tensor.transpose(ps_hT[:, k * P:(k + 1) * P], h_sb[:, k * P:(k + 1) * P], ident[:, :])
                        m.then_inc(z_ht, 1)

                    def second_product(g, b):
                        pe.wait_ge(z_hlo, g + 1)
                        pe.wait_ge(z_yc, g * 2 + 2)
                        for h in range(2):
                            o = slice(h * H, (h + 1) * H)
                            for k in range(FK):
                                w = slice(k * P, (k + 1) * P)
                                nc.tensor.matmul(ps_y2[:, o], hT_lo[:, w], w2_hi[b][:, k, o], start=(k == 0), stop=False)
                                nc.tensor.matmul(ps_y2[:, o], hT_hi[:, w], w2_lo[b][:, k, o], start=False, stop=False)
                                m = nc.tensor.matmul(ps_y2[:, o], hT_hi[:, w], w2_hi[b][:, k, o], start=False, stop=(k == FK - 1))
                        m.then_inc(z_y, 1)

                    def step(g, b, b_before):
                        turn_hidden(g - 1)
                        first_product(g, b)
                        turn(g + 2)
                        second_product(g - 1, b_before)

                    def expert(e, b, lead=False):
                        first, last = bounds(pe, e)
                        if lead:
                            pe.wait_ge(z_wlo, e * 8 + 4)
                            pe.sem_inc(z_pe, 1)
                            step(first, b, 1 - b)
                        with pe.If(first + 1 < last):
                            pe.wait_ge(z_wlo, e * 8 + 8)
                            pe.sem_inc(z_pe, 1)
                            with pe.Fori(first + 1, last) as g:
                                step(g, b, b)

                    turn(1)
                    pe.wait_ge(z_wlo, 4)
                    first_product(0, 0)
                    turn(2)
                    all_experts(pe, expert)
                    expert(NX - 1, 1, True)
                    total = pe.value_load(chunk0[0:1, NX:NX + 1], min_val=NX, max_val=NCH)
                    turn_hidden(total - 1)
                    pe.wait_ge(z_wlo, NX * 8)
                    second_product(total - 1, 1)

            ya = [e_stage[:, i, :] for i in range(2)]
            yb = [e_stage[:, 2 + i, :] for i in range(2)]
            xo = [xg[:, :], y_sb[:, :]]
            f_x, f_ga, f_mix, f_sum = [sem(f"x1_loaded{i}") for i in range(2)], [sem(f"out_gathered{i}") for i in range(2)], sem("x1_mixed"), sem("out_summed")
            f_out = [sem(f"out_stored{i}") for i in range(2)]
            with nc.Block() as block:
                @block.gpsimd
                def _(pool):
                    for t in range(T):
                        b = t % 2
                        if t >= 2:
                            pool.wait_ge(f_sum, 2 * (t - 2) + 2)
                        for c, to in enumerate((ya[b], yb[b])):
                            pool.indirect_dma_start(to, None, ye_dram, bass.IndirectOffsetOnAxis(idx_ga[:, c, t:t + 1], 0),
                                                    bounds_check=NCH * P - 1).then_inc(f_ga[b], 16)

                @block.sync
                def _(sp):
                    for t in range(T):
                        b = t % 2
                        if t >= 2:
                            sp.wait_ge(f_sum, 2 * (t - 2) + 2)
                            sp.dma_start(out[(t - 2) * P:(t - 1) * P, :], xo[b]).then_inc(f_out[b], 16)
                            sp.wait_ge(f_out[b], 16 * (t // 2))
                        sp.dma_start(xo[b], x1_dram[t * P:(t + 1) * P, :]).then_inc(f_x[b], 16)
                    for t in (T - 2, T - 1):
                        n = LAST if t == T - 1 else P
                        sp.wait_ge(f_sum, 2 * t + 2)
                        sp.dma_start(out[t * P:t * P + n, :], xo[t % 2][0:n, :]).then_inc(f_out[t % 2], 16)
                    for b in range(2):
                        sp.wait_ge(f_out[b], 16 * (T // 2))

                @block.scalar
                def _(act):
                    for t in range(T):
                        b = t % 2
                        act.wait_ge(f_x[b], 16 * (t // 2 + 1))
                        nc.scalar.activation(xo[b], xo[b], ACT.Identity, scale=mix[:, 0, t:t + 1], bias=mix[:, 1, t:t + 1]).then_inc(f_mix, 1)

                @block.vector
                def _(dve):
                    for t in range(T):
                        b = t % 2
                        dve.wait_ge(f_mix, t + 1)
                        dve.wait_ge(f_ga[b], 32 * (t // 2 + 1))
                        nc.vector.scalar_tensor_tensor(xo[b], ya[b], gates[:, 0, t:t + 1], xo[b], ALU.mult, ALU.add).then_inc(f_sum, 1)
                        dve.wait_ge(f_sum, 2 * t + 1)
                        nc.vector.scalar_tensor_tensor(xo[b], yb[b], gates[:, 1, t:t + 1], xo[b], ALU.mult, ALU.add).then_inc(f_sum, 1)


def kernel(**inputs):
    import numpy as np
    import concourse.bacc as bacc
    from concourse import mybir
    from concourse.bass_utils import run_bass_kernel_spmd

    a = lay_out(inputs)
    nc = bacc.Bacc("TRN2", target_bir_lowering=False, num_devices=1)
    args = {k: nc.dram_tensor(k, v.shape, mybir.dt.from_np(v.dtype), kind="ExternalInput").ap() for k, v in a.items()}
    out = nc.dram_tensor("out", inputs["x"].shape, mybir.dt.float32, kind="ExternalOutput").ap()
    build_program(nc, out=out, **args)
    r = run_bass_kernel_spmd(nc, [a], core_ids=[0])
    return r.results[0]["out"]


def lay_out(inputs):
    import numpy as np
    g = {k: np.ascontiguousarray(v) for k, v in inputs.items()}
    d = g["x"].shape[1]
    return dict(x=g["x"], src=g["src"], dst=g["dst"], typ=g["edge_type_8"],
                w_all=np.concatenate([g["L0_gnn_weight"], g["L0_gnn_root"][None], g["L0_gnn_w_gate"][None, d:]]),
                bias=g["L0_gnn_bias"][None], w_gate_u=g["L0_gnn_w_gate"][:d], b_gate=g["L0_gnn_b_gate"][None],
                router_w=g["L0_ffn_router_w"], router_b=g["L0_ffn_router_b"][None], w1=g["L0_ffn_w1"], w2=g["L0_ffn_w2"])
```

```python
def build_program(nc, x, src, dst, typ, w_all, bias, w_gate_u, b_gate, router_w, router_b, w1, w2, out):
    from contextlib import ExitStack
    import concourse.bass as bass
    from concourse import mybir

    F32, F32R, BF16, I32 = mybir.dt.float32, mybir.dt.float32r, mybir.dt.bfloat16, mybir.dt.int32
    F8 = mybir.dt.float8e4
    ALU, ACT, AX = mybir.AluOpType, mybir.ActivationFunctionType, mybir.AxisListType
    ds = bass.ds

    P = 128
    N, D = x.shape
    T = -(-N // P)
    NP = T * P
    LAST = N - (T - 1) * P
    KT = D // P
    H = 512
    UNITS = w_all.shape[0]
    R = UNITS - 2
    ROOT, GATE_X = R, R + 1
    E = src.shape[0]
    EP = 125
    EC = E // EP
    PAIR = 2 * P
    PAIRS = (E + T * PAIR) // PAIR
    CH = 16 * -(-PAIRS // 8)
    PC = 8
    NPIECE = EC // PC
    SC = 8
    EPS = 1e-5
    TR = T * R
    NX, F = w1.shape[0], w1.shape[2]
    NX1 = NX + 1
    NCH = (2 * N + NX * P) // P

    ctx = ExitStack()

    def sem(name):
        return ctx.enter_context(nc.semaphore(name))

    def dram(name, shape, dt):
        return nc.dram_tensor(name, shape, dt, kind="Internal").ap()

    y_dram = dram("y_scratch", [UNITS * NP, D], F32)
    winv_dram = dram("winv_scratch", [TR * P, 1], F32)
    sum_dram = dram("sum_scratch", [NP + P, D], F32)
    xn2_dram = dram("xn2_scratch", [NP, D], F32)
    slot_dram = dram("slot_scratch", [CH * P, 4], I32)

    with ctx:
        def sb(stack, name, shape, dt):
            return stack.enter_context(nc.sbuf_tensor(name, shape, dt))

        def ps(stack, name, shape, dt=F32):
            return stack.enter_context(nc.psum_tensor(name, shape, dt))

        ident = sb(ctx, "ident", [P, P], F32)
        lower = sb(ctx, "lower", [P, P], F32)
        ones = sb(ctx, "ones", [P, P], F32)
        iota_row = sb(ctx, "iota_row", [P, P], F32)
        stats = sb(ctx, "stats", [P, T, 2], F32)
        starts = sb(ctx, "starts", [P, T + 2], I32)
        slots = sb(ctx, "slots", [P, CH, 4], I32)
        stats2 = sb(ctx, "stats2", [P, T, 2], F32)
        logits = sb(ctx, "logits", [P, T, NX1], F32)
        newton = sb(ctx, "newton", [P, 4], F32)
        winv = sb(ctx, "winv", [P, CH], F32)

        def inverse_root(step, out_, var, tmp):
            v, a, y = tmp[:, 0:1], tmp[:, 1:2], tmp[:, 2:3]
            step(nc.vector.tensor_scalar(v, var, EPS, None, ALU.add))
            step(nc.vector.tensor_scalar(a.bitcast(I32), v.bitcast(I32), 1, None, ALU.arith_shift_right))
            step(nc.vector.tensor_scalar(y.bitcast(I32), a.bitcast(I32), -1.0, float(0x5F3759DF), ALU.mult, ALU.add))
            for n in range(3):
                step(nc.vector.tensor_scalar(a, y, y, v, ALU.mult, ALU.mult))
                step(nc.vector.tensor_scalar(a, a, -0.5, 1.5, ALU.mult, ALU.add))
                y_new = out_ if n == 2 else y
                step(nc.vector.tensor_tensor(y_new, y, a, ALU.mult))

        with ExitStack() as ph:
            xs = sb(ph, "xs", [P, 2, D], F32)
            xn = sb(ph, "xn", [P, 2, D], F32)
            bst = sb(ph, "bst", [P, 2, 2, 6], F32)
            mv = sb(ph, "mv", [P, 2, 2], F32)
            xT_hi = sb(ph, "xT_hi", [P, KT, NP], F32R)
            xT_lo = sb(ph, "xT_lo", [P, KT, NP], F32R)
            w_stage = sb(ph, "w_stage", [P, 4, 2, H], F32)
            w_hi = [sb(ph, f"w_hi{i}", [P, KT, H], F32R) for i in range(2)]
            w_lo = [sb(ph, f"w_lo{i}", [P, KT, H], F32R) for i in range(2)]
            y_out = sb(ph, "y_out", [P, 4, H], F32)
            ps_t = ps(ph, "ps_t", [P, 2, H])
            ps_y = ps(ph, "ps_y", [P, 4, H])
            ps_cnt = ps(ph, "ps_cnt", [P, H])
            ps_pre = ps(ph, "ps_pre", [P, 2, H // 2])

            edge_i = sb(ph, "edge_i", [EP, 3, EC], I32)
            tile_i = sb(ph, "tile_i", [EP, EC], I32)
            loc_i = edge_i[:, 1, :]
            edge_f = sb(ph, "edge_f", [EP, 5, EC], F32)
            ohT = sb(ph, "ohT", [EP, T, EC], BF16)
            cum = [v[0:EP, :, :].rearrange("p a b -> p (a b)")[:, 0:T * EC].rearrange("p (k c) -> p k c", k=T) for v in (xs, xn)]
            slot_f = edge_i[:, 0, :].bitcast(F32)
            slot_i = sb(ph, "slot_i", [EP, EC], I32)
            rec = sb(ph, "rec", [EP, EC, 4], I32)
            oh_key = sb(ph, "oh_key", [EP, 2, PC, TR], F8)
            oh_loc = sb(ph, "oh_loc", [EP, 2, PC, P], F8)
            pre = sb(ph, "pre", [P, 6, 16], F32)
            pre_i = sb(ph, "pre_i", [P, 16], I32)
            cnt = sb(ph, "cnt", [TR, 2, P], F32)
            fill = slots
            rec_buf = sb(ph, "rec_buf", [EP, 2, SC, 4], I32)
            idx_buf = sb(ph, "idx_buf", [P, 2, SC], I32)
            win_buf = sb(ph, "win_buf", [P, 2, SC], F32)

            s_x = [sem(f"x_loaded{i}") for i in range(2)]
            s_xpad = sem("x_padded")
            s_const = sem("constants_made")
            s_stat = sem("stats_chain")
            pool_passed, dve_passed, pe_passed = sem("pool_wait_passed"), sem("dve_wait_passed"), sem("pe_wait_passed")
            s_xn = sem("x_normed")
            s_xT = sem("x_transposed")
            s_xhi = sem("xT_hi_made")
            s_xlo = sem("xT_lo_made")
            s_w = [sem(f"w_loaded{i}") for i in range(4)]
            s_whi = sem("w_hi_made")
            s_wlo = sem("w_lo_made")
            s_half = sem("half_multiplied")
            s_y = sem("y_multiplied")
            s_ysb = sem("y_copied")
            s_yst = [sem(f"y_stored{i}") for i in range(4)]
            s_edge = sem("edges_loaded")
            s_fill = sem("filler_made")
            s_fst = sem("filler_stored")
            s_dve = sem("sort_chain")
            s_oh = sem("onehots_made")
            s_ohu = sem("onehots_used")
            s_row = sem("row_totals_made")
            s_pre = sem("prefixes_multiplied")
            s_cinv = sem("winv_made")
            s_cst = sem("winv_stored")
            s_rec = sem("records_made")
            s_cp = sem("scatter_copied")
            s_sc = [sem(f"scattered{i}") for i in range(2)]
            s_sl = sem("slots_loaded")
            s_ga = [sem(f"winv_gathered{i}") for i in range(2)]

            assert T + 3 <= NPIECE <= 2 * T + 3
            y_view = y_dram.rearrange("(u t p) (h n) -> u t p h n", t=T, p=P, h=2)
            w_view = w_all.rearrange("u (k p) (h n) -> u p k h n", p=P, h=2)

            with nc.Block() as block:
                @block.sync
                def _(sp):
                    for i in range(2):
                        sp.dma_start(xs[:, i, :], x[i * P:(i + 1) * P, :]).then_inc(s_x[i], 16)
                    for i, a in enumerate((src, dst, typ)):
                        sp.dma_start(edge_i[:, i, :], a.rearrange("(p c) -> p c", c=EC)).then_inc(s_edge, 16)

                    def load_w(u, half):
                        for q in range(4):
                            n = u * 2 + half
                            if not (isinstance(n, int) and n == 0):
                                sp.wait_ge(s_wlo, n * 4 - 3 + q)
                            sp.dma_start(w_stage[:, q, :, :], w_view[ds(u, 1), :, 2 * q:2 * q + 2, half, :]
                                         .rearrange("u p k n -> (u p) k n")).then_inc(s_w[q], 16)

                    load_w(0, 0)
                    for t in range(2, T):
                        sp.wait_ge(s_xn, t - 1)
                        if t < T - 1:
                            sp.dma_start(xs[:, t % 2, :], x[t * P:(t + 1) * P, :]).then_inc(s_x[t % 2], 16)
                        else:
                            sp.wait_ge(s_xpad, 1)
                            sp.dma_start(xs[0:LAST, t % 2, :], x[t * P:N, :]).then_inc(s_x[t % 2], 16)
                        if t == T // 2:
                            load_w(0, 1)

                    def store_y(u, half):
                        for t in range(T):
                            sp.wait_ge(s_ysb, (u * 2 + half) * T + t + 1)
                            sp.dma_start(y_view[ds(u, 1), t, :, half, :].rearrange("u p n -> (u p) n"),
                                         y_out[:, (half * T + t) % 4, :]).then_inc(s_yst[(half * T + t) % 4], 16)

                    load_w(1, 0)
                    load_w(1, 1)
                    store_y(0, 1)
                    with sp.Fori(1, UNITS - 1) as u:
                        for half in range(2):
                            load_w(u + 1, half)
                            store_y(u, half)
                    for half in range(2):
                        store_y(UNITS - 1, half)
                    for i in range(4):
                        sp.wait_ge(s_yst[i], 16 * UNITS * 2 * T // 4)

                @block.gpsimd
                def _(pool):
                    nc.gpsimd.memset(ident[:, :], 0.0).then_inc(s_const, 1)
                    nc.gpsimd.memset(lower[:, :], 1.0).then_inc(s_const, 1)
                    nc.gpsimd.memset(ones[:, :], 1.0).then_inc(s_const, 1)
                    nc.gpsimd.iota(iota_row[:, :], [[1, P]], base=0, channel_multiplier=0,
                                   allow_small_or_imprecise_dtypes=True).then_inc(s_const, 1)
                    pool.wait_ge(s_const, 4)
                    nc.gpsimd.affine_select(out=ident[:, :], in_=ident[:, :], compare_op=ALU.not_equal, fill=1.0,
                                            base=0, pattern=[[-1, P]], channel_multiplier=1).then_inc(s_const, 1)
                    nc.gpsimd.affine_select(out=lower[:, :], in_=lower[:, :], compare_op=ALU.is_gt, fill=0.0,
                                            base=0, pattern=[[1, P]], channel_multiplier=-1).then_inc(s_const, 1)
                    nc.gpsimd.memset(fill[:, :, :], 0).then_inc(s_fill, 1)
                    pool.wait_ge(s_fill, 1)
                    nc.gpsimd.memset(fill[:, :, 2:3], 2 * P - 1).then_inc(s_fill, 1)
                    pool.wait_ge(s_fill, 2)
                    pool.dma_start(slot_dram.rearrange("(p g) w -> p (g w)", p=P),
                                   fill[:, :, :].rearrange("p g w -> p (g w)")).then_inc(s_fst, 16)
                    pool.wait_ge(s_xn, T - 2)
                    nc.gpsimd.memset(xs[:, (T - 1) % 2, :], 0.0).then_inc(s_xpad, 1)
                    pool.wait_ge(s_fst, 16)
                    pool.wait_ge(s_cinv, 1)
                    pool.dma_start(winv_dram.rearrange("(k c) o -> k (c o)", c=P), cnt[:, 1, :]).then_inc(s_cst, 16)
                    pool.wait_ge(s_rec, 1)

                    def scatter(i, first=False):
                        for b in range(2):
                            n = i * 2 + b
                            if not first:
                                pool.wait_ge(s_sc[b], i * (16 * SC))
                            nc.gpsimd.tensor_copy(rec_buf[:, b, :, :], rec[:, ds(n * SC, SC), :]).then_inc(s_cp, 1)
                            nc.gpsimd.tensor_copy(idx_buf[0:EP, b, :], slot_i[:, ds(n * SC, SC)]).then_inc(s_cp, 1)
                            pool.wait_ge(s_cp, n * 2 + 2)
                            pool.sem_inc(pool_passed, 1)
                            for c in range(SC):
                                pool.indirect_dma_start(
                                    slot_dram, bass.IndirectOffsetOnAxis(idx_buf[0:EP, b, c:c + 1], 0),
                                    rec_buf[:, b, c, :], None, bounds_check=CH * P - 1).then_inc(s_sc[b], 16)

                    scatter(0, True)
                    with pool.Fori(1, EC // (2 * SC)) as i:
                        scatter(i)
                    for b in range(2):
                        pool.wait_ge(s_sc[b], 16 * EC // 2)
                    for i in range(2):
                        g = slice(i * CH // 2, (i + 1) * CH // 2)
                        pool.dma_start(slots[:, g, :], slot_dram.rearrange("(g p) w -> p g w", p=P)[:, g, :]).then_inc(s_sl, 16)
                        pool.wait_ge(s_sl, 16 * (i + 1))
                    pool.wait_ge(s_cst, 16)

                    COPIED = 2 * (EC // SC)

                    def gather(i, first=False):
                        for b in range(2):
                            n = i * 2 + b
                            nc.gpsimd.tensor_copy(idx_buf[:, b, :], slots[:, ds(n * SC, SC), 1]).then_inc(s_cp, 1)
                            pool.wait_ge(s_cp, n + (COPIED + 1))
                            pool.sem_inc(pool_passed, 1)
                            for c in range(SC):
                                pool.indirect_dma_start(
                                    win_buf[:, b, c:c + 1], None, winv_dram,
                                    bass.IndirectOffsetOnAxis(idx_buf[:, b, c:c + 1], 0),
                                    bounds_check=TR * P - 1).then_inc(s_ga[b], 16)
                            if not (first and b == 0):
                                take(n - 1, 1 - b, i - 1 + b)

                    def take(n, b, i):
                        pool.wait_ge(s_ga[b], i * (16 * SC) + 16 * SC)
                        nc.gpsimd.tensor_copy(winv[:, ds(n * SC, SC)], win_buf[:, b, :])

                    gather(0, True)
                    with pool.Fori(1, CH // (2 * SC)) as i:
                        gather(i)
                    take(CH // SC - 1, 1, CH // (2 * SC) - 1)

                @block.scalar
                def _(act):
                    def xT_high(t):
                        act.wait_ge(s_xT, t + 1)
                        nc.scalar.activation(xT_hi[:, :, t * P:(t + 1) * P],
                                             ps_t[:, :, :].rearrange("p b (k c) -> p (b k) c", c=P), ACT.Copy).then_inc(s_xhi, 1)

                    def split_hi(n, half, first=False, parts=range(4)):
                        if not first:
                            act.wait_ge(s_half, n - 1)
                        for q in parts:
                            act.wait_ge(s_w[q], n * 16 + 16)
                            nc.scalar.activation(w_hi[half][:, 2 * q:2 * q + 2, :], w_stage[:, q, :, :], ACT.Copy).then_inc(s_whi, 1)

                    def copy_tile(u, half, t, first=False):
                        m = half * T + t
                        act.wait_ge(s_y, u * (2 * T) + m + 1)
                        i = m % 4
                        if not (first and t < 4):
                            act.wait_ge(s_yst[i], u * (16 * 2 * T // 4) + 16 * (m // 4))
                        nc.scalar.activation(y_out[:, i, :], ps_y[:, i, :], ACT.Copy).then_inc(s_ysb, 1)

                    def copy_y(u, half):
                        for t in range(T):
                            copy_tile(u, half, t)

                    def first_y(t):
                        copy_tile(0, 0, t, True)
                        act.wait_ge(s_ysb, t + 1)
                        act.dma_start(y_view[0, t, :, 0, :], y_out[:, t % 4, :]).then_inc(s_yst[t % 4], 16)

                    for t in range(T):
                        xT_high(t)
                        if t == 0:
                            split_hi(0, 0, True)
                        if t >= T - 4:
                            split_hi(1, 1, True, (t - T + 4,))
                        if t >= 1:
                            first_y(t - 1)
                    first_y(T - 1)
                    split_hi(2, 0)
                    copy_y(0, 1)
                    split_hi(3, 1)
                    with act.Fori(1, UNITS - 1) as u:
                        for half in range(2):
                            copy_y(u, half)
                            split_hi(u * 2 + half + 2, half)
                    for half in range(2):
                        copy_y(UNITS - 1, half)

                @block.vector
                def _(dve):
                    st = [0]

                    def stat(ins):
                        st[0] += 1
                        ins.then_inc(s_stat, 1)
                        dve.wait_ge(s_stat, st[0])

                    def split_lo(n, half):
                        for q in range(4):
                            dve.wait_ge(s_whi, n * 4 + q + 1)
                            nc.vector.tensor_tensor(w_lo[half][:, 2 * q:2 * q + 2, :], w_stage[:, q, :, :],
                                                    w_hi[half][:, 2 * q:2 * q + 2, :].bitcast(F32), ALU.subtract).then_inc(s_wlo, 1)

                    def xT_low(t):
                        dve.wait_ge(s_xhi, t + 1)
                        nc.vector.tensor_tensor(xT_lo[:, :, t * P:(t + 1) * P],
                                                ps_t[:, :, :].rearrange("p b (k c) -> p (b k) c", c=P),
                                                xT_hi[:, :, t * P:(t + 1) * P].bitcast(F32), ALU.subtract).then_inc(s_xlo, 1)

                    for t in range(T):
                        b = t % 2
                        dve.wait_ge(s_x[b], 16 * (t // 2 + 1))
                        for h in range(2):
                            i = nc.vector.bn_stats(bst[:, b, h, :], xs[:, b, h * H:(h + 1) * H])
                        stat(i)
                        stat(nc.vector.bn_aggr(mv[:, b, :], bst[:, b, :, :].rearrange("p h s -> p (h s)")))
                        nc.vector.tensor_copy(stats[:, t, 0:1], mv[:, b, 0:1])
                        inverse_root(stat, stats[:, t, 1:2], mv[:, b, 1:2], newton)
                        if t >= 2:
                            dve.wait_ge(s_xT, t - 1)
                        nc.vector.tensor_scalar(xn[:, b, :], xs[:, b, :], stats[:, t, 0:1], stats[:, t, 1:2],
                                                ALU.subtract, ALU.mult).then_inc(s_xn, 1)
                        if t >= 1:
                            xT_low(t - 1)
                        if t == 1:
                            split_lo(0, 0)
                    xT_low(T - 1)
                    split_lo(1, 1)

                    ch = [0]

                    def step(ins):
                        ch[0] += 1
                        ins.then_inc(s_dve, 1)
                        dve.wait_ge(s_dve, ch[0])

                    dve.wait_ge(s_edge, 48)
                    dve.wait_ge(s_const, 6)
                    nc.vector.tensor_scalar(tile_i[:, :], edge_i[:, 1, :], 7, None, ALU.arith_shift_right)
                    nc.vector.tensor_scalar(loc_i, edge_i[:, 1, :], P - 1, None, ALU.bitwise_and)
                    nc.vector.tensor_copy(edge_f[:, 0, :], edge_i[:, 0, :])
                    step(nc.vector.tensor_copy(edge_f[:, 2, :], edge_i[:, 2, :]))
                    nc.vector.tensor_copy(edge_f[:, 1, :], loc_i)
                    step(nc.vector.tensor_copy(edge_f[:, 3, :], tile_i[:, :]))
                    step(nc.vector.scalar_tensor_tensor(edge_f[:, 4, :], edge_f[:, 2, :], float(T), edge_f[:, 3, :], ALU.mult, ALU.add))

                    def onehots(j):
                        c, b = slice(j * PC, (j + 1) * PC), j % 2
                        if j >= 2:
                            dve.wait_ge(s_ohu, j - 1)
                        nc.vector.tensor_tensor(oh_key[:, b, :, :], edge_f[:, 4, c].unsqueeze(2).broadcast_to([EP, PC, TR]),
                                                iota_row[0:EP, 0:TR].unsqueeze(1).broadcast_to([EP, PC, TR]), ALU.is_equal, saturate=False).then_inc(s_oh, 1)
                        nc.vector.tensor_tensor(oh_loc[:, b, :, :], edge_f[:, 1, c].unsqueeze(2).broadcast_to([EP, PC, P]),
                                                iota_row[0:EP, :].unsqueeze(1).broadcast_to([EP, PC, P]), ALU.is_equal, saturate=False).then_inc(s_oh, 1)

                    onehots(0)
                    onehots(1)
                    dve.wait_ge(s_xT, T)
                    step(nc.vector.tensor_tensor(ohT[:, :, :], edge_f[:, 3, :].unsqueeze(1).broadcast_to([EP, T, EC]),
                                                 iota_row[0:EP, 0:T].unsqueeze(2).broadcast_to([EP, T, EC]), ALU.is_equal))
                    a, b, d = ohT, cum[0], 1
                    while d < EC:
                        nc.vector.tensor_copy(b[:, :, 0:d], a[:, :, 0:d])
                        step(nc.vector.tensor_tensor(b[:, :, d:EC], a[:, :, d:EC], a[:, :, 0:EC - d], ALU.add))
                        a, b, d = b, (cum[1] if b is cum[0] else cum[0]), 2 * d
                    run, tmp = a, b
                    nc.vector.tensor_copy(pre[0:EP, 0, 0:T], run[:, :, EC - 1]).then_inc(s_row, 1)
                    split_lo(2, 0)
                    for j in range(2, 6):
                        onehots(j)
                    dve.wait_ge(s_pre, 1)
                    step(nc.vector.tensor_scalar(pre_i[:, 0:T], ps_pre[:, 1, 0:T], float(PAIR - 1), None, ALU.add))
                    step(nc.vector.tensor_scalar(pre_i[:, 0:T], pre_i[:, 0:T], PAIR.bit_length() - 1, None, ALU.arith_shift_right))
                    nc.vector.memset(pre[:, 2, 0:1], 0.0)
                    step(nc.vector.tensor_scalar(pre[:, 1, 0:T], pre_i[:, 0:T], 1.0, None, ALU.max))
                    for k in range(T):
                        step(nc.vector.tensor_tensor(pre[:, 2, k + 1:k + 2], pre[:, 2, k:k + 1], pre[:, 1, k:k + 1], ALU.add))
                    nc.vector.tensor_copy(starts[:, 0:T + 1], pre[:, 2, 0:T + 1])
                    step(nc.vector.tensor_scalar(pre_i[:, 0:1], pre[:, 2, T:T + 1], 3.0, None, ALU.add))
                    nc.vector.tensor_scalar(starts[:, T + 1:T + 2], pre_i[:, 0:1], 2, None, ALU.arith_shift_right)
                    step(nc.vector.scalar_tensor_tensor(pre[0:EP, 3, 0:T], pre[0:EP, 2, 0:T], float(PAIR), ps_pre[0:EP, 0, 0:T], ALU.mult, ALU.add))
                    step(nc.vector.tensor_scalar(pre[0:EP, 3, 0:T], pre[0:EP, 3, 0:T], -1.0, None, ALU.add))
                    step(nc.vector.tensor_tensor(tmp[:, :, :], run[:, :, :], pre[0:EP, 3, 0:T].unsqueeze(2).broadcast_to([EP, T, EC]), ALU.add))
                    step(nc.vector.tensor_tensor(tmp[:, :, :], tmp[:, :, :], ohT[:, :, :], ALU.mult))
                    step(nc.vector.tensor_reduce(slot_f, tmp[:, :, :].rearrange("p k c -> p c k"), AX.X, ALU.add))
                    nc.vector.tensor_copy(slot_i[:, :], slot_f)
                    nc.vector.memset(rec[:, :, 3], 0)
                    nc.vector.scalar_tensor_tensor(rec[:, :, 0], edge_f[:, 2, :], float(NP), edge_f[:, 0, :], ALU.mult, ALU.add)
                    nc.vector.scalar_tensor_tensor(rec[:, :, 1], edge_f[:, 4, :], float(P), edge_f[:, 1, :], ALU.mult, ALU.add)
                    step(nc.vector.tensor_copy(rec[:, :, 2], edge_f[:, 1, :]))
                    for j in range(6, NPIECE):
                        onehots(j)
                        if j == NPIECE // 2:
                            split_lo(3, 1)
                        if j == NPIECE - 3:
                            split_lo(4, 0)
                    dve.wait_ge(s_ohu, NPIECE)
                    step(nc.vector.tensor_scalar(cnt[:, 0, :], ps_cnt[0:TR, 0:P], 1.0, None, ALU.max))
                    nc.vector.reciprocal(cnt[:, 1, :], cnt[:, 0, :]).then_inc(s_cinv, 1)
                    dve.wait_ge(s_cinv, 1)
                    nc.vector.memset(cnt[:, 0, 0:1], 0.0).then_inc(s_rec, 1)
                    split_lo(5, 1)
                    with dve.Fori(3, UNITS) as u:
                        for half in range(2):
                            split_lo(u * 2 + half, half)

                @block.tensor
                def _(pe):
                    pe.wait_ge(s_const, 6)

                    def turn_x(t):
                        pe.wait_ge(s_xn, t + 1)
                        if t >= 1:
                            pe.wait_ge(s_xlo, t)
                        for k in range(KT):
                            i = nc.tensor.transpose(ps_t[:, k // 4, (k % 4) * P:(k % 4 + 1) * P],
                                                    xn[:, t % 2, k * P:(k + 1) * P], ident[:, :])
                        i.then_inc(s_xT, 1)

                    def product(n, half, t, first=False):
                        if not (first and t < 4):
                            pe.wait_ge(s_ysb, n * T + t - 3)
                        for k in range(KT):
                            hi, lo = xT_hi[:, k, t * P:(t + 1) * P], xT_lo[:, k, t * P:(t + 1) * P]
                            nc.tensor.matmul(ps_y[:, (half * T + t) % 4, :], lo, w_hi[half][:, k, :], start=(k == 0), stop=False)
                            nc.tensor.matmul(ps_y[:, (half * T + t) % 4, :], hi, w_lo[half][:, k, :], start=False, stop=False)
                            i = nc.tensor.matmul(ps_y[:, (half * T + t) % 4, :], hi, w_hi[half][:, k, :], start=False, stop=(k == KT - 1))
                        i.then_inc(s_y, 1)

                    def multiply(n, half, between=None):
                        pe.wait_ge(s_wlo, n * 4 + 4)
                        for t in range(T):
                            product(n, half, t)
                            if between:
                                between(t)
                        pe.wait_ge(s_y, n * T + T)
                        pe.sem_inc(s_half, 1)

                    def count(j):
                        pe.wait_ge(s_oh, 2 * j + 2)
                        for c in range(PC):
                            i = nc.tensor.matmul(ps_cnt[0:TR, 0:P], oh_key[:, j % 2, c, :], oh_loc[:, j % 2, c, :],
                                                 start=(j == 0 and c == 0), stop=(j == NPIECE - 1 and c == PC - 1))
                        i.then_inc(s_ohu, 1)

                    def prefixes():
                        pe.wait_ge(s_row, 1)
                        nc.tensor.matmul(ps_pre[0:EP, 0, 0:T], lower[0:EP, 0:EP], pre[0:EP, 0, 0:T], start=True, stop=True)
                        nc.tensor.matmul(ps_pre[:, 1, 0:T], ones[0:EP, :], pre[0:EP, 0, 0:T], start=True, stop=True).then_inc(s_pre, 1)

                    turn_x(0)
                    for t in range(1, T):
                        turn_x(t)
                        if t == 1:
                            pe.wait_ge(s_wlo, 4)
                        product(0, 0, t - 1, True)
                    pe.wait_ge(s_xlo, T)
                    product(0, 0, T - 1, True)
                    pe.wait_ge(s_y, T)
                    pe.sem_inc(s_half, 1)
                    def first_counts(t):
                        if t in (2, 3):
                            count(t - 2)
                        if t == T - 3:
                            prefixes()
                        if t >= T - 2:
                            count(t - T + 4)

                    multiply(1, 1, first_counts)
                    multiply(2, 0, lambda t: count(t + 3) if t >= 1 else None)
                    multiply(3, 1, lambda t: count(T + 3 + t) if T + 3 + t < NPIECE else None)
                    with pe.Fori(2, UNITS) as u:
                        for half in range(2):
                            multiply(u * 2 + half, half)

        with ExitStack() as ph:
            G8 = 8
            LAG = 3
            msg = sb(ph, "msg", [P, G8, D], F32)
            S = 512
            part_hi = sb(ph, "part_hi", [P, 4, S], F32R)
            part_lo = sb(ph, "part_lo", [P, 4, S], F32R)
            sel = [sb(ph, f"sel{i}", [P, P], F32R) for i in range(2)]
            row_idx = sb(ph, "row_idx", [P, 2, 4], I32)
            slot_loc = sb(ph, "slot_loc", [P, CH], F32)
            y_root = sb(ph, "y_root", [P, D], F32)
            y_gate = sb(ph, "y_gate", [P, D], F32)
            xr = sb(ph, "xr", [P, 2, D], F32)
            xnr = sb(ph, "xnr", [P, D], F32)
            u_sb = sb(ph, "u_sb", [P, 2, D], F32)
            tanh_u = sb(ph, "tanh_u", [P, D], F32)
            z_sb = sb(ph, "z_sb", [P, D], F32)
            uT_hi = sb(ph, "uT_hi", [P, KT, P], F32R)
            uT_lo = sb(ph, "uT_lo", [P, KT, P], F32R)
            x1 = sb(ph, "x1", [P, D], F32)
            xn2 = sb(ph, "xn2", [P, D], F32)
            xn2T = sb(ph, "xn2T", [P, KT, P], F32)
            wg_hi = sb(ph, "wg_hi", [P, KT, D], F32R)
            wg_lo = sb(ph, "wg_lo", [P, KT, D], F32R)
            wg_stage = sb(ph, "wg_stage", [P, 2, D], F32)
            rw = sb(ph, "rw", [P, KT, NX1], F32)
            rows = sb(ph, "rows", [3, D], F32)
            pick = sb(ph, "pick", [3, 3, P], F32)
            fast_pick = sb(ph, "fast_pick", [3, 2, P], F32R)
            rows_hi = sb(ph, "rows_hi", [3, D], F32R)
            rows_lo = sb(ph, "rows_lo", [3, D], F32R)
            affine = sb(ph, "affine", [P, 2, T], F32)
            bst2 = sb(ph, "bst2", [P, 2, 6], F32)
            mv2 = sb(ph, "mv2", [P, 2], F32)
            ps_u = ps(ph, "ps_u", [P, 2, H])
            ps_z = ps(ph, "ps_z", [P, 2, H])
            ps_tr = ps(ph, "ps_tr", [P, 2, H])
            ps_log = ps(ph, "ps_log", [P, 4, P])

            q_par = [sem(f"params_loaded{i}") for i in range(2)]
            q_wg = [sem(f"wg_loaded{i}") for i in range(2)]
            q_wghi, q_wglo = sem("wg_hi_made"), sem("wg_lo_made")
            q_cst = sem("phase2_constants")
            q_rhi, q_rlo = sem("rows_hi_made"), sem("rows_lo_made")
            q_yr, q_yg, q_xr = sem("y_root_loaded"), sem("y_gate_loaded"), [sem(f"x_again_loaded{i}") for i in range(2)]
            q_idx = sem("row_idx_copied")
            q_ga = [sem(f"message_gathered{i}") for i in range(G8)]
            q_land = sem("messages_there")
            q_mhi, q_msc = sem("message_hi_made"), sem("message_scaled")
            q_sel = sem("message_lo_and_selection_made")
            q_agg = sem("message_summed")
            q_psu, q_u, q_ut = sem("u_summed"), sem("u_made"), sem("u_transposed")
            q_uhi, q_ulo = sem("uT_hi_made"), sem("uT_lo_made")
            q_z, q_zc, q_act = sem("z_multiplied"), sem("z_copied"), sem("gate_terms_made")
            q_xn = sem("x_norm_again")
            q_dve = sem("gate_chain")
            q_st = sem("stat2_chain")
            q_x1, q_xn2 = sem("x1_made"), sem("xn2_made")
            q_x1s, q_xn2s = sem("x1_stored"), sem("xn2_stored")
            q_n2t, q_n2c, q_log = sem("xn2_transposed"), sem("xn2T_copied"), sem("logits_made")

            with nc.Block() as block:
                def bounds(eng, t):
                    a = eng.value_load(starts[0:1, ds(t, 1)], min_val=0, max_val=PAIRS - 1)
                    b = eng.value_load(starts[0:1, ds(t + 1, 1)], min_val=0, max_val=PAIRS)
                    return a, b

                def since(t, k):
                    return not isinstance(t, int) or t >= k

                def stages(eng, stage, begun=0, peel_last=False):
                    for t in range(begun, 4):
                        stage(t // 2, t % 2)
                    with eng.Fori(2, T // 2 - (1 if peel_last else 0)) as j:
                        for b in range(2):
                            stage(j, b)
                    if peel_last:
                        for b in range(2):
                            stage(T // 2 - 1, b)

                @block.sync
                def _(sp):
                    sp.wait_ge(q_cst, 4)
                    sp.dma_start(rows[0:1, :], bias).then_inc(q_par[0], 16)
                    sp.dma_start(rows[1:2, :], b_gate).then_inc(q_par[0], 16)
                    sp.dma_start(rows[2:3, 0:NX1], router_b).then_inc(q_par[0], 16)
                    sp.dma_start(rw[:, :, :], router_w.rearrange("(k p) e -> p k e", p=P)).then_inc(q_par[1], 16)
                    yr = y_dram[ROOT * NP:(ROOT + 1) * NP, :].rearrange("(t p) n -> t p n", p=P)
                    yg = y_dram[GATE_X * NP:(GATE_X + 1) * NP, :].rearrange("(t p) n -> t p n", p=P)
                    x_t = x[0:(T - 1) * P, :].rearrange("(t p) n -> t p n", p=P)
                    x1_t = sum_dram.rearrange("(t p) n -> t p n", p=P)
                    xn2_t = xn2_dram.rearrange("(t p) n -> t p n", p=P)
                    wg_t = w_gate_u.rearrange("(k p) n -> p k n", p=P)

                    def load_gate(t):
                        sp.dma_start(y_gate[:, :], yg[ds(t, 1), :, :].rearrange("t p n -> (t p) n")).then_inc(q_yg, 16)

                    def store(t):
                        sp.dma_start(x1_t[ds(t, 1), :, :].rearrange("t p n -> (t p) n"), x1[:, :]).then_inc(q_x1s, 16)
                        sp.wait_ge(q_xn2, t + 1)
                        sp.dma_start(xn2_t[ds(t, 1), :, :].rearrange("t p n -> (t p) n"), xn2[:, :]).then_inc(q_xn2s, 16)

                    def stage(j, b):
                        t = j * 2 + b
                        if since(t, 1):
                            sp.wait_ge(q_u, t)
                        sp.dma_start(y_root[:, :], yr[ds(t, 1), :, :].rearrange("t p n -> (t p) n")).then_inc(q_yr, 16)
                        if since(t, 2):
                            sp.wait_ge(q_x1, t - 1)
                        if since(t, 1):
                            load_gate(t - 1)
                        if isinstance(t, int) and t == T - 1:
                            sp.dma_start(xr[0:LAST, b, :], x[t * P:N, :]).then_inc(q_xr[b], 16)
                        else:
                            sp.dma_start(xr[:, b, :], x_t[ds(t, 1), :, :].rearrange("t p n -> (t p) n")).then_inc(q_xr[b], 16)
                        if since(t, 2):
                            store(t - 2)

                    for k in range(KT):
                        if k >= 2:
                            sp.wait_ge(q_wglo, k - 1)
                        sp.dma_start(wg_stage[:, k % 2, :], wg_t[:, k, :]).then_inc(q_wg[k % 2], 16)
                        if k == 1:
                            stage(0, 0)
                    stages(sp, stage, begun=1, peel_last=True)
                    for t in (T - 2, T - 1):
                        sp.wait_ge(q_x1, t + 1)
                        if t == T - 2:
                            load_gate(T - 1)
                        store(t)
                    sp.dma_start(x1_t[T, :, :], x1[:, :]).then_inc(q_x1s, 16)
                    sp.wait_ge(q_x1s, 16 * T + 16)
                    sp.wait_ge(q_xn2s, 16 * T)

                @block.gpsimd
                def _(pool):
                    eights = pool.value_load(starts[0:1, T + 1:T + 2], min_val=2, max_val=-(-CH // G8))

                    def eight(q, first=False):
                        for j in range(G8):
                            h = j // 4
                            if j % 4 == 0:
                                nc.gpsimd.tensor_copy(row_idx[:, h, :], slots[:, ds(q * G8 + j, 4), 0]).then_inc(q_idx, 1)
                                pool.wait_ge(q_idx, q * 2 + h + 1)
                            pool.wait_ge(q_agg, q * G8 + j + 1)
                            pool.sem_inc(pool_passed, 1)
                            pool.indirect_dma_start(msg[:, j, :], None, y_dram,
                                                    bass.IndirectOffsetOnAxis(row_idx[:, h, j % 4:j % 4 + 1], 0),
                                                    bounds_check=UNITS * NP - 1).then_inc(q_ga[j], 16)
                            if not (first and j < LAG):
                                pool.wait_ge(q_ga[(j - LAG) % G8], q * 16 + (16 if j >= LAG else 0))
                                pool.sem_inc(q_land, 1)

                    eight(0, True)
                    with pool.Fori(1, eights) as q:
                        eight(q)
                    for j in range(G8 - LAG, G8):
                        pool.wait_ge(q_ga[j], eights * 16)
                        pool.sem_inc(q_land, 1)

                @block.scalar
                def _(act):
                    def scale(i):
                        for j in range(2):
                            g = i * 2 + j
                            m, c = msg[:, ds((i % 4) * 2 + j, 1), :].rearrange("p a n -> p (a n)"), winv[:, ds(g, 1)]
                            act.wait_ge(q_land, g + 1)
                            act.wait_ge(q_agg, g + G8 - 3)
                            nc.scalar.activation(part_hi[:, ds((i % 2) * 2 + j, 1), :].rearrange("p a n -> p (a n)"), m[:, 0:S],
                                                 ACT.Copy, scale=c).then_inc(q_mhi, 1)
                            nc.scalar.activation(m[:, S:D], m[:, S:D], ACT.Copy, scale=c).then_inc(q_msc, 1)

                    def terms(j, b):
                        t = j * 2 + b
                        if since(t, 1):
                            act.wait_ge(q_dve, t * 3)
                        nc.scalar.activation(tanh_u[:, :], u_sb[:, b, :], ACT.Tanh).then_inc(q_act, 1)
                        act.wait_ge(q_xr[b], j * 16 + 16)
                        nc.scalar.activation(xnr[:, :], xr[:, b, :], ACT.Identity, scale=stats[:, ds(t, 1), 1], bias=affine[:, 1, ds(t, 1)]).then_inc(q_xn, 1)
                        act.wait_ge(q_xn, t + 1)
                        nc.scalar.activation(xr[:, b, :], xr[:, b, :], ACT.Identity, scale=affine[:, 0, ds(t, 1)], bias=affine[:, 1, ds(t, 1)]).then_inc(q_act, 1)

                    def copy_n2(t):
                        act.wait_ge(q_n2t, t + 1)
                        nc.scalar.activation(xn2T[:, :, :].rearrange("p k c -> p (k c)"),
                                             ps_tr[:, :, :].rearrange("p a n -> p (a n)"), ACT.Copy).then_inc(q_n2c, 1)

                    def copy_z(t):
                        act.wait_ge(q_z, t + 1)
                        nc.scalar.activation(z_sb[:, :],
                                             ps_z[:, :, :].rearrange("p a n -> p (a n)"), ACT.Copy).then_inc(q_zc, 1)

                    def high_u(t):
                        act.wait_ge(q_ut, t + 1)
                        nc.scalar.activation(uT_hi[:, :, :].rearrange("p k c -> p (k c)"),
                                             ps_tr[:, :, :].rearrange("p a n -> p (a n)"), ACT.Copy).then_inc(q_uhi, 1)

                    def wg_high(k):
                        act.wait_ge(q_wg[k % 2], 16 * (k // 2 + 1))
                        if k >= 2:
                            act.wait_ge(q_wglo, k - 1)
                        nc.scalar.activation(wg_hi[:, k, :], wg_stage[:, k % 2, :], ACT.Copy).then_inc(q_wghi, 1)

                    def stage(j, b):
                        t = j * 2 + b
                        first, last = bounds(act, t)
                        if not since(t, 2):
                            wg_high(4 * t)
                            wg_high(4 * t + 1)
                        with act.If(first + 1 < last):
                            with act.Fori(first + 1, last) as i:
                                scale(i)
                        if not since(t, 2):
                            wg_high(4 * t + 2)
                            wg_high(4 * t + 3)
                        if since(t, 3):
                            copy_n2(t - 3)
                        if since(t, 1):
                            terms(j if b else j - 1, 1 - b)
                        if not (isinstance(t, int) and t == T - 1):
                            scale(bounds(act, t + 1)[0])
                        if since(t, 1):
                            copy_z(t - 1)
                        high_u(t)

                    act.wait_ge(q_cst, 5)
                    act.wait_ge(q_par[0], 48)
                    nc.scalar.activation(rows_hi[:, :], rows[:, :], ACT.Copy).then_inc(q_rhi, 1)
                    scale(bounds(act, 0)[0])
                    stages(act, stage, peel_last=True)
                    terms(T // 2 - 1, 1)
                    copy_n2(T - 3)
                    copy_z(T - 1)
                    copy_n2(T - 2)
                    copy_n2(T - 1)

                @block.vector
                def _(dve):
                    nc.vector.memset(rows[:, :], 0.0).then_inc(q_cst, 1)
                    nc.vector.tensor_copy(slot_loc[:, :], slots[:, :, 2]).then_inc(q_cst, 1)
                    nc.vector.tensor_scalar(affine[:, 0, :], stats[:, :, 1], 1.0, None, ALU.add).then_inc(q_cst, 1)
                    nc.vector.scalar_tensor_tensor(affine[:, 1, :], stats[:, :, 0], -1.0, stats[:, :, 1], ALU.mult, ALU.mult).then_inc(q_cst, 1)
                    nc.vector.tensor_copy(fast_pick[:, :, :], ident[0:3, 0:2].unsqueeze(2).broadcast_to([3, 2, P]))
                    nc.vector.tensor_copy(pick[:, :, :], ident[0:3, 0:3].unsqueeze(2).broadcast_to([3, 3, P])).then_inc(q_cst, 1)
                    def wg_low(k):
                        dve.wait_ge(q_wghi, k + 1)
                        nc.vector.tensor_tensor(wg_lo[:, k, :], wg_stage[:, k % 2, :], wg_hi[:, k, :].bitcast(F32), ALU.subtract).then_inc(q_wglo, 1)

                    def select(i):
                        for j in range(2):
                            g = i * 2 + j
                            place = ds((i % 2) * 2 + j, 1)
                            dve.wait_ge(q_mhi, g + 1)
                            nc.vector.scalar_tensor_tensor(part_lo[:, place, :].rearrange("p a n -> p (a n)"),
                                                           msg[:, ds((i % 4) * 2 + j, 1), 0:S].rearrange("p a n -> p (a n)"), winv[:, ds(g, 1)],
                                                           part_hi[:, place, :].rearrange("p a n -> p (a n)").bitcast(F32), ALU.mult, ALU.subtract)
                            dve.wait_ge(q_agg, g + G8 - 1)
                            nc.vector.tensor_scalar(sel[j][:, :], iota_row[:, :], slot_loc[:, ds(g, 1)], None,
                                                    ALU.is_equal).then_inc(q_sel, 1)

                    def messages(t, between):
                        first, last = bounds(dve, t)
                        select(first)
                        between()
                        with dve.If(first + 1 < last):
                            with dve.Fori(first + 1, last) as i:
                                select(i)

                    def take_u(t, b):
                        dve.wait_ge(q_psu, t + 1)
                        dve.wait_ge(q_yr, t * 16 + 16)
                        nc.vector.tensor_tensor(u_sb[:, b, :], ps_u[:, :, :].rearrange("p a n -> p (a n)"), y_root[:, :], ALU.add).then_inc(q_u, 1)

                    def low_u(t):
                        dve.wait_ge(q_uhi, t + 1)
                        nc.vector.tensor_tensor(uT_lo[:, :, :].rearrange("p k c -> p (k c)"), ps_tr[:, :, :].rearrange("p a n -> p (a n)"),
                                                uT_hi[:, :, :].rearrange("p k c -> p (k c)").bitcast(F32), ALU.subtract).then_inc(q_ulo, 1)

                    NS = 12
                    def update(j, b):
                        t = j * 2 + b
                        n3, n12 = t * 3, t * (NS + 2)
                        dve.wait_ge(q_zc, t + 1)
                        dve.wait_ge(q_yg, t * 16 + 16)
                        dve.wait_ge(q_act, t * 2 + 2)
                        nc.vector.tensor_tensor(y_gate[:, :], z_sb[:, :], y_gate[:, :], ALU.add).then_inc(q_dve, 1)
                        nc.vector.tensor_tensor(xnr[:, :], tanh_u[:, :], xnr[:, :], ALU.subtract).then_inc(q_dve, 1)
                        dve.wait_ge(q_dve, n3 + 2)
                        nc.vector.tensor_tensor(y_gate[:, :], y_gate[:, :], xnr[:, :], ALU.mult).then_inc(q_dve, 1)
                        dve.wait_ge(q_dve, n3 + 3)
                        if since(t, 1):
                            dve.wait_ge(q_x1s, t * 16)
                        nc.vector.tensor_tensor(x1[:, :], y_gate[:, :], xr[:, b, :], ALU.add).then_inc(q_x1, 1)
                        dve.wait_ge(q_x1, t + 1)
                        for h in range(2):
                            i = nc.vector.bn_stats(bst2[:, h, :], x1[:, h * H:(h + 1) * H])
                        k = [0]

                        def step(ins):
                            k[0] += 1
                            ins.then_inc(q_st, 1)
                            dve.wait_ge(q_st, n12 + k[0])

                        step(i)
                        dve.sem_inc(dve_passed, 1)
                        step(nc.vector.bn_aggr(mv2[:, :], bst2[:, :, :].rearrange("p h s -> p (h s)")))
                        nc.vector.tensor_copy(stats2[:, ds(t, 1), 0], mv2[:, 0:1])
                        inverse_root(step, stats2[:, ds(t, 1), 1], mv2[:, 1:2], newton)
                        assert k[0] == NS + 2
                        if since(t, 1):
                            dve.wait_ge(q_xn2s, t * 16)
                            dve.wait_ge(q_n2t, t)
                        nc.vector.tensor_scalar(xn2[:, :], x1[:, :], mv2[:, 0:1], stats2[:, ds(t, 1), 1], ALU.subtract, ALU.mult).then_inc(q_xn2, 1)

                    def stage(j, b):
                        t = j * 2 + b

                        def between():
                            if since(t, 1):
                                low_u(t - 1)
                            if not since(t, 1):
                                dve.wait_ge(q_rhi, 1)
                                nc.vector.tensor_tensor(rows_lo[:, :], rows[:, :], rows_hi[:, :].bitcast(F32), ALU.subtract).then_inc(q_rlo, 1)
                            if not since(t, 2):
                                wg_low(4 * t)
                                wg_low(4 * t + 1)

                        messages(t, between)
                        take_u(t, b)
                        if not since(t, 2):
                            wg_low(4 * t + 2)
                            wg_low(4 * t + 3)
                        if since(t, 2):
                            update(j - 1, b)

                    stages(dve, stage)
                    low_u(T - 1)
                    for b in range(2):
                        update(T // 2 - 1, b)
                    dve.wait_ge(q_log, T)
                    nc.vector.tensor_copy(logits[:, :, :], ps_log[:, 0, 0:T * NX1].rearrange("p (t e) -> p t e", e=NX1))

                @block.tensor
                def _(pe):
                    pe.sem_inc(q_agg, G8)
                    pe.wait_ge(q_par[1], 16)
                    pe.wait_ge(q_cst, 5)
                    pe.wait_ge(q_rhi, 1)

                    def messages(t):
                        if not (isinstance(t, int) and t == 0):
                            pe.wait_ge(q_u, t)
                        for h in range(2):
                            nc.tensor.matmul(ps_u[:, h, :], fast_pick[:, 0, :], rows_hi[:, h * H:(h + 1) * H], start=True, stop=False)
                        first, last = bounds(pe, t)
                        with pe.Fori(first, last) as i:
                            for j in range(2):
                                g = i * 2 + j
                                pe.wait_ge(q_sel, g + 1)
                                for part in (part_hi, part_lo):
                                    for h in range(-(-S // H)):
                                        c = slice(h * H, min(S, h * H + H))
                                        nc.tensor.matmul(ps_u[:, h, 0:c.stop - c.start], sel[j][:, :],
                                                         part[:, ds((i % 2) * 2 + j, 1), c].rearrange("p a n -> p (a n)"),
                                                         start=False, stop=False)
                                pe.wait_ge(q_msc, g + 1)
                                nc.tensor.matmul(ps_u[:, 1, S - H:H], sel[j][:, :].bitcast(F32),
                                                 msg[:, ds((i % 4) * 2 + j, 1), S:D].rearrange("p a n -> p (a n)"),
                                                 start=False, stop=False).then_inc(q_agg, 1)
                        if not since(t, 1):
                            pe.wait_ge(q_rlo, 1)
                        for h in range(2):
                            m = nc.tensor.matmul(ps_u[:, h, :], fast_pick[:, 0, :], rows_lo[:, h * H:(h + 1) * H], start=False, stop=True)
                        m.then_inc(q_psu, 1)

                    def turn_u(t, b):
                        pe.wait_ge(q_u, t + 1)
                        if since(t, 1):
                            pe.wait_ge(q_ulo, t)
                        for k in range(KT):
                            m = nc.tensor.transpose(ps_tr[:, k // 4, (k % 4) * P:(k % 4 + 1) * P], u_sb[:, b, k * P:(k + 1) * P], ident[:, :])
                        m.then_inc(q_ut, 1)

                    def gate(t):
                        pe.wait_ge(q_ulo, t + 1)
                        if since(t, 1):
                            pe.wait_ge(q_zc, t)
                        else:
                            pe.wait_ge(q_wglo, KT)
                        for h in range(2):
                            w = slice(h * H, (h + 1) * H)
                            nc.tensor.matmul(ps_z[:, h, :], fast_pick[:, 1, :], rows_hi[:, w], start=True, stop=False)
                            nc.tensor.matmul(ps_z[:, h, :], fast_pick[:, 1, :], rows_lo[:, w], start=False, stop=False)
                            for k in range(KT):
                                nc.tensor.matmul(ps_z[:, h, :], uT_lo[:, k, :], wg_hi[:, k, w], start=False, stop=False)
                                nc.tensor.matmul(ps_z[:, h, :], uT_hi[:, k, :], wg_lo[:, k, w], start=False, stop=False)
                                m = nc.tensor.matmul(ps_z[:, h, :], uT_hi[:, k, :], wg_hi[:, k, w], start=False, stop=(k == KT - 1))
                        m.then_inc(q_z, 1)

                    def turn_n2(t):
                        pe.wait_ge(q_xn2, t + 1)
                        pe.wait_ge(q_ulo, min(t + 3, T) if isinstance(t, int) else t + 3)
                        for k in range(KT):
                            m = nc.tensor.transpose(ps_tr[:, k // 4, (k % 4) * P:(k % 4 + 1) * P], xn2[:, k * P:(k + 1) * P], ident[:, :])
                        m.then_inc(q_n2t, 1)

                    def router(t):
                        pe.wait_ge(q_n2c, t + 1)
                        o = ps_log[:, 0, ds(t * NX1, NX1)]
                        nc.tensor.matmul(o, pick[:, 2, :], rows[:, 0:NX1], start=True, stop=False)
                        for k in range(KT):
                            m = nc.tensor.matmul(o, xn2T[:, k, :], rw[:, k, :], start=False, stop=(k == KT - 1))
                        m.then_inc(q_log, 1)

                    def stage(j, b):
                        t = j * 2 + b
                        messages(t)
                        if since(t, 3):
                            turn_n2(t - 3)
                        if since(t, 1):
                            gate(t - 1)
                        if since(t, 3):
                            router(t - 3)
                        turn_u(t, b)

                    stages(pe, stage)
                    turn_n2(T - 3)
                    gate(T - 1)
                    router(T - 3)
                    turn_n2(T - 2)
                    router(T - 2)
                    turn_n2(T - 1)
                    router(T - 1)

        with ExitStack() as ph:
            FK = F // P
            tok_id = sb(ph, "tok_id", [P, T], F32)
            spare = sb(ph, "spare", [P, 1], F32)
            real = sb(ph, "real", [P, T], F32)
            tri = sb(ph, "tri", [P, NX1, NX1], F32)
            prob = sb(ph, "prob", [P, T, NX1], F32)
            cmp_ = sb(ph, "cmp", [P, 2, T * P], F32)
            rank = sb(ph, "rank", [P, T, NX1], F32)
            pickAB = sb(ph, "pick_ab", [P, 2, T, NX1], F32)
            tmp9 = sb(ph, "tmp9", [P, 2, T, NX1], F32)
            red = sb(ph, "red", [P, 12, T], F32)
            cume = [sb(ph, f"cume{i}", [P, NX, T], F32) for i in range(2)]
            pre3 = sb(ph, "pre3", [P, 4, 16], F32)
            pre3_i = sb(ph, "pre3_i", [P, 16], I32)
            chunk0 = sb(ph, "chunk0", [P, NX + 2], I32)
            has = sb(ph, "has", [P, 2, T], F32)
            slot = sb(ph, "slot", [P, 2, T], F32)
            slot_3 = sb(ph, "slot_3", [P, 3, 2, T], I32)
            place = sb(ph, "place", [P, 2, 2, T], F32)
            entry = sb(ph, "entry", [P, 2, 2 * T, NCH], F32)
            gates = sb(ph, "gates", [P, 3, T], F32)
            tok = sb(ph, "tok", [P, NCH + 1], I32)
            row = sb(ph, "row", [P, NCH], I32)
            row_f = sb(ph, "row_f", [P, NCH], F32)
            slot_gate = sb(ph, "slot_gate", [P, NCH], F32)
            tok_col = sb(ph, "tok_col", [P, 1], I32)
            row_col = sb(ph, "row_col", [P, 1], I32)
            null_gate = sb(ph, "null_gate", [P, 2], F32)
            null = sb(ph, "null", [P, 2, D], F32)
            e_stage = sb(ph, "e_stage", [P, 4, D], F32)
            w1_hi = [sb(ph, f"w1_hi{i}", [P, KT, F], F32R) for i in range(2)]
            w1_lo = [sb(ph, f"w1_lo{i}", [P, KT, F], F32R) for i in range(2)]
            w2_hi = [sb(ph, f"w2_hi{i}", [P, FK, D], F32R) for i in range(2)]
            w2_lo = [sb(ph, f"w2_lo{i}", [P, FK, D], F32R) for i in range(2)]
            xg = sb(ph, "xg", [P, D], F32)
            xgT_hi = sb(ph, "xgT_hi", [P, D], F32R)
            xgT_lo = sb(ph, "xgT_lo", [P, D], F32R)
            h_sb = sb(ph, "h_sb", [P, F], F32)
            hT_hi = sb(ph, "hT_hi", [P, F], F32R)
            hT_lo = sb(ph, "hT_lo", [P, F], F32R)
            y_sb = sb(ph, "y_sb", [P, D], F32)
            ps_x = ps(ph, "ps_x", [P, D])
            ps_h = ps(ph, "ps_h", [P, F])
            ps_hT = ps(ph, "ps_hT", [P, F])
            ps_y2 = ps(ph, "ps_y2", [P, D])
            ps_rt = ps(ph, "ps_rt", [P, 2, H // 2])

            z_cst = sem("phase3_constants")
            z_dve, z_exp = sem("routing_chain"), sem("exp_made")
            z_row, z_pre = sem("expert_row_totals"), sem("expert_prefixes")
            z_hot, z_entry, z_tok = sem("place_onehot_made"), sem("entries_summed"), sem("slot_tables_made")
            z_col, z_rcol = sem("token_column_copied"), sem("row_column_copied")
            z_nl, z_ng, z_nm, z_na = sem("null_loaded"), sem("null_gate_copied"), sem("null_scaled"), sem("null_added")
            z_added = sem("expert_out_added")
            z_fin = sem("output_stored")
            z_w = [sem(f"expert_stage{i}") for i in range(4)]
            z_whi, z_wlo = sem("expert_hi_made"), sem("expert_lo_made")
            z_xg, z_xt, z_xhi, z_xlo = sem("tokens_gathered"), sem("tokens_turned"), sem("tokens_hi_made"), sem("tokens_lo_made")
            z_h, z_gelu, z_ht = sem("hidden_multiplied"), sem("gelu_made"), sem("hidden_turned")
            z_hhi, z_hlo = sem("hidden_hi_made"), sem("hidden_lo_made")
            z_y, z_yc, z_ys = sem("expert_out_multiplied"), sem("expert_out_scaled"), sem("expert_out_add_done")

            with nc.Block() as block:
                def all_experts(eng, others):
                    others(0, 0)
                    with eng.Fori(0, NX // 2 - 1) as j:
                        for b in range(2):
                            others(j * 2 + b + 1, 1 - b, lead=True)

                def hot(i):
                    return cmp_[:, i // T, i % T * P:(i % T + 1) * P]

                def bounds(eng, e):
                    first = 0 if isinstance(e, int) and e == 0 else eng.value_load(chunk0[0:1, ds(e, 1)], min_val=1, max_val=NCH - 1)
                    last = eng.value_load(chunk0[0:1, ds(e + 1, 1)], min_val=1, max_val=NCH)
                    return first, last

                @block.gpsimd
                def _(pool):
                    nc.gpsimd.iota(tok_id[:, :], [[P, T]], base=P, channel_multiplier=1,
                                   allow_small_or_imprecise_dtypes=True).then_inc(z_cst, 1)
                    nc.gpsimd.iota(spare[:, :], [[1, 1]], base=NP + P, channel_multiplier=1,
                                   allow_small_or_imprecise_dtypes=True).then_inc(z_cst, 1)
                    nc.gpsimd.memset(real[:, :], 1.0).then_inc(z_cst, 1)
                    nc.gpsimd.memset(tri[:, :, :], 1.0).then_inc(z_cst, 1)
                    nc.gpsimd.memset(tok[:, :], 0).then_inc(z_cst, 1)
                    pool.wait_ge(z_cst, 5)
                    nc.gpsimd.affine_select(out=real[:, :], in_=real[:, :], compare_op=ALU.is_ge, fill=0.0, base=N - 1,
                                            pattern=[[-P, T]], channel_multiplier=-1).then_inc(z_cst, 1)
                    nc.gpsimd.affine_select(out=tri[:, :, :], in_=tri[:, :, :], compare_op=ALU.is_gt, fill=0.0, base=0,
                                            pattern=[[1, NX1], [-1, NX1]], channel_multiplier=0).then_inc(z_cst, 1)

                    xn2_t = xn2_dram.rearrange("(t p) n -> t p n", p=P)
                    sum_t = sum_dram.rearrange("(t p) n -> t p n", p=P)

                    def load_null(t, b):
                        pool.dma_start(null[:, b, :], xn2_t[ds(t, 1), :, :].rearrange("t p n -> (t p) n")).then_inc(z_nl, 16)

                    load_null(0, 0)
                    pool.wait_ge(z_tok, 1)
                    lead = pool.value_load(chunk0[0:1, NX + 1:NX + 2], min_val=T - 2, max_val=NCH - 2)

                    def gather(g):
                        nc.gpsimd.tensor_copy(tok_col[:, 0:1], tok[:, ds(g, 1)]).then_inc(z_col, 1)
                        pool.wait_ge(z_col, g + 1)
                        pool.sem_inc(pool_passed, 1)
                        pool.indirect_dma_start(xg[:, :], None, xn2_dram, bass.IndirectOffsetOnAxis(tok_col[:, 0:1], 0),
                                                bounds_check=NP - 1).then_inc(z_xg, 16)

                    def add_y(g):
                        pool.wait_ge(z_yc, g * 2 + 4)
                        nc.gpsimd.tensor_copy(row_col[:, 0:1], row[:, ds(g, 1)]).then_inc(z_rcol, 1)
                        pool.wait_ge(z_rcol, g + 1)
                        pool.sem_inc(pool_passed, 1)
                        pool.indirect_dma_start(sum_dram, bass.IndirectOffsetOnAxis(row_col[:, 0:1], 0), y_sb[:, :], None,
                                                bounds_check=NP + P - 1, compute_op=ALU.add).then_inc(z_ys, 16)

                    def added_y(g):
                        pool.wait_ge(z_ys, g * 16 + 16)
                        pool.sem_inc(z_added, 1)

                    def begin_null(t, b, more):
                        if not (isinstance(t, int) and t == 0):
                            pool.wait_ge(z_na, t * 16)
                        pool.wait_ge(z_nl, t * 16 + 16)
                        pool.sem_inc(pool_passed, 1)
                        if more:
                            load_null(t + 1, 1 - b)

                    def scale_null(t, b):
                        nc.gpsimd.tensor_copy(null_gate[:, b:b + 1], gates[:, 2, ds(t, 1)]).then_inc(z_ng, 1)
                        pool.wait_ge(z_ng, t + 1)
                        pool.sem_inc(pool_passed, 1)
                        nc.gpsimd.tensor_scalar(null[:, b, :], null[:, b, :], null_gate[:, b:b + 1], None, ALU.mult).then_inc(z_nm, 1)

                    def add_null(t, b, rows=P):
                        pool.wait_ge(z_nm, t + 1)
                        pool.sem_inc(pool_passed, 1)
                        pool.dma_start(sum_t[ds(t, 1), 0:rows, :].rearrange("t p n -> (t p) n"), null[0:rows, b, :],
                                       accum_op=ALU.add).then_inc(z_na, 16)

                    def step(g, t, b, more=True, rows=P):
                        begin_null(t, b, more)
                        add_y(g)
                        scale_null(t, b)
                        added_y(g)
                        add_null(t, b, rows)

                    def next_gather(g):
                        pool.wait_ge(z_xg, g * 16)
                        pool.wait_ge(z_xt, g)
                        gather(g)

                    gather(0)
                    next_gather(1)
                    next_gather(2)
                    next_gather(3)
                    step(0, 0, 0)
                    next_gather(4)
                    step(1, 1, 1)
                    with pool.Fori(1, T // 2 - 1) as j:
                        for b in range(2):
                            g = j * 2 + b
                            next_gather(g + 3)
                            step(g, g, b)
                    with pool.If(lead > T - 2):
                        next_gather(T + 1)
                    step(T - 2, T - 2, 0)
                    with pool.If(lead > T - 1):
                        next_gather(T + 2)
                    step(T - 1, T - 1, 1, False, LAST)
                    pool.wait_ge(z_na, 16 * T)
                    with pool.If(lead > T):
                        with pool.Fori(T, lead) as g:
                            next_gather(g + 3)
                            add_y(g)
                            added_y(g)
                    with pool.If(lead > T - 1):
                        add_y(lead)
                        added_y(lead)
                    with pool.If(lead > T - 2):
                        add_y(lead + 1)
                        added_y(lead + 1)
                    pool.wait_ge(z_xg, lead * 16 + 48)
                    pool.sem_inc(z_added, 1)

                @block.sync
                def _(sp):
                    w1_t = w1.rearrange("e (q k p) f -> e q p k f", p=P, k=2)
                    w2_t = w2.rearrange("e (k p) n -> e k p n", p=P)

                    def weights(e, first=False):
                        for q in range(8):
                            if not (first and q < 4):
                                sp.wait_ge(z_wlo, e * 8 + (q - 3))
                            part = w1_t[ds(e, 1), q, :, :, :].rearrange("e p k f -> (e p) k f") if q < 4 else \
                                w2_t[ds(e, 1), q - 4, :, :].rearrange("e p n -> (e p) n")
                            to = e_stage[:, q % 4, :].rearrange("p (k f) -> p k f", k=2) if q < 4 else e_stage[:, q % 4, :]
                            sp.dma_start(to, part).then_inc(z_w[q % 4], 16)

                    weights(0, True)
                    with sp.Fori(1, NX) as e:
                        weights(e)
                    total = sp.value_load(chunk0[0:1, NX:NX + 1], min_val=NX, max_val=NCH)
                    sp.wait_ge(z_added, total + 2)
                    sp.dma_start(out, sum_dram[0:N, :]).then_inc(z_fin, 16)
                    sp.wait_ge(z_fin, 16)

                @block.scalar
                def _(act):
                    act.sem_inc(z_added, 1)
                    act.sem_inc(z_yc, 2)
                    act.wait_ge(z_dve, 1)
                    nc.scalar.activation(prob[:, :, :], prob[:, :, :], ACT.Exp).then_inc(z_exp, 1)

                    def split_hi(e, b, q):
                        act.wait_ge(z_w[q % 4], e * 32 + (q // 4) * 16 + 16)
                        to = w1_hi[b][:, 2 * q:2 * q + 2, :].rearrange("p k f -> p (k f)") if q < 4 else w2_hi[b][:, q - 4, :]
                        nc.scalar.activation(to, e_stage[:, q % 4, :], ACT.Copy).then_inc(z_whi, 1)

                    def turn_hi(n):
                        act.wait_ge(z_xt, n)
                        nc.scalar.activation(xgT_hi[:, :], ps_x[:, :], ACT.Copy).then_inc(z_xhi, 1)

                    def hidden_hi(g):
                        act.wait_ge(z_ht, g + 1)
                        nc.scalar.activation(hT_hi[:, :], ps_hT[:, :], ACT.Copy).then_inc(z_hhi, 1)

                    def gelu(g):
                        act.wait_ge(z_h, g + 1)
                        nc.scalar.activation(h_sb[:, :], ps_h[:, :], ACT.Gelu).then_inc(z_gelu, 1)

                    def take_y(g):
                        act.wait_ge(z_y, g + 1)
                        act.wait_ge(z_added, g + 1)
                        nc.scalar.activation(y_sb[:, 0:H], ps_y2[:, 0:H], ACT.Copy, scale=slot_gate[:, ds(g, 1)]).then_inc(z_yc, 1)

                    def step(g, parts=()):
                        hidden_hi(g - 1)
                        for p in parts[:2]:
                            split_hi(*p)
                        gelu(g)
                        turn_hi(g + 2)
                        for p in parts[2:]:
                            split_hi(*p)
                        take_y(g - 1)

                    def expert(e, b, lead=False, more=True):
                        first, last = bounds(act, e)
                        parts = [[(e + 1, 1 - b, 4 * i + q) for q in range(4)] if more else [] for i in range(2)]
                        if lead:
                            step(first, parts[0])
                        else:
                            for p in parts[0]:
                                split_hi(*p)
                        if more:
                            with act.If(last - first < 2):
                                for p in parts[1]:
                                    split_hi(*p)
                        with act.If(first + 1 < last):
                            step(first + 1, parts[1])
                            with act.If(first + 2 < last):
                                with act.Fori(first + 2, last) as g:
                                    step(g)

                    for q in range(4):
                        split_hi(0, 0, q)
                    turn_hi(1)
                    for q in range(4, 8):
                        split_hi(0, 0, q)
                    gelu(0)
                    turn_hi(2)
                    all_experts(act, expert)
                    expert(NX - 1, 1, True, False)
                    total = act.value_load(chunk0[0:1, NX:NX + 1], min_val=NX, max_val=NCH)
                    hidden_hi(total - 1)
                    take_y(total - 1)

                @block.vector
                def _(dve):
                    n = [0]

                    def step(ins):
                        n[0] += 1
                        ins.then_inc(z_dve, 1)
                        dve.wait_ge(z_dve, n[0])

                    def split_lo(e, b, q):
                        dve.wait_ge(z_whi, e * 8 + q + 1)
                        hi = w1_hi[b][:, 2 * q:2 * q + 2, :].rearrange("p k f -> p (k f)") if q < 4 else w2_hi[b][:, q - 4, :]
                        lo = w1_lo[b][:, 2 * q:2 * q + 2, :].rearrange("p k f -> p (k f)") if q < 4 else w2_lo[b][:, q - 4, :]
                        nc.vector.tensor_tensor(lo, e_stage[:, q % 4, :], hi.bitcast(F32), ALU.subtract).then_inc(z_wlo, 1)

                    nc.vector.tensor_reduce(red[:, 0, :], logits[:, :, :], AX.X, ALU.max).then_inc(z_row, 1)
                    dve.wait_ge(z_row, 1)
                    step(nc.vector.tensor_tensor(prob[:, :, :], logits[:, :, :], red[:, 0, :].unsqueeze(2).broadcast_to([P, T, NX1]), ALU.subtract))
                    dve.wait_ge(z_exp, 1)
                    step(nc.vector.tensor_reduce(red[:, 1, :], prob[:, :, :], AX.X, ALU.add))
                    step(nc.vector.reciprocal(red[:, 2, :], red[:, 1, :]))
                    step(nc.vector.tensor_tensor(prob[:, :, :], prob[:, :, :], red[:, 2, :].unsqueeze(2).broadcast_to([P, T, NX1]), ALU.mult))
                    gt = cmp_[:, 0, 0:T * NX1 * NX1].rearrange("p (t j i) -> p t j i", j=NX1, i=NX1)
                    eq = cmp_[:, 1, 0:T * NX1 * NX1].rearrange("p (t j i) -> p t j i", j=NX1, i=NX1)
                    p_i = prob[:, :, :].unsqueeze(2).broadcast_to([P, T, NX1, NX1])
                    p_j = prob[:, :, :].unsqueeze(3).broadcast_to([P, T, NX1, NX1])
                    dve.wait_ge(z_cst, 7)
                    nc.vector.tensor_tensor(gt, p_i, p_j, ALU.is_gt)
                    step(nc.vector.tensor_tensor(eq, p_i, p_j, ALU.is_equal))
                    step(nc.vector.tensor_tensor(eq, eq, tri[:, :, :].unsqueeze(1).broadcast_to([P, T, NX1, NX1]), ALU.mult))
                    step(nc.vector.tensor_tensor(gt, gt, eq, ALU.add))
                    step(nc.vector.tensor_reduce(rank[:, :, :], gt, AX.X, ALU.add))
                    for c in range(2):
                        step(nc.vector.tensor_scalar(pickAB[:, c, :, :], rank[:, :, :], float(c), None, ALU.is_equal))
                    for c in range(2):
                        step(nc.vector.tensor_tensor(pickAB[:, c, :, :], pickAB[:, c, :, :], real[:, :].unsqueeze(2).broadcast_to([P, T, NX1]), ALU.mult))
                    step(nc.vector.tensor_tensor(cume[0][:, :, :], pickAB[:, 0, :, 0:NX].rearrange("p t e -> p e t"),
                                                 pickAB[:, 1, :, 0:NX].rearrange("p t e -> p e t"), ALU.add))
                    a, b, d = cume[0], cume[1], 1
                    while d < T:
                        nc.vector.tensor_copy(b[:, :, 0:d], a[:, :, 0:d])
                        step(nc.vector.tensor_tensor(b[:, :, d:T], a[:, :, d:T], a[:, :, 0:T - d], ALU.add))
                        a, b, d = b, a, 2 * d
                    nc.vector.tensor_copy(pre3[:, 0, 0:NX], a[:, :, T - 1]).then_inc(z_row, 1)
                    step(nc.vector.tensor_tensor(tmp9[:, :, :, :], prob[:, :, :].unsqueeze(1).broadcast_to([P, 2, T, NX1]), pickAB[:, :, :, :], ALU.mult))
                    nc.vector.tensor_reduce(gates[:, 0:2, :], tmp9[:, :, :, 0:NX], AX.X, ALU.add)
                    step(nc.vector.tensor_tensor(gates[:, 2, :], tmp9[:, 0, :, NX], tmp9[:, 1, :, NX], ALU.add))
                    step(nc.vector.tensor_reduce(has[:, :, :], pickAB[:, :, :, 0:NX], AX.X, ALU.add))
                    step(nc.vector.tensor_scalar(has[:, :, :], has[:, :, :], -float(2 * NCH * P), float(2 * NCH * P), ALU.mult, ALU.add))
                    dve.wait_ge(z_pre, 1)
                    step(nc.vector.tensor_scalar(pre3_i[:, 0:NX], ps_rt[:, 1, 0:NX], float(P - 1), None, ALU.add))
                    step(nc.vector.tensor_scalar(pre3_i[:, 0:NX], pre3_i[:, 0:NX], P.bit_length() - 1, None, ALU.arith_shift_right))
                    nc.vector.memset(pre3[:, 2, 0:1], 0.0)
                    step(nc.vector.tensor_scalar(pre3[:, 1, 0:NX], pre3_i[:, 0:NX], 1.0, None, ALU.max))
                    for k in range(NX):
                        step(nc.vector.tensor_tensor(pre3[:, 2, k + 1:k + 2], pre3[:, 2, k:k + 1], pre3[:, 1, k:k + 1], ALU.add))
                    nc.vector.tensor_copy(chunk0[:, 0:NX + 1], pre3[:, 2, 0:NX + 1])
                    nc.vector.tensor_scalar(chunk0[:, NX + 1:NX + 2], pre3[:, 2, NX:NX + 1], -2.0, None, ALU.add)
                    step(nc.vector.scalar_tensor_tensor(pre3[:, 3, 0:NX], pre3[:, 2, 0:NX], float(P), ps_rt[:, 0, 0:NX], ALU.mult, ALU.add))
                    step(nc.vector.tensor_scalar(pre3[:, 3, 0:NX], pre3[:, 3, 0:NX], -1.0, None, ALU.add))
                    step(nc.vector.tensor_tensor(b[:, :, :], a[:, :, :], pre3[:, 3, 0:NX].unsqueeze(2).broadcast_to([P, NX, T]), ALU.add))
                    step(nc.vector.tensor_tensor(tmp9[:, :, :, 0:NX], pickAB[:, :, :, 0:NX],
                                                 b[:, :, :].rearrange("p e t -> p t e").unsqueeze(1).broadcast_to([P, 2, T, NX]), ALU.mult))
                    step(nc.vector.tensor_reduce(slot[:, :, :], tmp9[:, :, :, 0:NX], AX.X, ALU.add))
                    step(nc.vector.tensor_tensor(slot[:, :, :], slot[:, :, :], has[:, :, :], ALU.add))
                    step(nc.vector.tensor_copy(slot_3[:, 0, :, :], slot[:, :, :]))
                    nc.vector.tensor_scalar(slot_3[:, 1, :, :], slot_3[:, 0, :, :], P - 1, None, ALU.bitwise_and)
                    step(nc.vector.tensor_scalar(slot_3[:, 2, :, :], slot_3[:, 0, :, :], P.bit_length() - 1, None, ALU.arith_shift_right))
                    step(nc.vector.tensor_copy(place[:, :, :, :], slot_3[:, 1:3, :, :]))
                    each = [P, 2 * T, NCH]
                    here = entry[:, 0, :, :]
                    step(nc.vector.tensor_tensor(here, place[:, 1, :, :].rearrange("p c t -> p (c t)").unsqueeze(2).broadcast_to(each),
                                                 iota_row[:, 0:NCH].unsqueeze(1).broadcast_to(each), ALU.is_equal))
                    step(nc.vector.tensor_tensor(entry[:, 1, :, :], here,
                                                 gates[:, 0:2, :].rearrange("p c t -> p (c t)").unsqueeze(2).broadcast_to(each), ALU.mult))
                    for c in range(2):
                        e = entry[:, 0, c * T:(c + 1) * T, :]
                        i = nc.vector.tensor_tensor(e, e, tok_id[:, :].unsqueeze(2).broadcast_to([P, T, NCH]), ALU.mult)
                    step(i)
                    for i in range(2 * T):
                        nc.vector.tensor_scalar(hot(i), iota_row[:, :], place[:, 0, i // T, i % T:i % T + 1], None, ALU.is_equal).then_inc(z_hot, 1)
                    for q in range(4):
                        split_lo(0, 0, q)
                    dve.wait_ge(z_entry, 1)
                    in_slot = ps_rt[:, 0, 0:NCH]
                    step(nc.vector.tensor_scalar(row_f[:, :], in_slot, 0.0, spare[:, :], ALU.is_equal, ALU.mult))
                    nc.vector.scalar_tensor_tensor(row[:, :], in_slot, -float(P), row_f[:, :], ALU.add, ALU.add)
                    nc.vector.tensor_scalar(tok[:, 0:NCH], in_slot, -float(P), 0.0, ALU.add, ALU.max).then_inc(z_tok, 1)

                    def turn_lo(n):
                        dve.wait_ge(z_xhi, n)
                        nc.vector.tensor_tensor(xgT_lo[:, :], ps_x[:, :], xgT_hi[:, :].bitcast(F32), ALU.subtract).then_inc(z_xlo, 1)

                    def hidden_lo(g):
                        dve.wait_ge(z_hhi, g + 1)
                        nc.vector.tensor_tensor(hT_lo[:, :], ps_hT[:, :], hT_hi[:, :].bitcast(F32), ALU.subtract).then_inc(z_hlo, 1)

                    def take_y(g):
                        dve.wait_ge(z_y, g + 1)
                        dve.wait_ge(z_added, g + 1)
                        nc.vector.tensor_scalar(y_sb[:, H:D], ps_y2[:, H:D], slot_gate[:, ds(g, 1)], None, ALU.mult).then_inc(z_yc, 1)

                    def low_step(g, parts=()):
                        hidden_lo(g - 1)
                        for p in parts[:2]:
                            split_lo(*p)
                        turn_lo(g + 2)
                        for p in parts[2:]:
                            split_lo(*p)
                        take_y(g - 1)

                    def expert(e, b, lead=False, more=True):
                        first, last = bounds(dve, e)
                        parts = [[(e + 1, 1 - b, 4 * i + q) for q in range(4)] if more else [] for i in range(2)]
                        if lead:
                            low_step(first, parts[0])
                        else:
                            for p in parts[0]:
                                split_lo(*p)
                        if more:
                            with dve.If(last - first < 2):
                                for p in parts[1]:
                                    split_lo(*p)
                        with dve.If(first + 1 < last):
                            low_step(first + 1, parts[1])
                            with dve.If(first + 2 < last):
                                with dve.Fori(first + 2, last) as g:
                                    low_step(g)

                    turn_lo(1)
                    for q in range(4, 8):
                        split_lo(0, 0, q)
                    turn_lo(2)
                    dve.wait_ge(z_entry, 2)
                    nc.vector.tensor_copy(slot_gate[:, :], ps_y2[:, 0:NCH])
                    all_experts(dve, expert)
                    expert(NX - 1, 1, True, False)
                    total = dve.value_load(chunk0[0:1, NX:NX + 1], min_val=NX, max_val=NCH)
                    hidden_lo(total - 1)
                    take_y(total - 1)

                @block.tensor
                def _(pe):
                    pe.wait_ge(z_row, 2)
                    nc.tensor.matmul(ps_rt[:, 0, 0:NX], lower[:, :], pre3[:, 0, 0:NX], start=True, stop=True)
                    nc.tensor.matmul(ps_rt[:, 1, 0:NX], ones[:, :], pre3[:, 0, 0:NX], start=True, stop=True).then_inc(z_pre, 1)
                    for i in range(2 * T):
                        pe.wait_ge(z_hot, i + 1)
                        m = nc.tensor.matmul(ps_rt[:, 0, 0:NCH], hot(i), entry[:, 0, i, :], start=(i == 0), stop=(i == 2 * T - 1))
                    m.then_inc(z_entry, 1)

                    def sum_gates(c):
                        for i in range(c * T, c * T + T):
                            m = nc.tensor.matmul(ps_y2[:, 0:NCH], hot(i), entry[:, 1, i, :], start=(i == 0), stop=(i == 2 * T - 1))
                        if c == 1:
                            m.then_inc(z_entry, 1)

                    def turn(n):
                        pe.wait_ge(z_xg, n * 16)
                        for k in range(KT):
                            m = nc.tensor.transpose(ps_x[:, k * P:(k + 1) * P], xg[:, k * P:(k + 1) * P], ident[:, :])
                        m.then_inc(z_xt, 1)

                    def first_product(g, b):
                        pe.wait_ge(z_xlo, g + 1)
                        for k in range(KT):
                            w = slice(k * P, (k + 1) * P)
                            nc.tensor.matmul(ps_h[:, :], xgT_lo[:, w], w1_hi[b][:, k, :], start=(k == 0), stop=False)
                            nc.tensor.matmul(ps_h[:, :], xgT_hi[:, w], w1_lo[b][:, k, :], start=False, stop=False)
                            m = nc.tensor.matmul(ps_h[:, :], xgT_hi[:, w], w1_hi[b][:, k, :], start=False, stop=(k == KT - 1))
                        m.then_inc(z_h, 1)

                    def turn_hidden(g):
                        pe.wait_ge(z_gelu, g + 1)
                        for k in range(FK):
                            m = nc.tensor.transpose(ps_hT[:, k * P:(k + 1) * P], h_sb[:, k * P:(k + 1) * P], ident[:, :])
                        m.then_inc(z_ht, 1)

                    def second_product(g, b):
                        pe.wait_ge(z_hlo, g + 1)
                        pe.wait_ge(z_yc, g * 2 + 2)
                        for h in range(2):
                            o = slice(h * H, (h + 1) * H)
                            for k in range(FK):
                                w = slice(k * P, (k + 1) * P)
                                nc.tensor.matmul(ps_y2[:, o], hT_lo[:, w], w2_hi[b][:, k, o], start=(k == 0), stop=False)
                                nc.tensor.matmul(ps_y2[:, o], hT_hi[:, w], w2_lo[b][:, k, o], start=False, stop=False)
                                m = nc.tensor.matmul(ps_y2[:, o], hT_hi[:, w], w2_hi[b][:, k, o], start=False, stop=(k == FK - 1))
                        m.then_inc(z_y, 1)

                    def step(g, b, b_before):
                        turn_hidden(g - 1)
                        first_product(g, b)
                        turn(g + 2)
                        second_product(g - 1, b_before)

                    def expert(e, b, lead=False):
                        first, last = bounds(pe, e)
                        if lead:
                            pe.wait_ge(z_wlo, e * 8 + 4)
                            pe.sem_inc(pe_passed, 1)
                            step(first, b, 1 - b)
                        with pe.If(first + 1 < last):
                            pe.wait_ge(z_wlo, e * 8 + 8)
                            pe.sem_inc(pe_passed, 1)
                            with pe.Fori(first + 1, last) as g:
                                step(g, b, b)

                    sum_gates(0)
                    turn(1)
                    pe.wait_ge(z_wlo, 4)
                    first_product(0, 0)
                    turn(2)
                    sum_gates(1)
                    all_experts(pe, expert)
                    expert(NX - 1, 1, True)
                    total = pe.value_load(chunk0[0:1, NX:NX + 1], min_val=NX, max_val=NCH)
                    turn_hidden(total - 1)
                    pe.wait_ge(z_wlo, NX * 8)
                    second_product(total - 1, 1)


def kernel(**inputs):
    import numpy as np
    import concourse.bacc as bacc
    from concourse import mybir
    from concourse.bass_utils import run_bass_kernel_spmd

    a = lay_out(inputs)
    nc = bacc.Bacc("TRN2", target_bir_lowering=False, num_devices=1)
    args = {k: nc.dram_tensor(k, v.shape, mybir.dt.from_np(v.dtype), kind="ExternalInput").ap() for k, v in a.items()}
    out = nc.dram_tensor("out", inputs["x"].shape, mybir.dt.float32, kind="ExternalOutput").ap()
    build_program(nc, out=out, **args)
    r = run_bass_kernel_spmd(nc, [a], core_ids=[0])
    return r.results[0]["out"]


def lay_out(inputs):
    import numpy as np
    g = {k: np.ascontiguousarray(v) for k, v in inputs.items()}
    d = g["x"].shape[1]
    return dict(x=g["x"], src=g["src"], dst=g["dst"], typ=g["edge_type_8"],
                w_all=np.concatenate([g["L0_gnn_weight"], g["L0_gnn_root"][None], g["L0_gnn_w_gate"][None, d:]]),
                bias=g["L0_gnn_bias"][None], w_gate_u=g["L0_gnn_w_gate"][:d], b_gate=g["L0_gnn_b_gate"][None],
                router_w=g["L0_ffn_router_w"], router_b=g["L0_ffn_router_b"][None], w1=g["L0_ffn_w1"], w2=g["L0_ffn_w2"])
```
